# Optimizing a Trainium2 kernel written in Bass

```python
import numpy as np
import jax
import jax.numpy as jnp

def _softmax(x, axis=-1):
    return jax.nn.softmax(x, axis=axis)

def _gelu(x):
    return jax.nn.gelu(x, approximate=True)

def _silu(x):
    return jax.nn.silu(x)

def _sigmoid(x):
    return jax.nn.sigmoid(x)

def _layernorm(x, axis=-1, eps=1e-05):
    m = jnp.mean(x, axis=axis, keepdims=True)
    v = jnp.var(x, axis=axis, keepdims=True)
    return (x - m) / jnp.sqrt(v + eps)

def _scatter_add(tgt, idx, src, axis=0):
    return tgt.at[idx].add(src)

def _segment_sum(src, seg, n):
    return jax.ops.segment_sum(src, seg, n)
kernel_name = 'mk_vit_tower_cls_d2_tok_img768_r4_572872'

def setup_inputs(seed: int=0):
    np.random.seed(seed)
    _w = jnp.asarray

    def _rec_inputs():
        import jax
        import jax.numpy as jnp
        _rk = jax.random.key(seed)
        x = -0.00016672 + 0.999947 * jax.random.normal(jax.random.fold_in(_rk, 1), (32, 3, 112, 112), jnp.float32)
        cls_tok = 0.02 * jax.random.normal(jax.random.fold_in(_rk, 5), (1, 1, 192), jnp.float32)
        return (x, cls_tok)
    x, cls_tok = _rec_inputs()

    def _L0_tok_setup():
        import jax, jax.numpy as jnp
        import numpy as np
        CHANNEL = 3
        PATCH = 16
        D_MODEL = 192
        key = jax.random.key(seed)
        kx, kw = jax.random.split(key)
        x = jax.random.normal(kx, (64, CHANNEL, 96, 96), dtype=jnp.float32)
        fan_in = PATCH * PATCH * CHANNEL
        bound = 1.0 / np.sqrt(fan_in)
        W = jax.random.uniform(kw, (D_MODEL, fan_in), dtype=jnp.float32, minval=-bound, maxval=bound)
        return {'x': x, 'W': W}
    _L0_tok_all = _L0_tok_setup()
    _L0_tok_in = {k: v for k, v in _L0_tok_all.items() if k in ('W',)}
    del _L0_tok_all

    def _L0_attn_setup():
        import jax, jax.numpy as jnp
        import numpy as np
        B, T, D, R = (8, 1024, 192, 16)
        DB = D // 3
        key = jax.random.key(seed)
        ks = jax.random.split(key, 10)
        s = 0.05
        x = jax.random.normal(ks[0], (B, T, D), dtype=jnp.float32)
        V_w = jax.random.normal(ks[1], (R, D), dtype=jnp.float32) * s
        U_w = jax.random.normal(ks[2], (D, R), dtype=jnp.float32) * s
        E1_w = jax.random.normal(ks[3], (DB, D), dtype=jnp.float32) * s
        E1_b = jnp.zeros((DB,), dtype=jnp.float32)
        E2_w = jax.random.normal(ks[4], (3, DB), dtype=jnp.float32) * s
        E2_b = jnp.zeros((3,), dtype=jnp.float32)
        a_base = jnp.concatenate([jnp.full((DB,), -0.6, dtype=jnp.float32), jnp.full((DB,), -1.0, dtype=jnp.float32), jnp.full((D - 2 * DB,), -1.6, dtype=jnp.float32)])
        a_delta = jax.random.normal(ks[5], (D,), dtype=jnp.float32) * 0.1
        C_w = jax.random.normal(ks[6], (D, D), dtype=jnp.float32) * s
        G_w = jax.random.normal(ks[7], (D, D), dtype=jnp.float32) * s
        G_b = jnp.zeros((D,), dtype=jnp.float32)
        return {'x': x, 'V_w': V_w, 'U_w': U_w, 'E1_w': E1_w, 'E1_b': E1_b, 'E2_w': E2_w, 'E2_b': E2_b, 'a_base': a_base, 'a_delta': a_delta, 'C_w': C_w, 'G_w': G_w, 'G_b': G_b}
    _L0_attn_all = _L0_attn_setup()
    _L0_attn_in = {k: v for k, v in _L0_attn_all.items() if k in ('V_w', 'U_w', 'E1_w', 'E1_b', 'E2_w', 'E2_b', 'a_base', 'a_delta', 'C_w', 'G_w', 'G_b')}
    del _L0_attn_all

    def _L0_ffn_setup():
        import jax, jax.numpy as jnp
        import numpy as np
        TOP_K = 2
        key = jax.random.key(seed)
        ks = jax.random.split(key, 5)
        B, T, C, H, E = (4, 256, 192, 768, 8)
        x = jax.random.normal(ks[0], (B, T, C), dtype=jnp.float32)
        Wg = jax.random.normal(ks[1], (C, E), dtype=jnp.float32) * 0.02
        W1 = jax.random.normal(ks[2], (E, C, H), dtype=jnp.float32) * (1.0 / np.sqrt(C))
        b1 = jnp.zeros((E, H), dtype=jnp.float32)
        W2 = jax.random.normal(ks[3], (E, H, C), dtype=jnp.float32) * (1.0 / np.sqrt(H))
        b2 = jnp.zeros((E, C), dtype=jnp.float32)
        return {'x': x, 'Wg': Wg, 'W1': W1, 'b1': b1, 'W2': W2, 'b2': b2}
    _L0_ffn_all = _L0_ffn_setup()
    _L0_ffn_in = {k: v for k, v in _L0_ffn_all.items() if k in ('Wg', 'W1', 'b1', 'W2', 'b2')}
    del _L0_ffn_all

    def _L1_attn_setup():
        import jax, jax.numpy as jnp
        import numpy as np
        H = 12

        def _heads(x, B, S):
            return x.reshape(B, S, H, -1).transpose(0, 2, 1, 3)
        key = jax.random.key(seed)
        ks = jax.random.split(key, 6)
        B, S, D = (2, 512, 192)
        sc = 0.02
        return {'hidden_states': jax.random.normal(ks[0], (B, S, D), jnp.float32), 'Wqr': jax.random.normal(ks[1], (D, D), jnp.float32) * sc, 'Wqi': jax.random.normal(ks[2], (D, D), jnp.float32) * sc, 'Wkr': jax.random.normal(ks[3], (D, D), jnp.float32) * sc, 'Wki': jax.random.normal(ks[4], (D, D), jnp.float32) * sc, 'Wv': jax.random.normal(ks[5], (D, D), jnp.float32) * sc}
    _L1_attn_all = _L1_attn_setup()
    _L1_attn_in = {k: v for k, v in _L1_attn_all.items() if k in ('Wqr', 'Wqi', 'Wkr', 'Wki', 'Wv')}
    del _L1_attn_all

    def _L1_ffn_setup():
        import jax, jax.numpy as jnp
        import numpy as np
        H = 192
        R = 64
        E = 8
        B, S = (8, 512)
        key = jax.random.key(seed)
        ks = jax.random.split(key, 10)
        s_in = 1.0 / np.sqrt(H)
        s_r = 1.0 / np.sqrt(R)
        return {'x': jax.random.normal(ks[0], (B, S, H), dtype=jnp.float32), 'enc_w': jax.random.uniform(ks[1], (H, R), jnp.float32, -s_in, s_in), 'enc_b': jax.random.uniform(ks[2], (R,), jnp.float32, -s_in, s_in), 'sw_w': jax.random.uniform(ks[3], (R, E), jnp.float32, -s_r, s_r), 'sw_b': jax.random.uniform(ks[4], (E,), jnp.float32, -s_r, s_r), 'w1': jax.random.uniform(ks[5], (E, H, R), jnp.float32, -s_in, s_in), 'b1': jax.random.uniform(ks[6], (E, R), jnp.float32, -s_in, s_in), 'w2': jax.random.uniform(ks[7], (E, R, H), jnp.float32, -s_r, s_r), 'b2': jax.random.uniform(ks[8], (E, H), jnp.float32, -s_r, s_r)}
    _L1_ffn_all = _L1_ffn_setup()
    _L1_ffn_in = {k: v for k, v in _L1_ffn_all.items() if k in ('enc_w', 'enc_b', 'sw_w', 'sw_b', 'w1', 'b1', 'w2', 'b2')}
    del _L1_ffn_all
    return {'x': x, 'cls_tok': cls_tok, 'L0_tok_W': _L0_tok_in['W'], 'L0_attn_V_w': _L0_attn_in['V_w'], 'L0_attn_U_w': _L0_attn_in['U_w'], 'L0_attn_E1_w': _L0_attn_in['E1_w'], 'L0_attn_E1_b': _L0_attn_in['E1_b'], 'L0_attn_E2_w': _L0_attn_in['E2_w'], 'L0_attn_E2_b': _L0_attn_in['E2_b'], 'L0_attn_a_base': _L0_attn_in['a_base'], 'L0_attn_a_delta': _L0_attn_in['a_delta'], 'L0_attn_C_w': _L0_attn_in['C_w'], 'L0_attn_G_w': _L0_attn_in['G_w'], 'L0_attn_G_b': _L0_attn_in['G_b'], 'L0_ffn_Wg': _L0_ffn_in['Wg'], 'L0_ffn_W1': _L0_ffn_in['W1'], 'L0_ffn_b1': _L0_ffn_in['b1'], 'L0_ffn_W2': _L0_ffn_in['W2'], 'L0_ffn_b2': _L0_ffn_in['b2'], 'L1_attn_Wqr': _L1_attn_in['Wqr'], 'L1_attn_Wqi': _L1_attn_in['Wqi'], 'L1_attn_Wkr': _L1_attn_in['Wkr'], 'L1_attn_Wki': _L1_attn_in['Wki'], 'L1_attn_Wv': _L1_attn_in['Wv'], 'L1_ffn_enc_w': _L1_ffn_in['enc_w'], 'L1_ffn_enc_b': _L1_ffn_in['enc_b'], 'L1_ffn_sw_w': _L1_ffn_in['sw_w'], 'L1_ffn_sw_b': _L1_ffn_in['sw_b'], 'L1_ffn_w1': _L1_ffn_in['w1'], 'L1_ffn_b1': _L1_ffn_in['b1'], 'L1_ffn_w2': _L1_ffn_in['w2'], 'L1_ffn_b2': _L1_ffn_in['b2']}

def reference(x, cls_tok, L0_tok_W, L0_attn_V_w, L0_attn_U_w, L0_attn_E1_w, L0_attn_E1_b, L0_attn_E2_w, L0_attn_E2_b, L0_attn_a_base, L0_attn_a_delta, L0_attn_C_w, L0_attn_G_w, L0_attn_G_b, L0_ffn_Wg, L0_ffn_W1, L0_ffn_b1, L0_ffn_W2, L0_ffn_b2, L1_attn_Wqr, L1_attn_Wqi, L1_attn_Wkr, L1_attn_Wki, L1_attn_Wv, L1_ffn_enc_w, L1_ffn_enc_b, L1_ffn_sw_w, L1_ffn_sw_b, L1_ffn_w1, L1_ffn_b1, L1_ffn_w2, L1_ffn_b2):
    import jax
    import jax.numpy as jnp

    def _L0_tok_ref(x, W):
        import jax, jax.numpy as jnp
        import numpy as np
        CHANNEL = 3
        PATCH = 16
        D_MODEL = 192
        B, C, H, Wd = x.shape
        p = PATCH
        nH, nW = (H // p, Wd // p)
        patches = x.reshape(B, C, nH, p, nW, p)
        patches = patches.transpose(0, 2, 4, 3, 5, 1)
        flat = patches.reshape(B, nH * nW, p * p * C)
        return jnp.einsum('bnk,dk->bnd', flat, W)

    def _L0_attn_ref(x, V_w, U_w, E1_w, E1_b, E2_w, E2_b, a_base, a_delta, C_w, G_w, G_b):
        import jax, jax.numpy as jnp
        import numpy as np
        B, T, D, R = (8, 1024, 192, 16)
        DB = D // 3
        d = x.shape[-1]
        db = d // 3
        Z = jnp.einsum('btd,rd->btr', x, V_w)
        Bu = jnp.einsum('btr,dr->btd', Z, U_w)
        h = jax.nn.gelu(jnp.einsum('btd,ed->bte', x, E1_w) + E1_b, approximate=False)
        alpha = jax.nn.sigmoid(jnp.einsum('bte,ce->btc', h, E2_w) + E2_b)
        alpha_rep = jnp.concatenate([jnp.broadcast_to(alpha[..., 0:1], alpha.shape[:-1] + (db,)), jnp.broadcast_to(alpha[..., 1:2], alpha.shape[:-1] + (db,)), jnp.broadcast_to(alpha[..., 2:3], alpha.shape[:-1] + (d - 2 * db,))], axis=-1)
        a_eff = a_base + alpha_rep * jnp.tanh(a_delta)
        lam = jnp.exp(-jax.nn.softplus(-a_eff))

        def step(s, inp):
            l_t, bu_t = inp
            s = l_t * s + bu_t
            return (s, s)
        s0 = jnp.zeros(x.shape[:1] + x.shape[2:], dtype=x.dtype)
        _, S = jax.lax.scan(step, s0, (jnp.swapaxes(lam, 0, 1), jnp.swapaxes(Bu, 0, 1)))
        S = jnp.swapaxes(S, 0, 1)
        y = jnp.einsum('btd,od->bto', S, C_w)
        gate = jax.nn.sigmoid(jnp.einsum('btd,od->bto', x, G_w) + G_b)
        y = jax.nn.gelu(y, approximate=False) * gate
        return x + y

    def _L0_ffn_ref(x, Wg, W1, b1, W2, b2):
        import jax, jax.numpy as jnp
        import numpy as np
        TOP_K = 2
        E = Wg.shape[-1]
        logits = jnp.einsum('btc,ce->bte', x, Wg)
        probs = jax.nn.softmax(logits, axis=-1)
        top_vals, top_idx = jax.lax.top_k(probs, TOP_K)
        gates = (jax.nn.one_hot(top_idx, E, dtype=probs.dtype) * top_vals[..., None]).sum(-2)
        h = jax.nn.relu(jnp.einsum('btc,ech->bteh', x, W1) + b1)
        y = jnp.einsum('bteh,ehc->btec', h, W2) + b2
        out = jnp.einsum('bte,btec->btc', gates, y)
        return out

    def _L1_attn_ref(hidden_states, Wqr, Wqi, Wkr, Wki, Wv):
        import jax, jax.numpy as jnp
        import numpy as np
        H = 12

        def _heads(x, B, S):
            return x.reshape(B, S, H, -1).transpose(0, 2, 1, 3)
        B, S, D = hidden_states.shape
        Dh = D // H
        x = hidden_states
        qr = _heads(x @ Wqr.T, B, S)
        qi = _heads(x @ Wqi.T, B, S)
        kr = _heads(x @ Wkr.T, B, S)
        ki = _heads(x @ Wki.T, B, S)
        v = _heads(x @ Wv.T, B, S)
        scale = 1.0 / jnp.sqrt(jnp.float32(Dh))
        sr = (jnp.einsum('bhqd,bhkd->bhqk', qr, kr) + jnp.einsum('bhqd,bhkd->bhqk', qi, ki)) * scale
        si = (jnp.einsum('bhqd,bhkd->bhqk', qi, kr) - jnp.einsum('bhqd,bhkd->bhqk', qr, ki)) * scale
        scores = jnp.sqrt(sr * sr + si * si)
        probs = jax.nn.softmax(scores, axis=-1)
        ctx = jnp.einsum('bhqk,bhkd->bhqd', probs, v)
        return ctx.transpose(0, 2, 1, 3).reshape(B, S, D)

    def _L1_ffn_ref(x, enc_w, enc_b, sw_w, sw_b, w1, b1, w2, b2):
        import jax, jax.numpy as jnp
        import numpy as np
        H = 192
        R = 64
        E = 8
        B, S = (8, 512)
        b, s, d = x.shape
        xt = x.reshape(-1, d)
        x_enc = xt @ enc_w + enc_b
        route_prob = jax.nn.softmax(x_enc @ sw_w + sw_b, axis=-1)
        route_prob_max = jnp.max(route_prob, axis=-1)
        routes = jnp.argmax(route_prob, axis=-1)
        onehot = jax.nn.one_hot(routes, E, dtype=xt.dtype)
        h = jnp.einsum('td,edr->ter', xt, w1) + b1[None]
        h = jax.nn.gelu(h, approximate=False)
        h = h * onehot[..., None]
        out = jnp.einsum('ter,erd->td', h, w2) + onehot @ b2
        out = out * route_prob_max[:, None]
        return out.reshape(b, s, d)
    h = _L0_tok_ref(x, L0_tok_W)
    h = jnp.concatenate([jnp.broadcast_to(cls_tok, (h.shape[0], 1, h.shape[2])), h], axis=1)
    h = h + _L0_attn_ref(_layernorm(h, axis=-1), L0_attn_V_w, L0_attn_U_w, L0_attn_E1_w, L0_attn_E1_b, L0_attn_E2_w, L0_attn_E2_b, L0_attn_a_base, L0_attn_a_delta, L0_attn_C_w, L0_attn_G_w, L0_attn_G_b)
    h = h + _L0_ffn_ref(_layernorm(h, axis=-1), L0_ffn_Wg, L0_ffn_W1, L0_ffn_b1, L0_ffn_W2, L0_ffn_b2)
    h = h + _L1_attn_ref(_layernorm(h, axis=-1), L1_attn_Wqr, L1_attn_Wqi, L1_attn_Wkr, L1_attn_Wki, L1_attn_Wv)
    h = h + _L1_ffn_ref(_layernorm(h, axis=-1), L1_ffn_enc_w, L1_ffn_enc_b, L1_ffn_sw_w, L1_ffn_sw_b, L1_ffn_w1, L1_ffn_b1, L1_ffn_w2, L1_ffn_b2)
    return h

_drawn_inputs = setup_inputs


def setup_inputs(seed=0):
    import zlib

    import numpy as np

    out = dict(_drawn_inputs(seed))
    spreads = {'L0_attn_E1_b': (0.0, 2.0),
     'L0_attn_E2_b': (0.0, 2.0),
     'L0_attn_G_b': (0.0, 0.8),
     'L0_ffn_b1': (0.0, 0.712),
     'L0_ffn_b2': (0.0, 0.512)}
    factors = {'L0_attn_V_w': 2.732,
     'L0_attn_E1_w': 64.0,
     'L0_attn_E2_w': 64.0,
     'L0_attn_a_base': 64.0,
     'L0_attn_a_delta': 64.0,
     'L0_attn_C_w': 2.862,
     'L0_attn_G_w': 6.341,
     'L1_attn_Wqr': 8.0,
     'L1_attn_Wqi': 8.0,
     'L1_attn_Wkr': 8.0,
     'L1_attn_Wki': 8.0,
     'L1_ffn_enc_b': 8.0,
     'L1_ffn_sw_b': 4.075,
     'L1_ffn_b1': 25.819,
     'L1_ffn_b2': 6.318}
    for name, (base, spread) in spreads.items():
        noise = np.random.default_rng([zlib.crc32(name.encode()), seed]).standard_normal(out[name].shape)
        drawn = base * np.exp(spread * noise) if base else spread * noise
        out[name] = jnp.asarray(drawn.astype(out[name].dtype))
    for name, factor in factors.items():
        out[name] = (out[name] * factor).astype(out[name].dtype)
    return out
```

```python
from contextlib import ExitStack

import concourse.bass as bass
from concourse import mybir

ALU = mybir.AluOpType
ACT = mybir.ActivationFunctionType
AX = mybir.AxisListType
F32 = mybir.dt.float32

P = 128
B, T, D = 32, 50, 192
FG = 96
HALF = 64
CB = 8
CT = CB * T
CW = CB * HALF
TILES = CB // 2
CHUNKS = B // CB
NT = B // 2
KC = 6
E = 8
HID = 768
HC = HID // P
R1 = 64
HEADS, DH = 12, 16
HG = 3
EPS = 1e-5
HW = 2 * T
VW = DH + 1
SCALE2 = 1.0 / DH
OFF = 1e18


def build(nc, A, out, stage="all"):
    with ExitStack() as ctx:
        def sb(name, shape, dt=F32):
            return ctx.enter_context(nc.sbuf_tensor(name, shape, dt))

        def sem(name):
            return ctx.enter_context(nc.semaphore(name))

        def seqs(ap):
            return ap.rearrange("p (s t) -> p s t", t=HALF)[:, :, 0:T]

        def packed(ap):
            return ap.rearrange("p (s t) -> p s t", t=T)

        ps = ctx.enter_context(nc.psum_tensor("ps", [P, 8, 512], F32))

        w_tok = sb("w_tok", [P, KC, D])
        cls_row = sb("cls_row", [1, D])
        cls_at = sb("cls_at", [1, P])
        v_w = sb("v_w", [FG, 2, 16])
        u_w = sb("u_w", [16, D])
        e1_w = sb("e1_w", [FG + 1, 2, 64])
        e2_w = sb("e2_w", [64, D])
        e2_b = sb("e2_b", [FG, 2])
        a_base = sb("a_base", [FG, 2])
        a_delta = sb("a_delta", [FG, 2])
        tanh_delta = sb("tanh_delta", [FG, 2])
        half_e2_b = sb("half_e2_b", [FG, 2])
        lam_scale = sb("lam_scale", [FG, 2])
        lam_bias = sb("lam_bias", [FG, 2])
        lam_mid = sb("lam_mid", [FG, 2])
        c_w = sb("c_w", [FG, 2, D])
        g_w = sb("g_w", [FG + 1, 2, D])
        gate_w = sb("gate_w", [FG, 2, E])
        ident = sb("ident", [P, P])
        neg_half = sb("neg_half", [P, TILES])
        eps = sb("eps", [P, TILES])

        expert_rank = sb("expert_rank", [P, E])
        wq = sb("wq", [FG, 2, HG * P])
        wk = sb("wk", [FG, 2, HG * P])
        wv = sb("wv", [FG, 2, D])
        to_kk = sb("to_kk", [P, P])
        enc_w = sb("enc_w", [FG, 2, R1])
        enc_b = sb("enc_b", [R1, 1])
        sw_w = sb("sw_w", [R1 + 1, E])
        s_w1 = sb("s_w1", [FG + E, 2, E * R1])
        s_w2 = sb("s_w2", [P, 4, D])
        s_b2 = sb("s_b2", [FG + E, D])

        def two(name, shape):
            return [sb(f"{name}{u}", shape) for u in range(2)]

        stats = two("stats", [P, TILES, 6])
        meanvar = two("meanvar", [P, TILES, 2])
        rstd = two("rstd", [P, TILES])
        carrier = two("carrier", [P, 6])
        x_tok = two("x_tok", [P, TILES, D])
        xT = two("xT", [FG + E, 2, CW])
        h = sb("h", [P, NT, D])
        logits = sb("logits", [P, NT, E])
        route_max = sb("route_max", [P, NT])
        route_sum = sb("route_sum", [P, NT])
        probs = sb("probs", [P, NT, E])
        best = sb("best", [P, NT])
        rank = sb("rank", [P, NT, E])
        first = sb("first", [P, NT, E])
        others = sb("others", [P, NT, E])
        second = sb("second", [P, NT, E])
        gates = sb("gates", [P, NT, E])

        early = ExitStack()

        def sb(name, shape, dt=F32):
            return early.enter_context(nc.sbuf_tensor(name, shape, dt))

        patches = two("patches", [P, KC, CW])
        h_plus_x = two("h_plus_x", [P, TILES, D])
        zT = two("zT", [16, CW])
        gelu_e = two("gelu_e", [64, CT])
        lam = two("lam", [FG, 2, CW])
        sT = two("sT", [FG, 2, CW])
        gelu_y = two("gelu_y", [P, TILES, D])
        tanh_g = two("tanh_g", [P, TILES, D])
        x2T = sb("x2T", [FG, CHUNKS, 2, CW])
        w1 = two("w1", [FG, 2, HID])
        w2 = two("w2", [P, HC, D])
        b1 = two("b1", [P, HC])
        b2 = two("b2", [1, D])
        ones_row = sb("ones_row", [1, P])
        hidT = two("hidT", [P, HC, CW])
        early.close()

        def sb(name, shape, dt=F32):
            return ctx.enter_context(nc.sbuf_tensor(name, shape, dt))

        q = two("q", [P, HG, CW])
        kk = two("kk", [P, HG, CB, 2, T])
        vals = two("vals", [P, CB, HEADS // 2, 2, VW])
        squares = two("squares", [P, HEADS, 2, T])
        sc = two("sc", [P, TILES * HEADS, HALF])
        sc_max = two("sc_max", [P, TILES * HEADS])
        probsT = two("probsT", [P, HEADS // 2, P])
        inv_sum = two("inv_sum", [P, HEADS])
        ctx_tok = two("ctx_tok", [P, TILES, D])
        xeT = two("xeT", [R1 + 1, CW])
        s_logits = two("s_logits", [P, TILES, E])
        s_max = two("s_max", [P, TILES])
        s_exp = two("s_exp", [P, TILES, E])
        s_sum = two("s_sum", [P, TILES])
        s_prob = two("s_prob", [P, TILES])
        s_rank = two("s_rank", [P, TILES, E])
        s_best = two("s_best", [P, TILES])
        s_onehot = two("s_onehot", [P, TILES, E])
        s_hidT = two("s_hidT", [P, 4, CW])
        out_tok = two("out_tok", [P, TILES, D])

        load = sem("load")
        ident_zero = sem("ident_zero")
        ident_done = sem("ident_done")
        cls_zero = sem("cls_zero")
        const_done = sem("const_done")
        patches_in = [sem("patches_in0"), sem("patches_in1")]
        patch_done = sem("patch_done")
        stats_done, var_done, eps_added, rstd_done, x_done, xT_in_psum, xT_done = (
            [sem(f"{name}{n}") for n in range(4)]
            for name in ("stats_done", "var_done", "eps_added", "rstd_done", "x_done", "xT_in_psum", "xT_done"))
        w_in = [sem("w_in0"), sem("w_in1")]
        route_bias = sem("route_bias")
        x2T_done = sem("x2T_done")
        logits_in_psum = sem("logits_in_psum")
        logits_done = sem("logits_done")
        route_max_done = sem("route_max_done")
        shifted_done = sem("shifted_done")
        route_exp_done = sem("route_exp_done")
        route_sum_done = sem("route_sum_done")
        route_inv_done = sem("route_inv_done")
        probs_done = sem("probs_done")
        best1_done = sem("best1_done")
        eq1_done = sem("eq1_done")
        rank1_done = sem("rank1_done")
        rankmax1_done = sem("rankmax1_done")
        first_done = sem("first_done")
        others_done = sem("others_done")
        best2_done = sem("best2_done")
        eq2_done = sem("eq2_done")
        rank2_done = sem("rank2_done")
        rankmax2_done = sem("rankmax2_done")
        second_done = sem("second_done")
        both_done = sem("both_done")
        gates_done = sem("gates_done")
        experts_zero = sem("experts_zero")
        hid_in_psum = sem("hid_in_psum")
        relu_act_done = sem("relu_act_done")
        relu_dve_done = sem("relu_dve_done")
        moe_in_psum = sem("moe_in_psum")
        moe_added = sem("moe_added")
        late_zero = sem("late_zero")
        late_const = sem("late_const")
        kk_map_zero = sem("kk_map_zero")
        kk_map_half = sem("kk_map_half")
        kk_map_done = sem("kk_map_done")
        q_in_psum = sem("q_in_psum")
        q_done = sem("q_done")
        k_in_psum = sem("k_in_psum")
        k_done = sem("k_done")
        v_in_psum = sem("v_in_psum")
        v_low_done = sem("v_low_done")
        v_high_done = sem("v_high_done")
        kk_in_psum = sem("kk_in_psum")
        kk_act_done = sem("kk_act_done")
        kk_dve_done = sem("kk_dve_done")
        scores_in_psum = sem("scores_in_psum")
        squares_done = sem("squares_done")
        sc2_done = sem("sc2_done")
        sc2_max_done = sem("sc2_max_done")
        sqrt_done = sem("sqrt_done")
        sqrt_max_done = sem("sqrt_max_done")
        sc_shifted = sem("sc_shifted")
        exp_done = sem("exp_done")
        pT_in_psum = sem("pT_in_psum")
        pT_act_done = sem("pT_act_done")
        pT_dve_done = sem("pT_dve_done")
        ctx_in_psum = sem("ctx_in_psum")
        inv_sum_done = sem("inv_sum_done")
        ctx_scaled = sem("ctx_scaled")
        attended = sem("attended")
        enc_in_psum = sem("enc_in_psum")
        enc_done = sem("enc_done")
        s_logits_in_psum = sem("s_logits_in_psum")
        s_logits_done = sem("s_logits_done")
        s_max_done = sem("s_max_done")
        s_shifted = sem("s_shifted")
        s_exp_done = sem("s_exp_done")
        s_sum_done = sem("s_sum_done")
        s_prob_done = sem("s_prob_done")
        s_eq_done = sem("s_eq_done")
        s_rank_done = sem("s_rank_done")
        s_best_done = sem("s_best_done")
        onehot_done = sem("onehot_done")
        onehotT_in_psum = sem("onehotT_in_psum")
        onehotT_done = sem("onehotT_done")
        s_hid_in_psum = sem("s_hid_in_psum")
        s_hid_done = sem("s_hid_done")
        s_out_in_psum = sem("s_out_in_psum")
        out_ready = sem("out_ready")
        hx_done = sem("hx_done")
        ze_done = sem("ze_done")
        zT_done = sem("zT_done")
        gelu_e_done = sem("gelu_e_done")
        bu_done = sem("bu_done")
        tanh_alpha_done = sem("tanh_alpha_done")
        tanh_lam_done = sem("tanh_lam_done")
        lam_done = sem("lam_done")
        lam_mid_done = sem("lam_mid_done")
        lam_coef_done = sem("lam_coef_done")
        scan_done = sem("scan_done")
        yg_done = sem("yg_done")
        gelu_y_done = sem("gelu_y_done")
        tanh_g_done = sem("tanh_g_done")
        gated_done = sem("gated_done")
        h_done = sem("h_done")
        tanh_done = sem("tanh_done")
        out_done = sem("out_done")

        MOE0 = 5

        def count(cc, u):
            return 2 * cc + u + 1

        def chunk_of(buf, cc, u):
            return buf[:, bass.ds((2 * cc + u) * TILES, TILES), :]

        def tile_of(buf, cc, u, i):
            return buf[:, bass.ds((2 * cc + u) * TILES + i, 1), :].rearrange("p i d -> p (i d)")

        def one(ap, e):
            ap = ap[bass.ds(e, 1)]
            return ap.rearrange("e p n -> (e p) n") if len(ap.shape) == 3 else ap.rearrange("e p k n -> (e p) k n")

        def spread(ap, n):
            return bass.AP(ap.tensor, ap.offset, [*map(list, ap.ap), [0, n]])

        def spread_rank(n):
            ap = expert_rank[:, :]
            return bass.AP(ap.tensor, ap.offset, [list(ap.ap[0]), [0, n], [1, E]])

        loads = [
            (w_tok[:, :, :], A["w_tok"]), (cls_row[:, :], A["cls"]),
            (v_w[:, :, :], A["V"]), (u_w[:, :], A["U"]),
            (e1_w[:, :, :], A["E1"]), (e2_w[:, :], A["E2"]), (e2_b[:, :], A["E2b"]),
            (a_base[:, :], A["a_base"]), (a_delta[:, :], A["a_delta"]),
            (c_w[:, :, :], A["C"]), (g_w[:, :, :], A["G"]), (gate_w[:, :, :], A["Wg"]),
            (wq[:, :, :], A["Wq"]), (wk[:, :, :], A["Wk"]), (wv[:, :, :], A["Wv"]),
            (enc_w[:, :, :], A["enc_w"]), (enc_b[:, :], A["enc_b"]), (sw_w[:, :], A["sw"]),
            (s_w1[0:FG, :, :], A["s_w1"]), (s_w2[:, :, :], A["s_w2"]), (s_b2[FG:FG + E, :], A["s_b2"]),
        ]
        LOADED = 16 * len(loads)

        def tokv(slot, width=D):
            return ps[:, slot:slot + 2, 0:2 * width].rearrange("p b (i d) -> p b i d", i=2)

        def tok(buf):
            return buf[:, :, :].rearrange("p (b i) d -> p b i d", b=2)

        with nc.Block() as block:

            @block.sync
            def _(sp):
                for c in range(2):
                    sp.dma_start(patches[c][:, :, :], A["patches"][c]).then_inc(patches_in[c], 16)
                    if c == 0:
                        for dst, src in loads:
                            sp.dma_start(dst, src).then_inc(load, 16)
                for c in range(2, CHUNKS):
                    sp.wait_ge(patch_done, c - 1)
                    sp.dma_start(patches[c % 2][:, :, :], A["patches"][c]).then_inc(patches_in[c % 2], 16)
                sp.wait_ge(const_done, 1)
                for e in range(E):
                    sp.dma_start(s_w1[FG + e:FG + e + 1, 1, R1 * e:R1 * e + R1], A["s_b1"][e:e + 1, :]).then_inc(route_bias, 16)
                sp.wait_ge(route_bias, 16 * E)
                sp.wait_ge(experts_zero, 1)
                if stage != "A":
                  with sp.Fori(0, E // 2) as ee:
                    for v in range(2):
                        sp.wait_ge(moe_in_psum, MOE0 + 8 * ee + 4 * v - 4)
                        for dst, name in ((w1[v][:, :, :], "W1"), (w2[v][:, :, :], "W2"), (b1[v][:, :], "b1"),
                                          (b2[v][:, :], "b2")):
                            sp.dma_start(dst, one(A[name], 2 * ee + v)).then_inc(w_in[v], 16)
                if stage == "all":
                    for c in range(CHUNKS):
                        sp.wait_ge(out_ready, c + 1)
                        for half in range(2):
                            sp.dma_start(
                                out[CT * c:CT * c + CT, :].rearrange("(i two t) d -> two t i d", two=2, t=T)[half],
                                out_tok[c % 2][HALF * half:HALF * half + T, :, :]).then_inc(out_done, 16)
                    sp.wait_ge(out_done, 32 * CHUNKS)
                else:
                    sp.wait_ge(*{"A": (h_done, CHUNKS), "B": (moe_added, E * CHUNKS), "C": (attended, CHUNKS)}[stage])
                    for half in range(2):
                        sp.dma_start(out.rearrange("(i two t) d -> two t i d", two=2, t=T)[half],
                                     h[HALF * half:HALF * half + T, :, :]).then_inc(out_done, 16)
                    sp.wait_ge(out_done, 32)

            @block.gpsimd
            def _(pool):
                nc.gpsimd.memset(neg_half[:, :], -0.5)
                nc.gpsimd.memset(eps[:, :], EPS)
                nc.gpsimd.memset(ident[:, :], 0.0).then_inc(ident_zero, 1)
                pool.wait_ge(ident_zero, 1)
                nc.gpsimd.affine_select(out=ident[:, :], in_=ident[:, :], compare_op=ALU.not_equal, fill=1.0,
                                        base=0, pattern=[[-1, P]], channel_multiplier=1).then_inc(ident_done, 1)

                halves = to_kk[:, :].rearrange("p (h two d) -> p h two d", h=4, two=2)
                nc.gpsimd.memset(to_kk[:, :], 0.0).then_inc(kk_map_zero, 1)
                pool.wait_ge(kk_map_zero, 1)
                nc.gpsimd.affine_select(out=halves[:, :, 0, :], in_=halves[:, :, 0, :], compare_op=ALU.not_equal,
                                        fill=-1.0, base=-DH, pattern=[[-2 * DH, 4], [-1, DH]],
                                        channel_multiplier=1).then_inc(kk_map_half, 1)
                pool.wait_ge(kk_map_half, 1)
                nc.gpsimd.affine_select(out=halves[:, :, 1, :], in_=halves[:, :, 1, :], compare_op=ALU.not_equal,
                                        fill=1.0, base=0, pattern=[[-2 * DH, 4], [-1, DH]],
                                        channel_multiplier=1).then_inc(kk_map_done, 1)

                def inverse_deviation(norm, u, n):
                    pool.wait_ge(var_done[norm], n)
                    nc.gpsimd.tensor_tensor(rstd[u][:, :], meanvar[u][:, :, 1], eps[:, :],
                                            ALU.add).then_inc(eps_added[norm], 1)
                    pool.wait_ge(eps_added[norm], n)
                    nc.gpsimd.tensor_tensor(rstd[u][:, :], rstd[u][:, :], neg_half[:, :],
                                            ALU.pow).then_inc(rstd_done[norm], 1)

                for layer in range(2 if stage in ("all", "C") else 1):
                    with pool.Fori(0, CHUNKS // 2) as cc:
                        for norm in (2 * layer, 2 * layer + 1)[:1 if (stage, layer) == ("C", 1) else 2]:
                            for u in range(2):
                                inverse_deviation(norm, u, count(cc, u))

            @block.tensor
            def _(pe):
                pe.wait_ge(const_done, 1)
                pe.wait_ge(ident_done, 1)

                def turn(norm, u, banks, n):
                    pe.wait_ge(x_done[norm], n)
                    for i in range(TILES):
                        for g in range(2):
                            mm = pe.transpose(ps[0:FG, banks + g, P * i:P * i + P],
                                              x_tok[u][:, i, FG * g:FG * g + FG], ident[:, :])
                    mm.then_inc(xT_in_psum[norm], 1)
                pe.wait_ge(load, LOADED)
                with pe.Fori(0, CHUNKS // 2) as cc:
                    X = [0, 4]
                    Y = [2, 6]
                    for u in range(2):
                        pe.wait_ge(patches_in[u], 16 * cc + 16)
                        for i in range(TILES):
                            dst = tokv(X[u])[:, i // 2, i % 2, :]
                            for k in range(KC):
                                pe.matmul(dst, patches[u][:, k, P * i:P * i + P],
                                          w_tok[:, k, :], start=(k == 0), stop=False)
                            mm = pe.matmul(dst, cls_at[:, :], cls_row[:, :], start=False, stop=True)
                        mm.then_inc(patch_done, 1)
                    for u in range(2):
                        turn(0, u, Y[u], count(cc, u))
                    for u in range(2):
                        pe.wait_ge(hx_done, 2 * cc + u + 1)
                        pe.wait_ge(xT_done[0], 2 * cc + u + 1)
                        for g in range(2):
                            pe.matmul(ps[0:16, X[u], 0:CT], v_w[:, g, :], seqs(xT[u][0:FG, g, :]),
                                      start=(g == 0), stop=(g == 1))
                        for g in range(2):
                            k = FG + g
                            mm = pe.matmul(ps[0:64, X[u] + 1, 0:CT], e1_w[0:k, g, :], seqs(xT[u][0:k, g, :]),
                                           start=(g == 0), stop=(g == 1))
                        mm.then_inc(ze_done, 1)
                    for u in range(2):
                        pe.wait_ge(zT_done, 2 * cc + u + 1)
                        for g in range(2):
                            pe.matmul(ps[0:FG, Y[u] + g, :], u_w[:, FG * g:FG * g + FG], zT[u][:, :],
                                      start=True, stop=True)
                        pe.wait_ge(gelu_e_done, 2 * cc + u + 1)
                        for g in range(2):
                            mm = pe.matmul(ps[0:FG, X[u] + g, 0:CT], e2_w[:, FG * g:FG * g + FG], gelu_e[u][:, :],
                                           start=True, stop=True)
                        mm.then_inc(bu_done, 1)
                    for u in range(2):
                        pe.wait_ge(scan_done, 2 * cc + u + 1)
                        pe.wait_ge(tanh_alpha_done, 2 * cc + u + 1)
                        for i in range(TILES):
                            for g in range(2):
                                pe.matmul(tokv(X[u])[:, i // 2, i % 2, :],
                                          sT[u][:, g, P * i:P * i + P], c_w[:, g, :],
                                          start=(g == 0), stop=(g == 1))
                        for i in range(TILES):
                            for g in range(2):
                                mm = pe.matmul(tokv(Y[u])[:, i // 2, i % 2, :],
                                               xT[u][0:FG + g, g, P * i:P * i + P], g_w[0:FG + g, g, :],
                                               start=(g == 0), stop=(g == 1))
                        mm.then_inc(yg_done, 1)

                    for u in range(2):
                        pe.wait_ge(gelu_y_done, count(cc, u))
                        turn(1, u, X[u], count(cc, u))
                    for u in range(2):
                        pe.wait_ge(xT_done[1], count(cc, u))
                        pe.wait_ge(tanh_g_done, count(cc, u))
                        for i in range(TILES):
                            for g in range(2):
                                mm = pe.matmul(ps[:, Y[u], E * i:E * i + E], xT[u][0:FG, g, P * i:P * i + P],
                                               gate_w[:, g, :], start=(g == 0), stop=(g == 1))
                        mm.then_inc(logits_in_psum, 1)

                if stage == "A":
                    return
                pe.wait_ge(logits_done, CHUNKS)
                pe.wait_ge(x2T_done, CHUNKS)
                with pe.Fori(0, E // 2) as ee:
                    for v in range(2):
                        pe.wait_ge(w_in[v], 64 * ee + 64)
                        for c in range(CHUNKS):
                            k = HC // 2 * (CHUNKS * v + c)
                            per = HC // 2 * CHUNKS * 2
                            for m in range(HC):
                                pe.wait_ge(relu_dve_done if m % 2 else relu_act_done, per * ee + k + m // 2 + 1)
                                for g in range(2):
                                    mm = pe.matmul(ps[:, (HC * c + m) % 4, 0:CT], w1[v][:, g, P * m:P * m + P],
                                                   seqs(x2T[:, c, g, :]), start=(g == 0), stop=(g == 1))
                                mm.then_inc(hid_in_psum, 1)
                            pe.wait_ge(moe_added, 8 * ee + 4 * v + c)
                            for m in range(HC):
                                pe.wait_ge(relu_dve_done if m % 2 else relu_act_done, per * ee + k + m // 2 + 3)
                                for i in range(TILES):
                                    pe.matmul(ps[:, 4 + i, 0:D], hidT[c % 2][:, m, P * i:P * i + P], w2[v][:, m, :],
                                              start=(m == 0), stop=False)
                            for i in range(TILES):
                                mm = pe.matmul(ps[:, 4 + i, 0:D], ones_row[:, :], b2[v][:, :], start=False, stop=True)
                            mm.then_inc(moe_in_psum, 1)

                if stage == "B":
                    return
                pe.wait_ge(kk_map_done, 1)
                pe.wait_ge(route_bias, 16 * E)
                pe.wait_ge(late_const, 1)
                pe.wait_ge(moe_added, E * CHUNKS)
                with pe.Fori(0, CHUNKS // 2) as cc:
                    W = [0, 4]
                    for u in range(2):
                        turn(2, u, W[u], count(cc, u))
                    for u in range(2):
                        pe.wait_ge(xT_done[2], count(cc, u))
                        for j in range(HG):
                            for bank, w, read, done, there in ((2, wq, 0, q_done, q_in_psum), (3, wk, 1, k_done, k_in_psum)):
                                if j == 2:
                                    pe.wait_ge(done, 3 * (2 * cc + u) + 1)
                                for g in range(2):
                                    mm = pe.matmul(ps[:, W[u] + (bank if j != 1 else read), 0:CT],
                                                   w[:, g, P * j:P * j + P], seqs(xT[u][0:FG, g, :]),
                                                   start=(g == 0), stop=(g == 1))
                                mm.then_inc(there, 1)
                        pe.wait_ge(q_done, 3 * (2 * cc + u) + 2)
                        pe.wait_ge(k_done, 3 * (2 * cc + u) + 2)
                        for s_ in range(CB):
                            for odd in range(2):
                                for g in range(2):
                                    mm = pe.matmul(ps[HALF * odd:HALF * odd + HALF, W[u] + s_ // 4,
                                                      FG * (s_ % 4):FG * (s_ % 4) + FG],
                                                   xT[u][0:FG, g, HALF * s_:HALF * s_ + HALF],
                                                   wv[:, g, FG * odd:FG * odd + FG], start=(g == 0), stop=(g == 1))
                        mm.then_inc(v_in_psum, 1)
                    for u in range(2):
                        pe.wait_ge(q_done, 3 * (2 * cc + u) + 3)
                        pe.wait_ge(k_done, 3 * (2 * cc + u) + 3)
                        for j in range(HG):
                            if j == 2:
                                pe.wait_ge(v_low_done, count(cc, u))
                                pe.wait_ge(v_high_done, count(cc, u))
                            mm = pe.matmul(ps[:, W[u] + (2, 3, 0)[j], 0:CT], to_kk[:, :], kk[u][:, j, :, 0, :],
                                           start=True, stop=True).then_inc(kk_in_psum, 1)
                    for i in range(TILES):
                        for u in range(2):
                            if i == 0:
                                pe.wait_ge(kk_act_done, 2 * (2 * cc + u) + 2)
                                pe.wait_ge(kk_dve_done, count(cc, u))
                            else:
                                pe.wait_ge(squares_done, 8 * cc + 2 * i + u - 1)
                            for b in range(2):
                                for j in range(HG):
                                    for r in range(4):
                                        mm = pe.matmul(ps[HALF * b:HALF * b + HALF, W[u] + r, HW * j:HW * j + HW],
                                                       q[u][32 * r:32 * r + 32, j, P * i + HALF * b:P * i + HALF * b + HALF],
                                                       kk[u][32 * r:32 * r + 32, j, 2 * i + b, :, :],
                                                       start=True, stop=True)
                            mm.then_inc(scores_in_psum, 1)
                    for i in range(TILES + 1):
                        for u in range(2):
                            t = 8 * cc + 2 * i + u
                            if i < TILES:
                                if i == 0:
                                    pe.wait_ge(exp_done, count(cc, u))
                                    pe.wait_ge(squares_done, 8 * cc + 7 + u)
                                else:
                                    pe.wait_ge(pT_act_done, t - 1)
                                    pe.wait_ge(pT_dve_done, t - 1)
                                for pr in range(HEADS // 2):
                                    h0 = HEADS * i + 2 * pr
                                    mm = pe.transpose(ps[:, W[u] + pr // 3, P * (pr % 3):P * (pr % 3) + P],
                                                      sc[u][:, h0:h0 + 2, :].rearrange("p h k -> p (h k)"), ident[:, :])
                                mm.then_inc(pT_in_psum, 1)
                            if i >= 1:
                                pe.wait_ge(pT_act_done, t - 1)
                                pe.wait_ge(pT_dve_done, t - 1)
                                if i >= 3:
                                    pe.wait_ge(ctx_scaled, t - 5)
                                for b in range(2):
                                    for pr in range(HEADS // 2):
                                        mm = pe.matmul(ps[HALF * b:HALF * b + HALF, W[u] + 2 + i % 2,
                                                          2 * VW * pr:2 * VW * pr + 2 * VW],
                                                       probsT[u][:, pr, HALF * b:HALF * b + HALF],
                                                       vals[u][:, 2 * (i - 1) + b, pr, :, :], start=True, stop=True)
                                mm.then_inc(ctx_in_psum, 1)
                    if stage == "C":
                        pe.wait_ge(ctx_scaled, 8 * cc + 8)
                        return
                    for u in range(2):
                        turn(3, u, W[u], count(cc, u))
                    for u in range(2):
                        pe.wait_ge(xT_done[3], count(cc, u))
                        pe.wait_ge(ctx_scaled, 8 * cc + 8)
                        for g in range(2):
                            mm = pe.matmul(ps[0:R1, W[u] + 2, 0:CT], enc_w[:, g, :], seqs(xT[u][0:FG, g, :]),
                                           start=(g == 0), stop=(g == 1))
                        mm.then_inc(enc_in_psum, 1)
                    for u in range(2):
                        pe.wait_ge(enc_done, count(cc, u))
                        for i in range(TILES):
                            mm = pe.matmul(ps[:, W[u] + 3, E * i:E * i + E], xeT[u][:, P * i:P * i + P], sw_w[:, :],
                                           start=True, stop=True)
                        mm.then_inc(s_logits_in_psum, 1)
                    for u in range(2):
                        pe.wait_ge(onehot_done, count(cc, u))
                        for i in range(TILES):
                            mm = pe.matmul(ps[FG:FG + E, W[u] + 2, P * i:P * i + P], s_onehot[u][:, i, :], ident[:, :],
                                           start=True, stop=True)
                        mm.then_inc(onehotT_in_psum, 1)
                    for u in range(2):
                        pe.wait_ge(onehotT_done, count(cc, u))
                        for m in range(4):
                            for g in range(2):
                                k = FG + E * g
                                mm = pe.matmul(ps[:, W[u] + m, 0:CT], s_w1[0:k, g, P * m:P * m + P],
                                               seqs(xT[u][0:k, g, :]), start=(g == 0), stop=(g == 1))
                            mm.then_inc(s_hid_in_psum, 1)
                    for u in range(2):
                        pe.wait_ge(s_hid_done, 4 * (2 * cc + u) + 4)
                        for i in range(TILES):
                            dst = tokv(W[u])[:, i // 2, i % 2, :]
                            for m in range(4):
                                pe.matmul(dst, s_hidT[u][:, m, P * i:P * i + P], s_w2[:, m, :], start=(m == 0), stop=False)
                            mm = pe.matmul(dst, xT[u][FG:FG + E, 1, P * i:P * i + P], s_b2[FG:FG + E, :],
                                           start=False, stop=True)
                        mm.then_inc(s_out_in_psum, 1)

            @block.scalar
            def _(act):
                act.wait_ge(load, LOADED)
                act.wait_ge(const_done, 1)
                nc.scalar.activation(tanh_delta[:, :], a_delta[:, :], ACT.Tanh).then_inc(tanh_done, 1)
                act.wait_ge(lam_coef_done, 3)

                def turned(norm, u, banks, n):
                    act.wait_ge(xT_in_psum[norm], n)
                    for g in range(2):
                        last = nc.scalar.copy(seqs(xT[u][0:FG, g, :]), seqs(ps[0:FG, banks + g, :]))
                    last.then_inc(xT_done[norm], 1)

                X = [0, 4]
                Y = [2, 6]
                with act.Fori(0, CHUNKS // 2) as cc:
                    for u in range(2):
                        turned(0, u, Y[u], count(cc, u))
                    for u in range(2):
                        act.wait_ge(ze_done, 2 * cc + u + 1)
                        nc.scalar.copy(seqs(zT[u][:, :]), packed(ps[0:16, X[u], 0:CT])).then_inc(zT_done, 1)
                        nc.scalar.activation(gelu_e[u][:, :], ps[0:64, X[u] + 1, 0:CT],
                                             ACT.Gelu).then_inc(gelu_e_done, 1)
                    for u in range(2):
                        act.wait_ge(bu_done, 2 * cc + u + 1)
                        for g in range(2):
                            last = nc.scalar.activation(seqs(lam[u][:, g, :]), packed(ps[0:FG, X[u] + g, 0:CT]),
                                                        ACT.Tanh, bias=half_e2_b[:, g:g + 1], scale=0.5)
                        last.then_inc(tanh_alpha_done, 1)
                        act.wait_ge(tanh_alpha_done, 2 * cc + u + 1)
                        for g in range(2):
                            last = nc.scalar.activation(seqs(lam[u][:, g, :]), seqs(lam[u][:, g, :]),
                                                        ACT.Tanh, bias=lam_bias[:, g:g + 1],
                                                        scale=lam_scale[:, g:g + 1])
                        last.then_inc(tanh_lam_done, 1)
                    for u in range(2):
                        act.wait_ge(yg_done, 2 * cc + u + 1)
                        nc.scalar.activation(tok(gelu_y[u]), tokv(X[u]), ACT.Gelu).then_inc(gelu_y_done, 1)
                        nc.scalar.activation(tok(tanh_g[u]), tokv(Y[u]), ACT.Tanh,
                                             scale=0.5).then_inc(tanh_g_done, 1)

                    for u in range(2):
                        turned(1, u, X[u], count(cc, u))
                if stage == "A":
                    return

                act.wait_ge(shifted_done, 1)
                nc.scalar.activation(probs[:, :, :], probs[:, :, :], ACT.Exp).then_inc(route_exp_done, 1)
                act.wait_ge(experts_zero, 1)
                with act.Fori(0, E // 2) as ee:
                    for v in range(2):
                        for c in range(CHUNKS):
                            act.wait_ge(moe_in_psum, MOE0 + 8 * ee + 4 * v + c - 1)
                            for m in range(0, HC, 2):
                                act.wait_ge(hid_in_psum, HC * (8 * ee + 4 * v + c) + m + 1)
                                nc.scalar.activation(seqs(hidT[c % 2][:, m, :]), packed(ps[:, (HC * c + m) % 4, 0:CT]),
                                                     ACT.Relu, bias=b1[v][:, m:m + 1]).then_inc(relu_act_done, 1)
                if stage == "B":
                    return
                act.wait_ge(late_const, 1)
                W = [0, 4]
                with act.Fori(0, CHUNKS // 2) as cc:
                    for u in range(2):
                        turned(2, u, W[u], count(cc, u))
                    for u in range(2):
                        for j in range(HG):
                            act.wait_ge(q_in_psum, 3 * (2 * cc + u) + j + 1)
                            nc.scalar.copy(seqs(q[u][:, j, :]), packed(ps[:, W[u] + (2, 0, 2)[j], 0:CT])).then_inc(q_done, 1)
                        act.wait_ge(v_in_psum, count(cc, u))
                        for bank in range(2):
                            last = nc.scalar.copy(
                                vals[u][0:HALF, 4 * bank:4 * bank + 4, :, 0, 0:DH],
                                ps[0:HALF, W[u] + bank, 0:4 * FG].rearrange("p (s h d) -> p s h d", s=4, d=DH))
                        last.then_inc(v_low_done, 1)
                    for u in range(2):
                        for n, j in enumerate((0, 2)):
                            act.wait_ge(kk_in_psum, 3 * (2 * cc + u) + j + 1)
                            nc.scalar.copy(kk[u][:, j, :, 1, :], packed(ps[:, W[u] + (2, 3, 0)[j], 0:CT])).then_inc(kk_act_done, 1)
                    for i in range(TILES):
                        for u in range(2):
                            act.wait_ge(scores_in_psum, 8 * cc + 2 * i + u + 1)
                            if i:
                                act.wait_ge(sc2_done, 8 * cc + 2 * i + u - 1)
                            nc.scalar.activation(squares[u][:, :, :, :].rearrange("p (r j) c k -> p r (j c k)", r=4),
                                                 ps[:, W[u]:W[u] + 4, 0:HG * HW], ACT.Square).then_inc(squares_done, 1)
                    for u in range(2):
                        act.wait_ge(sc2_max_done, 8 * cc + 7 + u)
                        nc.scalar.activation(sc[u][:, :, 0:T], sc[u][:, :, 0:T], ACT.Sqrt,
                                             scale=SCALE2).then_inc(sqrt_done, 1)
                        nc.scalar.activation(sc_max[u][:, :], sc_max[u][:, :], ACT.Sqrt,
                                             scale=SCALE2).then_inc(sqrt_max_done, 1)
                    for u in range(2):
                        act.wait_ge(sc_shifted, count(cc, u))
                        nc.scalar.activation(sc[u][:, :, 0:T], sc[u][:, :, 0:T], ACT.Exp).then_inc(exp_done, 1)
                    for i in range(TILES):
                        for u in range(2):
                            act.wait_ge(pT_in_psum, 8 * cc + 2 * i + u + 1)
                            if i:
                                act.wait_ge(ctx_in_psum, 8 * cc + 2 * i + u - 1)
                            nc.scalar.copy(probsT[u][:, 0:3, :], ps[:, W[u], 0:3 * P]).then_inc(pT_act_done, 1)
                    if stage == "C":
                        return
                    for u in range(2):
                        turned(3, u, W[u], count(cc, u))
                    for u in range(2):
                        act.wait_ge(enc_in_psum, count(cc, u))
                        nc.scalar.activation(seqs(xeT[u][0:R1, :]), packed(ps[0:R1, W[u] + 2, 0:CT]), ACT.Identity,
                                             bias=enc_b[:, 0:1]).then_inc(enc_done, 1)
                    for u in range(2):
                        act.wait_ge(s_shifted, count(cc, u))
                        nc.scalar.activation(s_exp[u][:, :, :], s_logits[u][:, :, :], ACT.Exp).then_inc(s_exp_done, 1)
                    for u in range(2):
                        act.wait_ge(onehotT_in_psum, count(cc, u))
                        nc.scalar.copy(xT[u][FG:FG + E, 1, :], ps[FG:FG + E, W[u] + 2, :]).then_inc(onehotT_done, 1)
                    for u in range(2):
                        for m in range(4):
                            act.wait_ge(s_hid_in_psum, 4 * (2 * cc + u) + m + 1)
                            nc.scalar.activation(seqs(s_hidT[u][:, m, :]), packed(ps[:, W[u] + m, 0:CT]),
                                                 ACT.Gelu).then_inc(s_hid_done, 1)

            @block.vector
            def _(dve):
                X = [0, 4]
                Y = [2, 6]
                nc.vector.memset(cls_at[:, :], 0.0).then_inc(cls_zero, 1)
                dve.wait_ge(cls_zero, 1)
                for b in range(2):
                    nc.vector.memset(cls_at[:, HALF * b:HALF * b + 1], 1.0)
                for e in range(E):
                    nc.vector.memset(expert_rank[:, e:e + 1], float(E - e))
                nc.vector.memset(ones_row[:, :], 1.0)
                for v in range(2):
                    nc.vector.memset(hidT[v][:, :, :], 0.0)
                nc.vector.memset(s_w1[FG:FG + E, 1, :], -OFF)
                for u in range(2):
                    nc.vector.memset(lam[u][:, :, :], 0.0)
                    nc.vector.memset(zT[u][:, :], 0.0)
                    nc.vector.memset(xT[u][0:FG, :, :], 0.0)
                    last = nc.vector.memset(xT[u][FG:FG + 1, :, :], 1.0)
                last.then_inc(const_done, 1)
                dve.sem_inc(relu_dve_done, 2)
                dve.sem_inc(relu_act_done, 2)
                dve.sem_inc(moe_in_psum, MOE0)
                dve.sem_inc(experts_zero, 1)
                dve.wait_ge(load, LOADED)
                nc.vector.tensor_scalar(half_e2_b[:, :], e2_b[:, :], 0.5, None, ALU.mult).then_inc(lam_coef_done, 1)
                dve.wait_ge(tanh_done, 1)
                nc.vector.tensor_scalar(lam_scale[:, :], tanh_delta[:, :], 0.25, None, ALU.mult).then_inc(lam_coef_done, 1)
                nc.vector.scalar_tensor_tensor(lam_mid[:, :], tanh_delta[:, :], 0.5, a_base[:, :], ALU.mult,
                                               ALU.add).then_inc(lam_mid_done, 1)
                dve.wait_ge(lam_mid_done, 1)
                nc.vector.tensor_scalar(lam_bias[:, :], lam_mid[:, :], 0.5, None, ALU.mult).then_inc(lam_coef_done, 1)

                def norm_stats(norm, u, src, n):
                    for i in range(TILES):
                        last = nc.vector.bn_stats(stats[u][:, i, :], src(i))
                    last.then_inc(stats_done[norm], 1)
                    dve.wait_ge(stats_done[norm], n)
                    nc.vector.tensor_copy(carrier[u][:, norm:norm + 1], stats[u][:, 0, 0:1])
                    for i in range(TILES):
                        last = nc.vector.bn_aggr(meanvar[u][:, i, :], stats[u][:, i, :])
                    last.then_inc(var_done[norm], 1)

                def norm_apply(norm, u, src, n):
                    dve.wait_ge(rstd_done[norm], n)
                    for i in range(TILES):
                        last = nc.vector.tensor_scalar(x_tok[u][:, i, :], src(i), meanvar[u][:, i, 0:1],
                                                       rstd[u][:, i:i + 1], ALU.subtract, ALU.mult)
                    last.then_inc(x_done[norm], 1)

                with dve.Fori(0, CHUNKS // 2) as cc:
                    for u in range(2):
                        dve.wait_ge(patch_done, count(cc, u))
                        norm_stats(0, u, lambda i: tokv(X[u])[:, i // 2, i % 2, :], count(cc, u))
                    for u in range(2):
                        norm_apply(0, u, lambda i: tokv(X[u])[:, i // 2, i % 2, :], count(cc, u))
                        dve.wait_ge(x_done[0], count(cc, u))
                        nc.vector.tensor_tensor(tok(h_plus_x[u]), tokv(X[u]), tok(x_tok[u]),
                                                ALU.add).then_inc(hx_done, 1)
                    for u in range(2):
                        n = 2 * cc + u + 1
                        dve.wait_ge(tanh_lam_done, n)
                        for g in range(2):
                            last = nc.vector.tensor_scalar(seqs(lam[u][:, g, :]), seqs(lam[u][:, g, :]), 0.5, 0.5,
                                                           ALU.mult, ALU.add)
                        last.then_inc(lam_done, 1)
                        dve.wait_ge(lam_done, n)
                        dve.wait_ge(bu_done, n)
                        for g in range(2):
                            last = nc.vector.tensor_tensor_scan(sT[u][:, g, :], lam[u][:, g, :], ps[0:FG, Y[u] + g, :],
                                                                0.0, ALU.mult, ALU.add)
                        last.then_inc(scan_done, 1)
                    for u in range(2):
                        n = 2 * cc + u + 1
                        dve.wait_ge(gelu_y_done, n)
                        dve.wait_ge(tanh_g_done, n)
                        nc.vector.scalar_tensor_tensor(gelu_y[u][:, :, :], tanh_g[u][:, :, :], 1.0, gelu_y[u][:, :, :],
                                                       ALU.add, ALU.mult).then_inc(gated_done, 1)
                        dve.wait_ge(gated_done, n)
                        nc.vector.scalar_tensor_tensor(h[:, bass.ds((2 * cc + u) * TILES, TILES), :],
                                                       gelu_y[u][:, :, :], 0.5, h_plus_x[u][:, :, :],
                                                       ALU.mult, ALU.add).then_inc(h_done, 1)
                    for u in range(2):
                        dve.wait_ge(h_done, count(cc, u))
                        nc.vector.tensor_copy(carrier[u][:, 4:5], gelu_y[u][:, 0, 0:1])
                        norm_stats(1, u, lambda i: tile_of(h, cc, u, i), count(cc, u))
                    for u in range(2):
                        norm_apply(1, u, lambda i: tile_of(h, cc, u, i), count(cc, u))
                    for u in range(2):
                        dve.wait_ge(xT_done[1], count(cc, u))
                        nc.vector.tensor_scalar(
                            x2T[:, bass.ds(2 * cc + u, 1), :, :].rearrange("p c g t -> p (c g t)"),
                            xT[u][0:FG, :, :].rearrange("p g t -> p (g t)"), 1.0, None, ALU.mult).then_inc(x2T_done, 1)
                        dve.wait_ge(logits_in_psum, count(cc, u))
                        nc.vector.tensor_scalar(chunk_of(logits, cc, u).rearrange("p i e -> p (i e)"),
                                                ps[:, Y[u], 0:TILES * E], 1.0, None, ALU.mult).then_inc(logits_done, 1)
                if stage == "A":
                    return

                dve.wait_ge(logits_done, CHUNKS)
                nc.vector.tensor_reduce(route_max[:, :], logits[:, :, :], AX.X, ALU.max).then_inc(route_max_done, 1)
                dve.wait_ge(route_max_done, 1)
                nc.vector.tensor_tensor(probs[:, :, :], logits[:, :, :], spread(route_max[:, :], E),
                                        ALU.subtract).then_inc(shifted_done, 1)
                dve.wait_ge(route_exp_done, 1)
                nc.vector.tensor_reduce(route_sum[:, :], probs[:, :, :], AX.X, ALU.add).then_inc(route_sum_done, 1)
                dve.wait_ge(route_sum_done, 1)
                nc.vector.reciprocal(route_sum[:, :], route_sum[:, :]).then_inc(route_inv_done, 1)
                dve.wait_ge(route_inv_done, 1)
                nc.vector.tensor_tensor(probs[:, :, :], probs[:, :, :], spread(route_sum[:, :], E),
                                        ALU.mult).then_inc(probs_done, 1)
                dve.wait_ge(probs_done, 1)

                def first_largest(src, dst, best_done, eq_done, rank_done, rankmax_done, onehot):
                    nc.vector.tensor_reduce(best[:, :], src[:, :, :], AX.X, ALU.max).then_inc(best_done, 1)
                    dve.wait_ge(best_done, 1)
                    nc.vector.tensor_tensor(rank[:, :, :], src[:, :, :], spread(best[:, :], E),
                                            ALU.is_equal).then_inc(eq_done, 1)
                    dve.wait_ge(eq_done, 1)
                    nc.vector.tensor_tensor(rank[:, :, :], rank[:, :, :], spread_rank(NT), ALU.mult).then_inc(rank_done, 1)
                    dve.wait_ge(rank_done, 1)
                    nc.vector.tensor_reduce(best[:, :], rank[:, :, :], AX.X, ALU.max).then_inc(rankmax_done, 1)
                    dve.wait_ge(rankmax_done, 1)
                    nc.vector.tensor_tensor(dst[:, :, :], rank[:, :, :], spread(best[:, :], E),
                                            ALU.is_equal).then_inc(onehot, 1)
                    dve.wait_ge(onehot, 1)

                first_largest(probs, first, best1_done, eq1_done, rank1_done, rankmax1_done, first_done)
                nc.vector.scalar_tensor_tensor(others[:, :, :], first[:, :, :], -2.0, probs[:, :, :], ALU.mult,
                                               ALU.add).then_inc(others_done, 1)
                dve.wait_ge(others_done, 1)
                first_largest(others, second, best2_done, eq2_done, rank2_done, rankmax2_done, second_done)
                nc.vector.tensor_tensor(first[:, :, :], first[:, :, :], second[:, :, :], ALU.add).then_inc(both_done, 1)
                dve.wait_ge(both_done, 1)
                nc.vector.tensor_tensor(gates[:, :, :], first[:, :, :], probs[:, :, :], ALU.mult).then_inc(gates_done, 1)
                dve.wait_ge(gates_done, 1)

                with dve.Fori(0, E // 2) as ee:
                    for v in range(2):
                        for c in range(CHUNKS):
                            dve.wait_ge(moe_in_psum, MOE0 + 8 * ee + 4 * v + c - 1)
                            for m in range(1, HC, 2):
                                dve.wait_ge(hid_in_psum, HC * (8 * ee + 4 * v + c) + m + 1)
                                nc.vector.tensor_scalar(seqs(hidT[c % 2][:, m, :]), packed(ps[:, (HC * c + m) % 4, 0:CT]),
                                                        b1[v][:, m:m + 1], 0.0, ALU.add, ALU.max).then_inc(relu_dve_done, 1)
                            dve.wait_ge(moe_in_psum, MOE0 + 8 * ee + 4 * v + c + 1)
                            for i in range(TILES):
                                t = TILES * c + i
                                last = nc.vector.scalar_tensor_tensor(
                                    h[:, t, :], ps[:, 4 + i, 0:D],
                                    gates[:, t, bass.ds(2 * ee + v, 1)], h[:, t, :], ALU.mult, ALU.add)
                            last.then_inc(moe_added, 1)
                if stage == "B":
                    return

                dve.wait_ge(moe_added, E * CHUNKS)
                for u in range(2):
                    nc.vector.memset(q[u][:, :, :], 0.0)
                    nc.vector.memset(sc[u][:, :, :], 0.0)
                    nc.vector.memset(s_hidT[u][:, :, :], 0.0)
                    nc.vector.memset(xeT[u][0:R1, :], 0.0)
                    nc.vector.memset(xeT[u][R1:R1 + 1, :], 1.0)
                    last = nc.vector.memset(vals[u][:, :, :, :, :], 0.0)
                last.then_inc(late_zero, 1)
                dve.wait_ge(late_zero, 1)
                for u in range(2):
                    nc.vector.memset(vals[u][0:HALF, :, :, 0, DH:VW], 1.0)
                    last = nc.vector.memset(vals[u][HALF:P, :, :, 1, DH:VW], 1.0)
                last.then_inc(late_const, 1)

                W = [0, 4]
                with dve.Fori(0, CHUNKS // 2) as cc:
                    for u in range(2):
                        norm_stats(2, u, lambda i: tile_of(h, cc, u, i), count(cc, u))
                    for u in range(2):
                        norm_apply(2, u, lambda i: tile_of(h, cc, u, i), count(cc, u))
                    for u in range(2):
                        for j in range(HG):
                            dve.wait_ge(k_in_psum, 3 * (2 * cc + u) + j + 1)
                            nc.vector.tensor_copy(kk[u][:, j, :, 0, :], packed(ps[:, W[u] + (3, 1, 3)[j], 0:CT])).then_inc(k_done, 1)
                        dve.wait_ge(v_in_psum, count(cc, u))
                        for bank in range(2):
                            last = nc.vector.tensor_copy(
                                vals[u][HALF:P, 4 * bank:4 * bank + 4, :, 1, 0:DH],
                                ps[HALF:P, W[u] + bank, 0:4 * FG].rearrange("p (s h d) -> p s h d", s=4, d=DH))
                        last.then_inc(v_high_done, 1)
                    for u in range(2):
                        dve.wait_ge(kk_in_psum, 3 * (2 * cc + u) + 2)
                        nc.vector.tensor_copy(kk[u][:, 1, :, 1, :], packed(ps[:, W[u] + 3, 0:CT])).then_inc(kk_dve_done, 1)
                    for i in range(TILES):
                        for u in range(2):
                            n = 8 * cc + 2 * i + u + 1
                            dst = sc[u][:, HEADS * i:HEADS * i + HEADS, 0:T]
                            dve.wait_ge(squares_done, n)
                            nc.vector.tensor_tensor(dst, squares[u][:, :, 0, :], squares[u][:, :, 1, :],
                                                    ALU.add).then_inc(sc2_done, 1)
                            dve.wait_ge(sc2_done, n)
                            nc.vector.tensor_reduce(sc_max[u][:, HEADS * i:HEADS * i + HEADS], dst, AX.X,
                                                    ALU.max).then_inc(sc2_max_done, 1)
                    for u in range(2):
                        dve.wait_ge(sqrt_done, count(cc, u))
                        dve.wait_ge(sqrt_max_done, count(cc, u))
                        nc.vector.tensor_tensor(sc[u][:, :, 0:T], sc[u][:, :, 0:T], spread(sc_max[u][:, :], T),
                                                ALU.subtract).then_inc(sc_shifted, 1)
                    for i in range(TILES + 1):
                        for u in range(2):
                            if i < TILES:
                                dve.wait_ge(pT_in_psum, 8 * cc + 2 * i + u + 1)
                                if i:
                                    dve.wait_ge(ctx_in_psum, 8 * cc + 2 * i + u - 1)
                                nc.vector.tensor_copy(probsT[u][:, 3:6, :], ps[:, W[u] + 1, 0:3 * P]).then_inc(pT_dve_done, 1)
                            if i >= 1:
                                n = 8 * cc + 2 * (i - 1) + u + 1
                                got = ps[:, W[u] + 2 + i % 2, 0:HEADS * VW].rearrange("p (r j d) -> p r j d", r=4, d=VW)
                                dve.wait_ge(ctx_in_psum, n)
                                nc.vector.reciprocal(inv_sum[u][:, :].rearrange("p (r j) -> p r j", r=4),
                                                     got[:, :, :, DH]).then_inc(inv_sum_done, 1)
                                dve.wait_ge(inv_sum_done, n)
                                nc.vector.tensor_tensor(
                                    ctx_tok[u][:, i - 1, :].rearrange("p (j r d) -> p r j d", j=HG, r=4),
                                    got[:, :, :, 0:DH],
                                    spread(inv_sum[u][:, :].rearrange("p (r j) -> p r j", r=4), DH),
                                    ALU.mult).then_inc(ctx_scaled, 1)
                    for u in range(2):
                        dve.wait_ge(ctx_scaled, 8 * cc + 7 + u)
                        nc.vector.tensor_tensor(chunk_of(h, cc, u), chunk_of(h, cc, u), ctx_tok[u][:, :, :],
                                                ALU.add).then_inc(attended, 1)
                    if stage == "C":
                        return
                    for u in range(2):
                        dve.wait_ge(attended, count(cc, u))
                        nc.vector.tensor_copy(carrier[u][:, 5:6], ctx_tok[u][:, 0, 0:1])
                        norm_stats(3, u, lambda i: tile_of(h, cc, u, i), count(cc, u))
                    for u in range(2):
                        norm_apply(3, u, lambda i: tile_of(h, cc, u, i), count(cc, u))
                    for u in range(2):
                        n = count(cc, u)
                        got = ps[:, W[u] + 3, 0:TILES * E].rearrange("p (i e) -> p i e", e=E)
                        dve.wait_ge(s_logits_in_psum, n)
                        nc.vector.tensor_reduce(s_max[u][:, :], got, AX.X, ALU.max).then_inc(s_max_done, 1)
                        dve.wait_ge(s_max_done, n)
                        nc.vector.tensor_tensor(s_logits[u][:, :, :], got, spread(s_max[u][:, :], E),
                                                ALU.subtract).then_inc(s_shifted, 1)
                    for u in range(2):
                        n = count(cc, u)
                        dve.wait_ge(s_exp_done, n)
                        nc.vector.scalar_tensor_tensor(s_rank[u][:, :, :], s_exp[u][:, :, :], 1.0, spread_rank(TILES),
                                                       ALU.is_equal, ALU.mult).then_inc(s_rank_done, 1)
                        nc.vector.tensor_reduce(s_sum[u][:, :], s_exp[u][:, :, :], AX.X, ALU.add).then_inc(s_sum_done, 1)
                        dve.wait_ge(s_rank_done, n)
                        nc.vector.tensor_reduce(s_best[u][:, :], s_rank[u][:, :, :], AX.X, ALU.max).then_inc(s_best_done, 1)
                        dve.wait_ge(s_best_done, n)
                        nc.vector.tensor_tensor(s_onehot[u][:, :, :], s_rank[u][:, :, :], spread(s_best[u][:, :], E),
                                                ALU.is_equal).then_inc(onehot_done, 1)
                        dve.wait_ge(s_sum_done, n)
                        nc.vector.reciprocal(s_prob[u][:, :], s_sum[u][:, :]).then_inc(s_prob_done, 1)
                    for u in range(2):
                        n = count(cc, u)
                        dve.wait_ge(s_out_in_psum, n)
                        dve.wait_ge(s_prob_done, n)
                        dve.wait_ge(out_done, 64 * cc)
                        for i in range(TILES):
                            last = nc.vector.scalar_tensor_tensor(
                                out_tok[u][:, i, :], tokv(W[u])[:, i // 2, i % 2, :], s_prob[u][:, i:i + 1],
                                tile_of(h, cc, u, i), ALU.mult, ALU.add)
                        last.then_inc(out_ready, 1)


def _layout(x, cls_tok, L0_tok_W, L0_attn_V_w, L0_attn_U_w, L0_attn_E1_w, L0_attn_E1_b, L0_attn_E2_w, L0_attn_E2_b,
            L0_attn_a_base, L0_attn_a_delta, L0_attn_C_w, L0_attn_G_w, L0_attn_G_b, L0_ffn_Wg, L0_ffn_W1, L0_ffn_b1,
            L0_ffn_W2, L0_ffn_b2, L1_attn_Wqr, L1_attn_Wqi, L1_attn_Wkr, L1_attn_Wki, L1_attn_Wv, L1_ffn_enc_w,
            L1_ffn_enc_b, L1_ffn_sw_w, L1_ffn_sw_b, L1_ffn_w1, L1_ffn_b1, L1_ffn_w2, L1_ffn_b2):
    import numpy as np
    np_ = {}

    def groups(w, bias=None):
        a = np.reshape(np.asarray(w), (2, FG, -1)).transpose(1, 0, 2)
        if bias is None:
            return np.ascontiguousarray(a)
        row = np.zeros((1, 2, a.shape[2]), a.dtype)
        row[0, 1] = np.asarray(bias)
        return np.concatenate([a, row], 0)

    p = np.asarray(x).reshape(B, 3, 7, 16, 7, 16).transpose(3, 5, 1, 0, 2, 4).reshape(HID, B, T - 1)
    full = np.zeros((HID, B, HALF), p.dtype)
    full[:, :, 1:T] = p
    np_["patches"] = np.ascontiguousarray(
        full.reshape(KC, P, CHUNKS, CW).transpose(2, 1, 0, 3))
    np_["w_tok"] = np.ascontiguousarray(np.asarray(L0_tok_W).T.reshape(KC, P, D).transpose(1, 0, 2))
    np_["cls"] = np.asarray(cls_tok).reshape(1, D)
    np_["V"] = groups(np.asarray(L0_attn_V_w).T)
    np_["U"] = np.ascontiguousarray(np.asarray(L0_attn_U_w).T)
    np_["E1"] = groups(np.asarray(L0_attn_E1_w).T, L0_attn_E1_b)
    np_["E2"] = np.ascontiguousarray(np.repeat(np.asarray(L0_attn_E2_w), D // 3, axis=0).T)
    np_["E2b"] = np.ascontiguousarray(np.repeat(np.asarray(L0_attn_E2_b), D // 3).reshape(2, FG).T)
    np_["a_base"] = np.ascontiguousarray(np.asarray(L0_attn_a_base).reshape(2, FG).T)
    np_["a_delta"] = np.ascontiguousarray(np.asarray(L0_attn_a_delta).reshape(2, FG).T)
    np_["C"] = groups(np.asarray(L0_attn_C_w).T)
    np_["G"] = groups(np.asarray(L0_attn_G_w).T, L0_attn_G_b)
    np_["Wg"] = groups(L0_ffn_Wg)
    np_["W1"] = np.asarray(L0_ffn_W1).reshape(E, 2, FG, HID).transpose(0, 2, 1, 3)
    np_["W2"] = np.asarray(L0_ffn_W2).reshape(E, HC, P, D).transpose(0, 2, 1, 3)
    np_["b1"] = np.asarray(L0_ffn_b1).reshape(E, HC, P).transpose(0, 2, 1)
    np_["b2"] = np.asarray(L0_ffn_b2).reshape(E, 1, D)

    def complex_heads(re, im):
        both = np.stack([np.asarray(re).reshape(HEADS, DH, D), np.asarray(im).reshape(HEADS, DH, D)], 1)
        return groups(both.reshape(HEADS * 2 * DH, D).T)

    np_["Wq"] = complex_heads(L1_attn_Wqr, L1_attn_Wqi)
    np_["Wk"] = complex_heads(L1_attn_Wkr, L1_attn_Wki)
    order = [(n % HG) * 4 + n // HG for n in range(HEADS)]
    wv = np.asarray(L1_attn_Wv).reshape(HEADS, DH, D)[order[0::2] + order[1::2]]
    np_["Wv"] = groups(wv.reshape(D, D).T)
    np_["enc_w"] = groups(L1_ffn_enc_w)
    np_["enc_b"] = np.asarray(L1_ffn_enc_b).reshape(R1, 1)
    np_["sw"] = np.concatenate([np.asarray(L1_ffn_sw_w), np.asarray(L1_ffn_sw_b)[None]], 0)
    np_["s_w1"] = groups(np.asarray(L1_ffn_w1).transpose(1, 0, 2).reshape(D, E * R1))
    np_["s_b1"] = np.asarray(L1_ffn_b1)
    np_["s_w2"] = np.asarray(L1_ffn_w2).reshape(4, P, D).transpose(1, 0, 2)
    np_["s_b2"] = np.asarray(L1_ffn_b2)
    return np_


def kernel(**inputs):
    import numpy as _np
    import concourse.bacc as _bacc
    from concourse import mybir as _mybir
    from concourse.bass_utils import run_bass_kernel_spmd as _run

    nc = _bacc.Bacc("TRN2", target_bir_lowering=False, num_devices=1)
    laid = _layout(**inputs)
    arrays, A = {}, {}
    for name, a in laid.items():
        arrays[f"in_{name}"] = _np.ascontiguousarray(a)
        A[name] = nc.dram_tensor(f"in_{name}", a.shape, _mybir.dt.from_np(a.dtype), kind="ExternalInput").ap()
    out = nc.dram_tensor("out_0", (B * T, D), _mybir.dt.from_np(_np.dtype("float32")), kind="ExternalOutput").ap()
    build(nc, A, out)
    r = _run(nc, [arrays], core_ids=[0])
    return r.results[0]["out_0"].reshape(B, T, D)
```

```python
from contextlib import ExitStack

import concourse.bass as bass
from concourse import mybir

ALU = mybir.AluOpType
ACT = mybir.ActivationFunctionType
AX = mybir.AxisListType
F32 = mybir.dt.float32
I32 = mybir.dt.int32

P = 128
B, T, D = 32, 50, 192
FG = 96
HALF = 64
CB = 8
CT = CB * T
CW = CB * HALF
TILES = CB // 2
CHUNKS = B // CB
NT = B // 2
KC = 6
E = 8
HID = 768
HC = HID // P
R1 = 64
HEADS, DH = 12, 16
HG = 3
EPS = 1e-5
HW = 2 * T
VW = DH + 1
SCALE2 = 1.0 / DH
SLOTS = 14 * P
MOE_TILES = 2 * B * T // P + E - 1
NULL_ROW = E * SLOTS
ROWS = NULL_ROW + P
SKIP = float(1 << 20)
SBUF_START = 16512
OFF = 1e18


def build(nc, A, out):
    with ExitStack() as ctx:
        here = [SBUF_START]

        def sb(name, shape, dt=F32):
            size = 4
            for n in shape[1:]:
                size *= n
            t = nc.alloc_sbuf_tensor_at(name, shape, dt, offset=here[0])
            here[0] += -(-size // 32) * 32
            return t

        def sem(name):
            return ctx.enter_context(nc.semaphore(name))

        def seqs(ap):
            return ap.rearrange("p (s t) -> p s t", t=HALF)[:, :, 0:T]

        def packed(ap):
            return ap.rearrange("p (s t) -> p s t", t=T)

        ps = ctx.enter_context(nc.psum_tensor("ps", [P, 8, 512], F32))

        w_tok = sb("w_tok", [P, KC, D])
        cls_row = sb("cls_row", [1, D])
        cls_at = sb("cls_at", [1, P])
        v_w = sb("v_w", [FG, 2, 16])
        u_w = sb("u_w", [16, D])
        e1_w = sb("e1_w", [FG + 1, 2, 64])
        e2_w = sb("e2_w", [64, D])
        e2_b = sb("e2_b", [FG, 2])
        a_base = sb("a_base", [FG, 2])
        a_delta = sb("a_delta", [FG, 2])
        tanh_delta = sb("tanh_delta", [FG, 2])
        half_e2_b = sb("half_e2_b", [FG, 2])
        lam_scale = sb("lam_scale", [FG, 2])
        lam_bias = sb("lam_bias", [FG, 2])
        lam_mid = sb("lam_mid", [FG, 2])
        c_w = sb("c_w", [FG, 2, D])
        g_w = sb("g_w", [FG + 1, 2, D])
        gate_w = sb("gate_w", [FG, 2, E])
        ident = sb("ident", [P, P])
        neg_half = sb("neg_half", [P, TILES])
        eps = sb("eps", [P, TILES])

        to_kk = sb("to_kk", [P, P])

        def two(name, shape, dt=F32):
            return [sb(f"{name}{u}", shape, dt) for u in range(2)]

        stats = two("stats", [P, TILES, 6])
        meanvar = two("meanvar", [P, TILES, 2])
        rstd = two("rstd", [P, TILES])
        carrier = two("carrier", [P, 9])
        pool_carrier = two("pool_carrier", [P, 3])
        x_tok = two("x_tok", [P, TILES, D])
        xT = two("xT", [FG + E, 2, CW])
        h = sb("h", [P, NT, D])
        ramp = sb("ramp", [P, MOE_TILES + 2])
        ramp_int = sb("ramp_int", [P, MOE_TILES + 2], I32)
        expert_rank = sb("expert_rank", [P, E])
        later = sb("later", [P, P])
        ones_sq = sb("ones_sq", [P, P])
        row_index_int = sb("row_index_int", [P, 1], I32)
        row_index = sb("row_index", [P, 1])
        in_first = sb("in_first", [P, 1])
        in_second = sb("in_second", [P, 1])
        valid = sb("valid", [P, 1])
        skip = sb("skip", [P, 1])
        region = sb("region", [P, E])
        next_row = sb("next_row", [P, E])
        r_max = two("r_max", [P, TILES])
        r_exp = two("r_exp", [P, TILES, E])
        r_sum = two("r_sum", [P, TILES])
        probs = two("probs", [P, TILES, E])
        best = two("best", [P, TILES])
        rank = two("rank", [P, TILES, E])
        others = two("others", [P, TILES, E])
        chosen = two("chosen", [P, TILES, E])
        before = two("before", [P, TILES + 1, E])
        row_of = two("row_of", [P, TILES, E])
        row_sum = two("row_sum", [P, 2, TILES])
        rows = two("rows", [P, 2, TILES], I32)
        all_first = sb("all_first", [P, NT, E])
        all_second = sb("all_second", [P, NT, E])
        all_rows = sb("all_rows", [P, 2, NT])
        row_move = sb("row_move", [P, 2, NT])
        moved = sb("moved", [P, E])
        y_rows = sb("y_rows", [P, 2, NT], I32)
        all_gates = sb("all_gates", [P, NT, 2])
        rows_now = two("rows_now", [P, 2, TILES], I32)
        counts = sb("counts", [P, E])
        steps128 = sb("steps128", [P, 13])
        n_tiles = sb("n_tiles", [P, E])
        ones_e = sb("ones_e", [P, E])
        tiles_to = sb("tiles_to", [P, E])
        tile_expert = sb("tile_expert", [P, MOE_TILES + 2])
        tiles_behind = sb("tiles_behind", [P, MOE_TILES + 2])
        live = sb("live", [P, MOE_TILES + 2])
        tile_row = sb("tile_row", [P, MOE_TILES + 2])
        load_row = sb("load_row", [P, MOE_TILES + 2])
        tile_expert_int = sb("tile_expert_int", [P, MOE_TILES + 2], I32)
        load_row_int = sb("load_row_int", [P, MOE_TILES + 2], I32)
        next_row_int = sb("next_row_int", [P, E], I32)
        zeros = sb("zeros", [P, D])
        shared = here[0]

        patches = two("patches", [P, KC, CW])
        h_plus_x = two("h_plus_x", [P, TILES, D])
        x2_tok = two("x2_tok", [P, TILES, D])
        zT = two("zT", [16, CW])
        gelu_e = two("gelu_e", [64, CT])
        lam = two("lam", [FG, 2, CW])
        sT = two("sT", [FG, 2, CW])
        gelu_at = here[0]
        gelu_y = two("gelu_y", [P, TILES, D])
        tanh_g = two("tanh_g", [P, TILES, D])
        experts_at = here[0]

        w1 = sb("w1", [FG + 1, E, 2, HID])
        w2 = sb("w2", [P, E, HC * D])
        b2 = sb("b2", [P, E, D])

        here[0] = gelu_at
        over = sb("over", [P, E, 13])
        behind = sb("behind", [P, MOE_TILES + 2, E - 1])
        here[0] = shared
        wq = sb("wq", [FG, 2, HG * P])
        wk = sb("wk", [FG, 2, HG * P])
        wv = sb("wv", [FG, 2, D])
        enc_w = sb("enc_w", [FG, 2, R1])
        enc_b = sb("enc_b", [R1, 1])
        sw_w = sb("sw_w", [R1 + 1, E])
        s_w1 = sb("s_w1", [FG + E, 2, E * R1])
        s_w2 = sb("s_w2", [P, 4, D])
        s_b2 = sb("s_b2", [FG + E, D])
        assert here[0] <= shared + 2 * 4 * KC * CW
        xs = two("xs", [P, D])
        xsT = two("xsT", [FG + 1, 2, P])
        hid = two("hid", [P, HID])
        hidT = two("hidT", [P, HC, P])
        ys = two("ys", [P, D])
        tiles_end = here[0]
        q = two("q", [P, HG, CW])
        vals = two("vals", [P, CB, HEADS // 2, 2, VW])
        xeT = two("xeT", [R1 + 1, CW])
        assert here[0] <= experts_at

        sc = two("sc", [P, TILES * HEADS, HALF])
        kk = two("kk", [P, HG, CB, 2, T])
        y_first = two("y_first", [P, TILES, D])
        y_second = two("y_second", [P, TILES, D])
        squares = two("squares", [P, HEADS, 2, T])
        sc_max = two("sc_max", [P, TILES * HEADS])
        probsT = two("probsT", [P, HEADS // 2, P])
        inv_sum = two("inv_sum", [P, HEADS])
        ctx_tok = two("ctx_tok", [P, TILES, D])
        s_logits = two("s_logits", [P, TILES, E])
        s_max = two("s_max", [P, TILES])
        s_exp = two("s_exp", [P, TILES, E])
        s_sum = two("s_sum", [P, TILES])
        s_prob = two("s_prob", [P, TILES])
        s_rank = two("s_rank", [P, TILES, E])
        s_best = two("s_best", [P, TILES])
        s_onehot = two("s_onehot", [P, TILES, E])
        s_hidT = two("s_hidT", [P, 4, CW])
        out_tok = two("out_tok", [P, TILES, D])

        xs_dram = nc.dram_tensor("xs_dram", (ROWS, D), F32, kind="Internal").ap()
        ys_dram = nc.dram_tensor("ys_dram", (MOE_TILES * P, D), F32, kind="Internal").ap()

        load = sem("load")
        ident_zero = sem("ident_zero")
        ident_done = sem("ident_done")
        cls_zero = sem("cls_zero")
        const_done = sem("const_done")
        patches_in = [sem("patches_in0"), sem("patches_in1")]
        patch_done = sem("patch_done")
        stats_done, var_done, eps_added, rstd_done, x_done, xT_in_psum, xT_done = (
            [sem(f"{name}{n}") for n in range(4)]
            for name in ("stats_done", "var_done", "eps_added", "rstd_done", "x_done", "xT_in_psum", "xT_done"))
        r_shifted = sem("r_shifted")
        r_exp_done = sem("r_exp_done")
        route_step = sem("route_step")
        chosen_done = sem("chosen_done")
        ranks_in_psum = sem("ranks_in_psum")
        rows_done = sem("rows_done")
        off_done = sem("off_done")
        ramp_copied = sem("ramp_copied")
        row_step = sem("row_step")
        xsT_ones = sem("xsT_ones")
        y_init = sem("y_init")
        scattered = [sem("scattered0"), sem("scattered1")]
        x2_moved = sem("x2_moved")
        null_zero = sem("null_zero")
        tails_zero = sem("tails_zero")
        table_step = sem("table_step")
        table_done = sem("table_done")
        ramp_done = sem("ramp_done")
        later_done = sem("later_done")
        ones_done = sem("ones_done")
        w_in = sem("w_in")
        late_in = sem("late_in")
        xs_in = sem("xs_in")
        xsT_in_psum = sem("xsT_in_psum")
        xsT_done = sem("xsT_done")
        hid_in_psum = sem("hid_in_psum")
        hid_act_done = sem("hid_act_done")
        hid_dve_done = sem("hid_dve_done")
        hidT_in_psum = sem("hidT_in_psum")
        hidT_act_done = sem("hidT_act_done")
        hidT_dve_done = sem("hidT_dve_done")
        ys_in_psum = sem("ys_in_psum")
        ys_done = sem("ys_done")
        ys_stored = sem("ys_stored")
        vals_zero = sem("vals_zero")
        gathered = [sem("gathered0"), sem("gathered1")]
        rows_now_done = sem("rows_now_done")
        first_added = sem("first_added")
        moe_added = sem("moe_added")
        route_bias = sem("route_bias")
        logits_in_psum = sem("logits_in_psum")
        late_const = sem("late_const")
        kk_map_zero = sem("kk_map_zero")
        kk_map_half = sem("kk_map_half")
        kk_map_done = sem("kk_map_done")
        q_in_psum = sem("q_in_psum")
        q_done = sem("q_done")
        k_in_psum = sem("k_in_psum")
        k_done = sem("k_done")
        v_in_psum = sem("v_in_psum")
        v_low_done = sem("v_low_done")
        v_high_done = sem("v_high_done")
        kk_in_psum = sem("kk_in_psum")
        kk_act_done = sem("kk_act_done")
        kk_dve_done = sem("kk_dve_done")
        scores_in_psum = sem("scores_in_psum")
        squares_done = sem("squares_done")
        sc2_done = sem("sc2_done")
        sc2_max_done = sem("sc2_max_done")
        sqrt_done = sem("sqrt_done")
        sqrt_max_done = sem("sqrt_max_done")
        sc_shifted = sem("sc_shifted")
        exp_done = sem("exp_done")
        pT_in_psum = sem("pT_in_psum")
        pT_act_done = sem("pT_act_done")
        pT_dve_done = sem("pT_dve_done")
        ctx_in_psum = sem("ctx_in_psum")
        inv_sum_done = sem("inv_sum_done")
        ctx_scaled = sem("ctx_scaled")
        attended = sem("attended")
        enc_in_psum = sem("enc_in_psum")
        enc_done = sem("enc_done")
        s_logits_in_psum = sem("s_logits_in_psum")
        s_logits_done = sem("s_logits_done")
        s_max_done = sem("s_max_done")
        s_shifted = sem("s_shifted")
        s_exp_done = sem("s_exp_done")
        s_sum_done = sem("s_sum_done")
        s_prob_done = sem("s_prob_done")
        s_eq_done = sem("s_eq_done")
        s_rank_done = sem("s_rank_done")
        s_best_done = sem("s_best_done")
        onehot_done = sem("onehot_done")
        onehotT_in_psum = sem("onehotT_in_psum")
        onehotT_done = sem("onehotT_done")
        s_hid_in_psum = sem("s_hid_in_psum")
        s_hid_done = sem("s_hid_done")
        s_out_in_psum = sem("s_out_in_psum")
        out_ready = sem("out_ready")
        hx_done = sem("hx_done")
        ze_done = sem("ze_done")
        zT_done = sem("zT_done")
        gelu_e_done = sem("gelu_e_done")
        bu_done = sem("bu_done")
        tanh_alpha_done = sem("tanh_alpha_done")
        tanh_lam_done = sem("tanh_lam_done")
        lam_done = sem("lam_done")
        lam_mid_done = sem("lam_mid_done")
        lam_coef_done = sem("lam_coef_done")
        scan_done = sem("scan_done")
        yg_done = sem("yg_done")
        gelu_y_done = sem("gelu_y_done")
        tanh_g_done = sem("tanh_g_done")
        gated_done = sem("gated_done")
        h_done = sem("h_done")
        tanh_done = sem("tanh_done")
        out_done = sem("out_done")

        MOVED0, STORED0, OUT0, YS0, HIDT0, YSP0 = 2, 16, 16, 2, 2, 2

        MOVES = 2 * TILES * 16
        ROUTE_STEPS, ROW_STEPS = 21, 5

        def repeat(ap, n):
            return bass.AP(ap.tensor, ap.offset, [list(ap.ap[0]), [0, n], *map(list, ap.ap[1:])])

        def count(cc, u):
            return 2 * cc + u + 1

        def chunk_of(buf, cc, u):
            return buf[:, bass.ds((2 * cc + u) * TILES, TILES), :]

        def tile_of(buf, cc, u, i):
            return buf[:, bass.ds((2 * cc + u) * TILES + i, 1), :].rearrange("p i d -> p (i d)")

        def spread(ap, n):
            return bass.AP(ap.tensor, ap.offset, [*map(list, ap.ap), [0, n]])

        loads = [
            (w_tok[:, :, :], A["w_tok"]), (cls_row[:, :], A["cls"]),
            (v_w[:, :, :], A["V"]), (u_w[:, :], A["U"]),
            (e1_w[:, :, :], A["E1"]), (e2_w[:, :], A["E2"]), (e2_b[:, :], A["E2b"]),
            (a_base[:, :], A["a_base"]), (a_delta[:, :], A["a_delta"]),
            (c_w[:, :, :], A["C"]), (g_w[:, :, :], A["G"]), (gate_w[:, :, :], A["Wg"]),
        ]
        late_loads = [
            (wq[:, :, :], A["Wq"]), (wk[:, :, :], A["Wk"]), (wv[:, :, :], A["Wv"]),
            (enc_w[:, :, :], A["enc_w"]), (enc_b[:, :], A["enc_b"]), (sw_w[:, :], A["sw"]),
            (s_w1[0:FG, :, :], A["s_w1"]), (s_w2[:, :, :], A["s_w2"]), (s_b2[FG:FG + E, :], A["s_b2"]),
        ]
        LOADED = 16 * len(loads)
        LATE = 16 * (len(late_loads) + E)

        def tokv(slot, width=D):
            return ps[:, slot:slot + 2, 0:2 * width].rearrange("p b (i d) -> p b i d", i=2)

        def tok(buf):
            return buf[:, :, :].rearrange("p (b i) d -> p b i d", b=2)

        with nc.Block() as block:

            @block.sync
            def _(sp):
                def load_patches(c):
                    sp.dma_start(patches[c % 2][:, :, :], A["patches"][c]).then_inc(patches_in[c % 2], 16)

                def load_expert(e):
                    sp.dma_start(w1[:, e, :, :], A["W1"][e]).then_inc(w_in, 16)
                    sp.dma_start(w2[:, e, :], A["W2"][e]).then_inc(w_in, 16)
                    sp.dma_start(b2[:, e, :], A["b2"][e].to_broadcast([P, D])).then_inc(w_in, 16)

                load_patches(0)
                for dst, src in loads:
                    sp.dma_start(dst, src).then_inc(load, 16)
                load_patches(1)
                for e in range(E // 2):
                    load_expert(e)
                for c in range(2, CHUNKS):
                    sp.wait_ge(patch_done, c - 1)
                    load_patches(c)
                for e in range(E // 2, E):
                    load_expert(e)
                sp.wait_ge(const_done, 1)
                sp.dma_start(xs_dram[NULL_ROW:NULL_ROW + P, :], zeros[:, :]).then_inc(null_zero, 16)

                sp.wait_ge(patch_done, CHUNKS)
                for dst, src in late_loads:
                    sp.dma_start(dst, src).then_inc(late_in, 16)
                sp.wait_ge(off_done, 1)
                for e in range(E):
                    sp.dma_start(s_w1[FG + e:FG + e + 1, 1, R1 * e:R1 * e + R1], A["s_b1"][e:e + 1, :]).then_inc(late_in, 16)

                sp.wait_ge(table_done, 1)
                sp.wait_ge(x2_moved, MOVED0 + CHUNKS)
                for e in range(E):
                    row = sp.value_load(next_row_int[0:1, e:e + 1], min_val=0, max_val=NULL_ROW - P)
                    sp.dma_start(xs_dram[bass.ds(row, P), :], zeros[:, :]).then_inc(tails_zero, 16)
                sp.wait_ge(tails_zero, 16 * E)
                sp.wait_ge(null_zero, 16)
                sp.wait_ge(late_in, LATE)
                for v in range(2):
                    row = sp.value_load(load_row_int[0:1, v:v + 1], min_val=0, max_val=ROWS - P)
                    sp.dma_start(xs[v][:, :], xs_dram[bass.ds(row, P), :]).then_inc(xs_in, 16)
                with sp.Fori(0, MOE_TILES // 2) as tt:
                    for v in range(2):
                        sp.wait_ge(xsT_in_psum, 2 * tt + v + 1)
                        row = sp.value_load(load_row_int[0:1, bass.ds(2 * tt + 2 + v, 1)], min_val=0, max_val=ROWS - P)
                        sp.dma_start(xs[v][:, :], xs_dram[bass.ds(row, P), :]).then_inc(xs_in, 16)
                    for v in range(2):
                        sp.wait_ge(ys_done, YS0 + 2 * tt + v + 1)
                        sp.dma_start(ys_dram[bass.ds((2 * tt + v) * P, P), :], ys[v][:, :]).then_inc(ys_stored, 16)
                sp.wait_ge(ys_stored, STORED0 + 16 * MOE_TILES)
                sp.wait_ge(xs_in, 16 * (MOE_TILES + 2))
                for c in range(CHUNKS):
                    sp.wait_ge(out_ready, c + 1)
                    for half in range(2):
                        sp.dma_start(
                            out[CT * c:CT * c + CT, :].rearrange("(i two t) d -> two t i d", two=2, t=T)[half],
                            out_tok[c % 2][HALF * half:HALF * half + T, :, :]).then_inc(out_done, 16)
                sp.wait_ge(out_done, OUT0 + 32 * CHUNKS)

            @block.gpsimd
            def _(pool):
                nc.gpsimd.memset(neg_half[:, :], -0.5)
                nc.gpsimd.memset(eps[:, :], EPS)
                nc.gpsimd.memset(ident[:, :], 0.0).then_inc(ident_zero, 1)
                pool.wait_ge(ident_zero, 1)
                nc.gpsimd.affine_select(out=ident[:, :], in_=ident[:, :], compare_op=ALU.not_equal, fill=1.0,
                                        base=0, pattern=[[-1, P]], channel_multiplier=1).then_inc(ident_done, 1)

                nc.gpsimd.iota(ramp_int[:, :], [[1, MOE_TILES + 2]], base=0, channel_multiplier=0).then_inc(ramp_done, 1)
                nc.gpsimd.iota(row_index_int[:, :], [[1, 1]], base=0, channel_multiplier=1).then_inc(ramp_done, 1)
                nc.gpsimd.memset(ones_sq[:, :], 1.0).then_inc(ones_done, 1)
                pool.wait_ge(ones_done, 1)
                nc.gpsimd.affine_select(out=later[:, :], in_=ones_sq[:, :], compare_op=ALU.is_gt, fill=0.0,
                                        base=0, pattern=[[1, P]], channel_multiplier=-1).then_inc(later_done, 1)
                halves = to_kk[:, :].rearrange("p (h two d) -> p h two d", h=4, two=2)
                nc.gpsimd.memset(to_kk[:, :], 0.0).then_inc(kk_map_zero, 1)
                pool.wait_ge(kk_map_zero, 1)
                nc.gpsimd.affine_select(out=halves[:, :, 0, :], in_=halves[:, :, 0, :], compare_op=ALU.not_equal,
                                        fill=-1.0, base=-DH, pattern=[[-2 * DH, 4], [-1, DH]],
                                        channel_multiplier=1).then_inc(kk_map_half, 1)
                pool.wait_ge(kk_map_half, 1)
                nc.gpsimd.affine_select(out=halves[:, :, 1, :], in_=halves[:, :, 1, :], compare_op=ALU.not_equal,
                                        fill=1.0, base=0, pattern=[[-2 * DH, 4], [-1, DH]],
                                        channel_multiplier=1).then_inc(kk_map_done, 1)

                def inverse_deviation(norm, u, n):
                    pool.wait_ge(var_done[norm], n)
                    nc.gpsimd.tensor_tensor(rstd[u][:, :], meanvar[u][:, :, 1], eps[:, :],
                                            ALU.add).then_inc(eps_added[norm], 1)
                    pool.wait_ge(eps_added[norm], n)
                    nc.gpsimd.tensor_tensor(rstd[u][:, :], rstd[u][:, :], neg_half[:, :],
                                            ALU.pow).then_inc(rstd_done[norm], 1)

                with pool.Fori(0, CHUNKS // 2) as cc:
                    for norm in (0, 1):
                        for u in range(2):
                            inverse_deviation(norm, u, count(cc, u))
                    for u in range(2):
                        pool.wait_ge(rows_done, count(cc, u))
                        nc.gpsimd.tensor_tensor(pool_carrier[u][:, 0:1], eps[:, 0:1], eps[:, 0:1], ALU.add)
                        for i in range(TILES):
                            for k in range(2):
                                nc.gpsimd.indirect_dma_start(
                                    out=xs_dram[:, :], out_offset=bass.IndirectOffsetOnAxis(ap=rows[u][:, k, i:i + 1], axis=0),
                                    in_=x2_tok[u][:, i, :], in_offset=None, bounds_check=ROWS - 1,
                                    oob_is_err=False).then_inc(scattered[u], 16)
                    for u in range(2):
                        pool.wait_ge(scattered[u], MOVES * cc + MOVES)
                        nc.gpsimd.tensor_tensor(pool_carrier[u][:, 2:3], eps[:, 0:1], eps[:, 0:1],
                                                ALU.add).then_inc(x2_moved, 1)
                pool.wait_ge(x2_moved, MOVED0 + CHUNKS)
                pool.wait_ge(table_done, 1)
                for u in range(2):
                    nc.gpsimd.memset(q[u][:, :, :], 0.0)
                    last = nc.gpsimd.memset(vals[u][:, :, :, :, :], 0.0)
                last.then_inc(vals_zero, 1)

                pool.wait_ge(ys_stored, STORED0 + 16 * MOE_TILES)
                pool.wait_ge(y_init, 1)
                with pool.Fori(0, CHUNKS // 2) as cc:
                    for u in range(2):
                        pool.wait_ge(rows_now_done, count(cc, u))
                        nc.gpsimd.tensor_tensor(pool_carrier[u][:, 1:2], eps[:, 0:1], eps[:, 0:1], ALU.add)
                        for k, dst in enumerate((y_first, y_second)):
                            for i in range(TILES):
                                nc.gpsimd.indirect_dma_start(
                                    out=dst[u][:, i, :], out_offset=None, in_=ys_dram[:, :],
                                    in_offset=bass.IndirectOffsetOnAxis(ap=rows_now[u][:, k, i:i + 1], axis=0),
                                    bounds_check=MOE_TILES * P - 1, oob_is_err=False).then_inc(gathered[u], 16)
                    for norm in (2, 3):
                        for u in range(2):
                            inverse_deviation(norm, u, count(cc, u))

            @block.tensor
            def _(pe):
                pe.wait_ge(const_done, 1)
                pe.wait_ge(ident_done, 1)

                def turn(norm, u, banks, n):
                    pe.wait_ge(x_done[norm], n)
                    for i in range(TILES):
                        for g in range(2):
                            mm = pe.transpose(ps[0:FG, banks + g, P * i:P * i + P],
                                              (x2_tok if norm == 1 else x_tok)[u][:, i, FG * g:FG * g + FG],
                                              ident[:, :])
                    mm.then_inc(xT_in_psum[norm], 1)
                pe.wait_ge(load, LOADED)
                with pe.Fori(0, CHUNKS // 2) as cc:
                    X = [0, 4]
                    Y = [2, 6]
                    for u in range(2):
                        pe.wait_ge(patches_in[u], 16 * cc + 16)
                        for i in range(TILES):
                            dst = tokv(X[u])[:, i // 2, i % 2, :]
                            for k in range(KC):
                                pe.matmul(dst, patches[u][:, k, P * i:P * i + P],
                                          w_tok[:, k, :], start=(k == 0), stop=False)
                            mm = pe.matmul(dst, cls_at[:, :], cls_row[:, :], start=False, stop=True)
                        mm.then_inc(patch_done, 1)
                    for u in range(2):
                        turn(0, u, Y[u], count(cc, u))
                    for u in range(2):
                        pe.wait_ge(hx_done, 2 * cc + u + 1)
                        pe.wait_ge(xT_done[0], 2 * cc + u + 1)
                        for g in range(2):
                            pe.matmul(ps[0:16, X[u], 0:CT], v_w[:, g, :], seqs(xT[u][0:FG, g, :]),
                                      start=(g == 0), stop=(g == 1))
                        for g in range(2):
                            k = FG + g
                            mm = pe.matmul(ps[0:64, X[u] + 1, 0:CT], e1_w[0:k, g, :], seqs(xT[u][0:k, g, :]),
                                           start=(g == 0), stop=(g == 1))
                        mm.then_inc(ze_done, 1)
                    for u in range(2):
                        pe.wait_ge(zT_done, 2 * cc + u + 1)
                        for g in range(2):
                            pe.matmul(ps[0:FG, Y[u] + g, :], u_w[:, FG * g:FG * g + FG], zT[u][:, :],
                                      start=True, stop=True)
                        pe.wait_ge(gelu_e_done, 2 * cc + u + 1)
                        for g in range(2):
                            mm = pe.matmul(ps[0:FG, X[u] + g, 0:CT], e2_w[:, FG * g:FG * g + FG], gelu_e[u][:, :],
                                           start=True, stop=True)
                        mm.then_inc(bu_done, 1)
                    for u in range(2):
                        pe.wait_ge(scan_done, 2 * cc + u + 1)
                        pe.wait_ge(tanh_alpha_done, 2 * cc + u + 1)
                        for i in range(TILES):
                            for g in range(2):
                                pe.matmul(tokv(X[u])[:, i // 2, i % 2, :],
                                          sT[u][:, g, P * i:P * i + P], c_w[:, g, :],
                                          start=(g == 0), stop=(g == 1))
                        for i in range(TILES):
                            for g in range(2):
                                mm = pe.matmul(tokv(Y[u])[:, i // 2, i % 2, :],
                                               xT[u][0:FG + g, g, P * i:P * i + P], g_w[0:FG + g, g, :],
                                               start=(g == 0), stop=(g == 1))
                        mm.then_inc(yg_done, 1)

                    for u in range(2):
                        pe.wait_ge(gelu_y_done, count(cc, u))
                        turn(1, u, X[u], count(cc, u))
                    for u in range(2):
                        pe.wait_ge(xT_done[1], count(cc, u))
                        pe.wait_ge(tanh_g_done, count(cc, u))
                        for i in range(TILES):
                            for g in range(2):
                                mm = pe.matmul(ps[:, Y[u], E * i:E * i + E], xT[u][0:FG, g, P * i:P * i + P],
                                               gate_w[:, g, :], start=(g == 0), stop=(g == 1))
                        mm.then_inc(logits_in_psum, 1)

                    for u in range(2):
                        pe.wait_ge(chosen_done, count(cc, u))
                        dst = ps[:, Y[u], 64:64 + (TILES + 1) * E]
                        pe.matmul(dst, ones_sq[:, :], before[u][:, :, :].rearrange("p i e -> p (i e)"),
                                  start=True, stop=False)
                        pe.matmul(dst[:, 0:TILES * E], later[:, :], chosen[u][:, :, :].rearrange("p i e -> p (i e)"),
                                  start=False, stop=True).then_inc(ranks_in_psum, 1)

                def turn_rows(v, n):
                    pe.wait_ge(xs_in, 16 * n)
                    for g in range(2):
                        mm = pe.transpose(ps[0:FG, 2 * v, P * g:P * g + P], xs[v][:, FG * g:FG * g + FG], ident[:, :])
                    mm.then_inc(xsT_in_psum, 1)

                pe.wait_ge(w_in, 3 * 16 * E)
                pe.wait_ge(xsT_ones, 1)
                pe.wait_ge(table_done, 1)
                for v in range(2):
                    turn_rows(v, 2)
                with pe.Fori(0, MOE_TILES // 2) as tt:
                    experts = [pe.value_load(tile_expert_int[0:1, bass.ds(2 * tt + v, 1)], min_val=0, max_val=E - 1)
                               for v in range(2)]
                    for v in range(2):
                        pe.wait_ge(xsT_done, 2 * tt + v + 1)
                        pe.wait_ge(ys_done, 2 * tt + v + 1)
                        for half in range(2):
                            for g in range(2):
                                k = FG + g
                                mm = pe.matmul(ps[:, 2 * v + half, 0:HID // 2], xsT[v][0:k, g, :],
                                               w1[0:k, bass.ds(experts[v], 1), g, half * (HID // 2):(half + 1) * (HID // 2)]
                                               .rearrange("p e n -> p (e n)"), start=(g == 0), stop=(g == 1))
                            mm.then_inc(hid_in_psum, 1)
                    for v in range(2):
                        pe.wait_ge(hid_act_done, 2 * tt + v + 1)
                        for m in range(HC):
                            if m == HC // 2:
                                pe.wait_ge(hid_dve_done, 2 * tt + v + 1)
                            mm = pe.transpose(ps[:, 4 + 2 * v + m // 3, P * (m % 3):P * (m % 3) + P],
                                              hid[v][:, P * m:P * m + P], ident[:, :])
                        mm.then_inc(hidT_in_psum, 1)
                    for v in range(2):
                        turn_rows(v, 2 * tt + 4)
                    for v in range(2):
                        pe.wait_ge(hidT_act_done, 2 * tt + v + 1)
                        for m in range(HC):
                            if m == HC // 2:
                                pe.wait_ge(hidT_dve_done, 2 * tt + v + 1)
                            mm = pe.matmul(ps[:, 2 * v + 1, 0:D], hidT[v][:, m, :],
                                           w2[:, bass.ds(experts[v], 1), D * m:D * m + D].rearrange("p e n -> p (e n)"),
                                           start=(m == 0), stop=(m == HC - 1))
                        mm.then_inc(ys_in_psum, 1)

                pe.wait_ge(kk_map_done, 1)
                pe.wait_ge(late_const, 1)
                pe.wait_ge(late_in, LATE)
                pe.wait_ge(xsT_done, MOE_TILES + 2)
                pe.wait_ge(ys_done, YS0 + MOE_TILES)
                with pe.Fori(0, CHUNKS // 2) as cc:
                    W = [0, 4]
                    for u in range(2):
                        turn(2, u, W[u], count(cc, u))
                    for u in range(2):
                        pe.wait_ge(xT_done[2], count(cc, u))
                        for j in range(HG):
                            for bank, w, read, done, there in ((2, wq, 0, q_done, q_in_psum), (3, wk, 1, k_done, k_in_psum)):
                                if j == 2:
                                    pe.wait_ge(done, 3 * (2 * cc + u) + 1)
                                for g in range(2):
                                    mm = pe.matmul(ps[:, W[u] + (bank if j != 1 else read), 0:CT],
                                                   w[:, g, P * j:P * j + P], seqs(xT[u][0:FG, g, :]),
                                                   start=(g == 0), stop=(g == 1))
                                mm.then_inc(there, 1)
                        pe.wait_ge(q_done, 3 * (2 * cc + u) + 2)
                        pe.wait_ge(k_done, 3 * (2 * cc + u) + 2)
                        for s_ in range(CB):
                            for odd in range(2):
                                for g in range(2):
                                    mm = pe.matmul(ps[HALF * odd:HALF * odd + HALF, W[u] + s_ // 4,
                                                      FG * (s_ % 4):FG * (s_ % 4) + FG],
                                                   xT[u][0:FG, g, HALF * s_:HALF * s_ + HALF],
                                                   wv[:, g, FG * odd:FG * odd + FG], start=(g == 0), stop=(g == 1))
                        mm.then_inc(v_in_psum, 1)
                    for u in range(2):
                        pe.wait_ge(q_done, 3 * (2 * cc + u) + 3)
                        pe.wait_ge(k_done, 3 * (2 * cc + u) + 3)
                        for j in range(HG):
                            if j == 2:
                                pe.wait_ge(v_low_done, count(cc, u))
                                pe.wait_ge(v_high_done, count(cc, u))
                            mm = pe.matmul(ps[:, W[u] + (2, 3, 0)[j], 0:CT], to_kk[:, :], kk[u][:, j, :, 0, :],
                                           start=True, stop=True).then_inc(kk_in_psum, 1)
                    for i in range(TILES):
                        for u in range(2):
                            if i == 0:
                                pe.wait_ge(kk_act_done, 2 * (2 * cc + u) + 2)
                                pe.wait_ge(kk_dve_done, count(cc, u))
                            else:
                                pe.wait_ge(squares_done, 8 * cc + 2 * i + u - 1)
                            for b in range(2):
                                for j in range(HG):
                                    for r in range(4):
                                        mm = pe.matmul(ps[HALF * b:HALF * b + HALF, W[u] + r, HW * j:HW * j + HW],
                                                       q[u][32 * r:32 * r + 32, j, P * i + HALF * b:P * i + HALF * b + HALF],
                                                       kk[u][32 * r:32 * r + 32, j, 2 * i + b, :, :],
                                                       start=True, stop=True)
                            mm.then_inc(scores_in_psum, 1)
                    for i in range(TILES + 1):
                        for u in range(2):
                            t = 8 * cc + 2 * i + u
                            if i < TILES:
                                if i == 0:
                                    pe.wait_ge(exp_done, count(cc, u))
                                    pe.wait_ge(squares_done, 8 * cc + 7 + u)
                                else:
                                    pe.wait_ge(pT_act_done, t - 1)
                                    pe.wait_ge(pT_dve_done, t - 1)
                                for pr in range(HEADS // 2):
                                    h0 = HEADS * i + 2 * pr
                                    mm = pe.transpose(ps[:, W[u] + pr // 3, P * (pr % 3):P * (pr % 3) + P],
                                                      sc[u][:, h0:h0 + 2, :].rearrange("p h k -> p (h k)"), ident[:, :])
                                mm.then_inc(pT_in_psum, 1)
                            if i >= 1:
                                pe.wait_ge(pT_act_done, t - 1)
                                pe.wait_ge(pT_dve_done, t - 1)
                                if i >= 3:
                                    pe.wait_ge(ctx_scaled, t - 5)
                                for b in range(2):
                                    for pr in range(HEADS // 2):
                                        mm = pe.matmul(ps[HALF * b:HALF * b + HALF, W[u] + 2 + i % 2,
                                                          2 * VW * pr:2 * VW * pr + 2 * VW],
                                                       probsT[u][:, pr, HALF * b:HALF * b + HALF],
                                                       vals[u][:, 2 * (i - 1) + b, pr, :, :], start=True, stop=True)
                                mm.then_inc(ctx_in_psum, 1)
                    for u in range(2):
                        turn(3, u, W[u], count(cc, u))
                    for u in range(2):
                        pe.wait_ge(xT_done[3], count(cc, u))
                        pe.wait_ge(ctx_scaled, 8 * cc + 8)
                        for g in range(2):
                            mm = pe.matmul(ps[0:R1, W[u] + 2, 0:CT], enc_w[:, g, :], seqs(xT[u][0:FG, g, :]),
                                           start=(g == 0), stop=(g == 1))
                        mm.then_inc(enc_in_psum, 1)
                    for u in range(2):
                        pe.wait_ge(enc_done, count(cc, u))
                        for i in range(TILES):
                            mm = pe.matmul(ps[:, W[u] + 3, E * i:E * i + E], xeT[u][:, P * i:P * i + P], sw_w[:, :],
                                           start=True, stop=True)
                        mm.then_inc(s_logits_in_psum, 1)
                    for u in range(2):
                        pe.wait_ge(onehot_done, count(cc, u))
                        for i in range(TILES):
                            mm = pe.matmul(ps[FG:FG + E, W[u] + 2, P * i:P * i + P], s_onehot[u][:, i, :], ident[:, :],
                                           start=True, stop=True)
                        mm.then_inc(onehotT_in_psum, 1)
                    for u in range(2):
                        pe.wait_ge(onehotT_done, count(cc, u))
                        for m in range(4):
                            for g in range(2):
                                k = FG + E * g
                                mm = pe.matmul(ps[:, W[u] + m, 0:CT], s_w1[0:k, g, P * m:P * m + P],
                                               seqs(xT[u][0:k, g, :]), start=(g == 0), stop=(g == 1))
                            mm.then_inc(s_hid_in_psum, 1)
                    for u in range(2):
                        pe.wait_ge(s_hid_done, 4 * (2 * cc + u) + 4)
                        for i in range(TILES):
                            dst = tokv(W[u])[:, i // 2, i % 2, :]
                            for m in range(4):
                                pe.matmul(dst, s_hidT[u][:, m, P * i:P * i + P], s_w2[:, m, :], start=(m == 0), stop=False)
                            mm = pe.matmul(dst, xT[u][FG:FG + E, 1, P * i:P * i + P], s_b2[FG:FG + E, :],
                                           start=False, stop=True)
                        mm.then_inc(s_out_in_psum, 1)

            @block.scalar
            def _(act):
                act.wait_ge(load, LOADED)
                act.wait_ge(const_done, 1)
                nc.scalar.activation(tanh_delta[:, :], a_delta[:, :], ACT.Tanh).then_inc(tanh_done, 1)
                act.wait_ge(lam_coef_done, 3)

                def turned(norm, u, banks, n):
                    act.wait_ge(xT_in_psum[norm], n)
                    for g in range(2):
                        last = nc.scalar.copy(seqs(xT[u][0:FG, g, :]), seqs(ps[0:FG, banks + g, :]))
                    last.then_inc(xT_done[norm], 1)

                X = [0, 4]
                Y = [2, 6]
                with act.Fori(0, CHUNKS // 2) as cc:
                    for u in range(2):
                        turned(0, u, Y[u], count(cc, u))
                    for u in range(2):
                        act.wait_ge(ze_done, 2 * cc + u + 1)
                        nc.scalar.copy(seqs(zT[u][:, :]), packed(ps[0:16, X[u], 0:CT])).then_inc(zT_done, 1)
                        nc.scalar.activation(gelu_e[u][:, :], ps[0:64, X[u] + 1, 0:CT],
                                             ACT.Gelu).then_inc(gelu_e_done, 1)
                    for u in range(2):
                        act.wait_ge(bu_done, 2 * cc + u + 1)
                        for g in range(2):
                            last = nc.scalar.activation(seqs(lam[u][:, g, :]), packed(ps[0:FG, X[u] + g, 0:CT]),
                                                        ACT.Tanh, bias=half_e2_b[:, g:g + 1], scale=0.5)
                        last.then_inc(tanh_alpha_done, 1)
                        act.wait_ge(tanh_alpha_done, 2 * cc + u + 1)
                        for g in range(2):
                            last = nc.scalar.activation(seqs(lam[u][:, g, :]), seqs(lam[u][:, g, :]),
                                                        ACT.Tanh, bias=lam_bias[:, g:g + 1],
                                                        scale=lam_scale[:, g:g + 1])
                        last.then_inc(tanh_lam_done, 1)
                    for u in range(2):
                        act.wait_ge(yg_done, 2 * cc + u + 1)
                        nc.scalar.activation(tok(gelu_y[u]), tokv(X[u]), ACT.Gelu).then_inc(gelu_y_done, 1)
                        nc.scalar.activation(tok(tanh_g[u]), tokv(Y[u]), ACT.Tanh,
                                             scale=0.5).then_inc(tanh_g_done, 1)

                    for u in range(2):
                        turned(1, u, X[u], count(cc, u))
                    for u in range(2):
                        act.wait_ge(r_shifted, count(cc, u))
                        nc.scalar.activation(r_exp[u][:, :, :], r_exp[u][:, :, :], ACT.Exp).then_inc(r_exp_done, 1)

                def rows_turned(v, n):
                    act.wait_ge(xsT_in_psum, n)
                    nc.scalar.copy(xsT[v][0:FG, :, :], ps[0:FG, 2 * v, 0:2 * P].rearrange("p (g t) -> p g t", g=2)
                                   ).then_inc(xsT_done, 1)

                act.wait_ge(xsT_ones, 1)
                for v in range(2):
                    rows_turned(v, v + 1)
                with act.Fori(0, MOE_TILES // 2) as tt:
                    for v in range(2):
                        act.wait_ge(hid_in_psum, 2 * (2 * tt + v) + 1)
                        act.wait_ge(hidT_in_psum, HIDT0 + 2 * tt + v - 1)
                        nc.scalar.activation(hid[v][:, 0:HID // 2], ps[:, 2 * v, 0:HID // 2],
                                             ACT.Relu).then_inc(hid_act_done, 1)
                    for v in range(2):
                        act.wait_ge(hidT_in_psum, HIDT0 + 2 * tt + v + 1)
                        act.wait_ge(ys_in_psum, YSP0 + 2 * tt + v - 1)
                        nc.scalar.copy(hidT[v][:, 0:3, :], ps[:, 4 + 2 * v, 0:3 * P].rearrange("p (m t) -> p m t", m=3)
                                       ).then_inc(hidT_act_done, 1)
                    for v in range(2):
                        rows_turned(v, 2 * tt + v + 3)
                act.wait_ge(late_const, 1)
                W = [0, 4]
                with act.Fori(0, CHUNKS // 2) as cc:
                    for u in range(2):
                        turned(2, u, W[u], count(cc, u))
                    for u in range(2):
                        for j in range(HG):
                            act.wait_ge(q_in_psum, 3 * (2 * cc + u) + j + 1)
                            nc.scalar.copy(seqs(q[u][:, j, :]), packed(ps[:, W[u] + (2, 0, 2)[j], 0:CT])).then_inc(q_done, 1)
                        act.wait_ge(v_in_psum, count(cc, u))
                        for bank in range(2):
                            last = nc.scalar.copy(
                                vals[u][0:HALF, 4 * bank:4 * bank + 4, :, 0, 0:DH],
                                ps[0:HALF, W[u] + bank, 0:4 * FG].rearrange("p (s h d) -> p s h d", s=4, d=DH))
                        last.then_inc(v_low_done, 1)
                    for u in range(2):
                        for n, j in enumerate((0, 2)):
                            act.wait_ge(kk_in_psum, 3 * (2 * cc + u) + j + 1)
                            nc.scalar.copy(kk[u][:, j, :, 1, :], packed(ps[:, W[u] + (2, 3, 0)[j], 0:CT])).then_inc(kk_act_done, 1)
                    for i in range(TILES):
                        for u in range(2):
                            act.wait_ge(scores_in_psum, 8 * cc + 2 * i + u + 1)
                            if i:
                                act.wait_ge(sc2_done, 8 * cc + 2 * i + u - 1)
                            nc.scalar.activation(squares[u][:, :, :, :].rearrange("p (r j) c k -> p r (j c k)", r=4),
                                                 ps[:, W[u]:W[u] + 4, 0:HG * HW], ACT.Square).then_inc(squares_done, 1)
                    for u in range(2):
                        act.wait_ge(sc2_max_done, 8 * cc + 7 + u)
                        nc.scalar.activation(sc[u][:, :, 0:T], sc[u][:, :, 0:T], ACT.Sqrt,
                                             scale=SCALE2).then_inc(sqrt_done, 1)
                        nc.scalar.activation(sc_max[u][:, :], sc_max[u][:, :], ACT.Sqrt,
                                             scale=SCALE2).then_inc(sqrt_max_done, 1)
                    for u in range(2):
                        act.wait_ge(sc_shifted, count(cc, u))
                        nc.scalar.activation(sc[u][:, :, 0:T], sc[u][:, :, 0:T], ACT.Exp).then_inc(exp_done, 1)
                    for i in range(TILES):
                        for u in range(2):
                            act.wait_ge(pT_in_psum, 8 * cc + 2 * i + u + 1)
                            if i:
                                act.wait_ge(ctx_in_psum, 8 * cc + 2 * i + u - 1)
                            nc.scalar.copy(probsT[u][:, 0:3, :], ps[:, W[u], 0:3 * P]).then_inc(pT_act_done, 1)
                    for u in range(2):
                        turned(3, u, W[u], count(cc, u))
                    for u in range(2):
                        act.wait_ge(enc_in_psum, count(cc, u))
                        nc.scalar.activation(seqs(xeT[u][0:R1, :]), packed(ps[0:R1, W[u] + 2, 0:CT]), ACT.Identity,
                                             bias=enc_b[:, 0:1]).then_inc(enc_done, 1)
                    for u in range(2):
                        act.wait_ge(s_shifted, count(cc, u))
                        nc.scalar.activation(s_exp[u][:, :, :], s_logits[u][:, :, :], ACT.Exp).then_inc(s_exp_done, 1)
                    for u in range(2):
                        act.wait_ge(onehotT_in_psum, count(cc, u))
                        nc.scalar.copy(xT[u][FG:FG + E, 1, :], ps[FG:FG + E, W[u] + 2, :]).then_inc(onehotT_done, 1)
                    for u in range(2):
                        for m in range(4):
                            act.wait_ge(s_hid_in_psum, 4 * (2 * cc + u) + m + 1)
                            nc.scalar.activation(seqs(s_hidT[u][:, m, :]), packed(ps[:, W[u] + m, 0:CT]),
                                                 ACT.Gelu).then_inc(s_hid_done, 1)

            @block.vector
            def _(dve):
                X = [0, 4]
                Y = [2, 6]
                nc.vector.memset(cls_at[:, :], 0.0).then_inc(cls_zero, 1)
                dve.wait_ge(cls_zero, 1)
                for b in range(2):
                    nc.vector.memset(cls_at[:, HALF * b:HALF * b + 1], 1.0)
                nc.vector.memset(zeros[:, :], 0.0)
                nc.vector.memset(ones_e[:, :], 1.0)
                dve.wait_ge(ramp_done, 2)
                nc.vector.tensor_copy(row_index[:, :], row_index_int[:, :])
                nc.vector.tensor_copy(ramp[:, :], ramp_int[:, :]).then_inc(ramp_copied, 1)
                dve.wait_ge(ramp_copied, 1)
                nc.vector.tensor_scalar(in_first[:, :], row_index[:, :], float(T), None, ALU.is_lt)
                nc.vector.tensor_scalar(in_second[:, :], row_index[:, :], float(HALF), None, ALU.is_ge).then_inc(ramp_copied, 1)
                dve.wait_ge(ramp_copied, 2)
                nc.vector.scalar_tensor_tensor(in_second[:, :], row_index[:, :], float(HALF + T), in_second[:, :],
                                               ALU.is_lt, ALU.mult).then_inc(ramp_copied, 1)
                dve.wait_ge(ramp_copied, 3)
                nc.vector.tensor_tensor(valid[:, :], in_first[:, :], in_second[:, :], ALU.add).then_inc(ramp_copied, 1)
                dve.wait_ge(ramp_copied, 4)
                nc.vector.tensor_scalar(skip[:, :], valid[:, :], -SKIP, SKIP, ALU.mult, ALU.add)
                nc.vector.tensor_scalar(expert_rank[:, :], ramp[:, 0:E], -1.0, float(E), ALU.mult, ALU.add)
                nc.vector.tensor_scalar(steps128[:, :], ramp[:, 0:13], float(P), None, ALU.mult)
                nc.vector.tensor_scalar(region[:, :], ramp[:, 0:E], float(SLOTS), None, ALU.mult)
                nc.vector.tensor_scalar(next_row[:, :], ramp[:, 0:E], float(SLOTS), None, ALU.mult)
                for u in range(2):
                    nc.vector.memset(before[u][:, 0, :], 0.0)
                for u in range(2):
                    nc.vector.memset(lam[u][:, :, :], 0.0)
                    nc.vector.memset(zT[u][:, :], 0.0)
                    nc.vector.memset(xT[u][0:FG, :, :], 0.0)
                    last = nc.vector.memset(xT[u][FG:FG + 1, :, :], 1.0)
                last.then_inc(const_done, 1)
                for started, at in ((x2_moved, MOVED0), (ys_stored, STORED0), (out_done, OUT0), (ys_done, YS0),
                                    (hidT_in_psum, HIDT0), (ys_in_psum, YSP0)):
                    dve.sem_inc(started, at)
                dve.wait_ge(load, LOADED)
                nc.vector.tensor_scalar(half_e2_b[:, :], e2_b[:, :], 0.5, None, ALU.mult).then_inc(lam_coef_done, 1)
                dve.wait_ge(tanh_done, 1)
                nc.vector.tensor_scalar(lam_scale[:, :], tanh_delta[:, :], 0.25, None, ALU.mult).then_inc(lam_coef_done, 1)
                nc.vector.scalar_tensor_tensor(lam_mid[:, :], tanh_delta[:, :], 0.5, a_base[:, :], ALU.mult,
                                               ALU.add).then_inc(lam_mid_done, 1)
                dve.wait_ge(lam_mid_done, 1)
                nc.vector.tensor_scalar(lam_bias[:, :], lam_mid[:, :], 0.5, None, ALU.mult).then_inc(lam_coef_done, 1)

                def norm_stats(norm, u, src, n):
                    for i in range(TILES):
                        last = nc.vector.bn_stats(stats[u][:, i, :], src(i))
                    last.then_inc(stats_done[norm], 1)
                    dve.wait_ge(stats_done[norm], n)
                    nc.vector.tensor_copy(carrier[u][:, norm:norm + 1], stats[u][:, 0, 0:1])
                    for i in range(TILES):
                        last = nc.vector.bn_aggr(meanvar[u][:, i, :], stats[u][:, i, :])
                    last.then_inc(var_done[norm], 1)

                def norm_apply(norm, u, src, n):
                    dve.wait_ge(rstd_done[norm], n)
                    for i in range(TILES):
                        last = nc.vector.tensor_scalar((x2_tok if norm == 1 else x_tok)[u][:, i, :], src(i), meanvar[u][:, i, 0:1],
                                                       rstd[u][:, i:i + 1], ALU.subtract, ALU.mult)
                    last.then_inc(x_done[norm], 1)

                with dve.Fori(0, CHUNKS // 2) as cc:
                    for u in range(2):
                        dve.wait_ge(patch_done, count(cc, u))
                        norm_stats(0, u, lambda i: tokv(X[u])[:, i // 2, i % 2, :], count(cc, u))
                    for u in range(2):
                        norm_apply(0, u, lambda i: tokv(X[u])[:, i // 2, i % 2, :], count(cc, u))
                        dve.wait_ge(x_done[0], count(cc, u))
                        nc.vector.tensor_tensor(tok(h_plus_x[u]), tokv(X[u]), tok(x_tok[u]),
                                                ALU.add).then_inc(hx_done, 1)
                    for u in range(2):
                        n = 2 * cc + u + 1
                        dve.wait_ge(tanh_lam_done, n)
                        for g in range(2):
                            last = nc.vector.tensor_scalar(seqs(lam[u][:, g, :]), seqs(lam[u][:, g, :]), 0.5, 0.5,
                                                           ALU.mult, ALU.add)
                        last.then_inc(lam_done, 1)
                        dve.wait_ge(lam_done, n)
                        dve.wait_ge(bu_done, n)
                        for g in range(2):
                            last = nc.vector.tensor_tensor_scan(sT[u][:, g, :], lam[u][:, g, :], ps[0:FG, Y[u] + g, :],
                                                                0.0, ALU.mult, ALU.add)
                        last.then_inc(scan_done, 1)
                    for u in range(2):
                        n = 2 * cc + u + 1
                        dve.wait_ge(gelu_y_done, n)
                        dve.wait_ge(tanh_g_done, n)
                        nc.vector.scalar_tensor_tensor(gelu_y[u][:, :, :], tanh_g[u][:, :, :], 1.0, gelu_y[u][:, :, :],
                                                       ALU.add, ALU.mult).then_inc(gated_done, 1)
                        dve.wait_ge(gated_done, n)
                        nc.vector.scalar_tensor_tensor(h[:, bass.ds((2 * cc + u) * TILES, TILES), :],
                                                       gelu_y[u][:, :, :], 0.5, h_plus_x[u][:, :, :],
                                                       ALU.mult, ALU.add).then_inc(h_done, 1)
                    for u in range(2):
                        dve.wait_ge(h_done, count(cc, u))
                        nc.vector.tensor_copy(carrier[u][:, 4:5], gelu_y[u][:, 0, 0:1])
                        norm_stats(1, u, lambda i: tile_of(h, cc, u, i), count(cc, u))
                    for u in range(2):
                        dve.wait_ge(x2_moved, MOVED0 + 2 * cc + u - 1)
                        norm_apply(1, u, lambda i: tile_of(h, cc, u, i), count(cc, u))
                    for u in range(2):
                        n = count(cc, u)
                        got = ps[:, Y[u], 0:TILES * E].rearrange("p (i e) -> p i e", e=E)
                        k = ROUTE_STEPS * (2 * cc + u)
                        dve.wait_ge(logits_in_psum, n)
                        nc.vector.tensor_reduce(r_max[u][:, :], got, AX.X, ALU.max).then_inc(route_step, 1)
                        dve.wait_ge(route_step, k + 1)
                        nc.vector.tensor_tensor(r_exp[u][:, :, :], got, spread(r_max[u][:, :], E),
                                                ALU.subtract).then_inc(r_shifted, 1)
                        dve.wait_ge(r_exp_done, n)
                        nc.vector.tensor_reduce(r_sum[u][:, :], r_exp[u][:, :, :], AX.X, ALU.add).then_inc(route_step, 1)
                        dve.wait_ge(route_step, k + 2)
                        nc.vector.reciprocal(r_sum[u][:, :], r_sum[u][:, :]).then_inc(route_step, 1)
                        dve.wait_ge(route_step, k + 3)
                        nc.vector.tensor_tensor(probs[u][:, :, :], r_exp[u][:, :, :], spread(r_sum[u][:, :], E),
                                                ALU.mult).then_inc(route_step, 1)
                        dve.wait_ge(route_step, k + 4)
                        first, second = chunk_of(all_first, cc, u), chunk_of(all_second, cc, u)
                        for src, dst, gate, at in ((probs, first, 0, 4), (others, second, 1, 9)):
                            nc.vector.tensor_reduce(best[u][:, :], src[u][:, :, :], AX.X, ALU.max).then_inc(route_step, 1)
                            dve.wait_ge(route_step, k + at + 1)
                            nc.vector.tensor_scalar(chunk_of(all_gates, cc, u)[:, :, gate], best[u][:, :], 1.0, None,
                                                    ALU.mult)
                            nc.vector.tensor_tensor(rank[u][:, :, :], src[u][:, :, :], spread(best[u][:, :], E),
                                                    ALU.is_equal).then_inc(route_step, 1)
                            dve.wait_ge(route_step, k + at + 2)
                            nc.vector.tensor_tensor(rank[u][:, :, :], rank[u][:, :, :], repeat(expert_rank[:, :], TILES),
                                                    ALU.mult).then_inc(route_step, 1)
                            dve.wait_ge(route_step, k + at + 3)
                            nc.vector.tensor_reduce(best[u][:, :], rank[u][:, :, :], AX.X, ALU.max).then_inc(route_step, 1)
                            dve.wait_ge(route_step, k + at + 4)
                            nc.vector.tensor_tensor(dst, rank[u][:, :, :], spread(best[u][:, :], E),
                                                    ALU.is_equal).then_inc(route_step, 1)
                            dve.wait_ge(route_step, k + at + 5)
                            if dst is first:
                                nc.vector.scalar_tensor_tensor(others[u][:, :, :], first, -2.0, probs[u][:, :, :],
                                                               ALU.mult, ALU.add).then_inc(route_step, 1)
                                dve.wait_ge(route_step, k + 10)
                                k = k + 1
                        nc.vector.tensor_tensor(chosen[u][:, :, :], first, second,
                                                ALU.add).then_inc(route_step, 1)
                        dve.wait_ge(route_step, k + 15)
                        nc.vector.tensor_scalar(chosen[u][:, :, :], chosen[u][:, :, :], valid[:, 0:1], None,
                                                ALU.mult).then_inc(route_step, 1)
                        for i in range(TILES):
                            dve.wait_ge(route_step, k + 16 + i)
                            nc.vector.tensor_tensor(before[u][:, i + 1, :], before[u][:, i, :], chosen[u][:, i, :],
                                                    ALU.add).then_inc(route_step, 1)
                        dve.wait_ge(route_step, k + 16 + TILES)
                        nc.vector.tensor_copy(carrier[u][:, 6:7], before[u][:, TILES, 0:1]).then_inc(chosen_done, 1)
                    for u in range(2):
                        n = count(cc, u)
                        k = ROW_STEPS * (2 * cc + u)
                        got = ps[:, Y[u], 64:64 + TILES * E].rearrange("p (i e) -> p i e", e=E)
                        dve.wait_ge(ranks_in_psum, n)
                        nc.vector.tensor_tensor(row_of[u][:, :, :], got, repeat(next_row[:, :], TILES),
                                                ALU.add).then_inc(row_step, 1)
                        dve.wait_ge(row_step, k + 1)
                        nc.vector.tensor_tensor(next_row[:, :], ps[:, Y[u], 64 + TILES * E:64 + (TILES + 1) * E],
                                                next_row[:, :], ALU.add).then_inc(row_step, 1)
                        nc.vector.tensor_tensor(rank[u][:, :, :], chunk_of(all_first, cc, u), row_of[u][:, :, :],
                                                ALU.mult).then_inc(row_step, 1)
                        nc.vector.tensor_tensor(others[u][:, :, :], chunk_of(all_second, cc, u), row_of[u][:, :, :],
                                                ALU.mult).then_inc(row_step, 1)
                        dve.wait_ge(row_step, k + 4)
                        nc.vector.tensor_reduce(row_sum[u][:, 0, :], rank[u][:, :, :], AX.X, ALU.add)
                        nc.vector.tensor_reduce(row_sum[u][:, 1, :], others[u][:, :, :], AX.X, ALU.add).then_inc(row_step, 1)
                        dve.wait_ge(row_step, k + 5)
                        nc.vector.tensor_scalar(rows[u][:, :, :], row_sum[u][:, :, :], valid[:, 0:1], skip[:, 0:1],
                                                ALU.mult, ALU.add)
                        nc.vector.tensor_scalar(all_rows[:, :, bass.ds((2 * cc + u) * TILES, TILES)], row_sum[u][:, :, :],
                                                valid[:, 0:1], skip[:, 0:1], ALU.mult, ALU.add).then_inc(rows_done, 1)

                N = MOE_TILES + 2
                steps = [0]

                def linked(ins):
                    steps[0] += 1
                    ins.then_inc(table_step, 1)
                    dve.wait_ge(table_step, steps[0])

                dve.wait_ge(rows_done, CHUNKS)
                dve.wait_ge(row_step, ROW_STEPS * CHUNKS)
                linked(nc.vector.tensor_tensor(counts[:, :], next_row[:, :], region[:, :], ALU.subtract))
                linked(nc.vector.tensor_tensor(over[:, :, :], spread(counts[:, :], 13), repeat(steps128[:, :], E), ALU.is_gt))
                linked(nc.vector.tensor_reduce(n_tiles[:, :], over[:, :, :], AX.X, ALU.add))
                linked(nc.vector.tensor_tensor_scan(tiles_to[:, :], ones_e[:, :], n_tiles[:, :], 0.0, ALU.mult, ALU.add))
                linked(nc.vector.tensor_tensor(behind[:, :, :], spread(ramp[:, :], E - 1), repeat(tiles_to[:, 0:E - 1], N),
                                               ALU.is_ge))
                linked(nc.vector.tensor_reduce(tile_expert[:, :], behind[:, :, :], AX.X, ALU.add))
                linked(nc.vector.tensor_tensor(behind[:, :, :], behind[:, :, :], repeat(n_tiles[:, 0:E - 1], N), ALU.mult))
                linked(nc.vector.tensor_reduce(tiles_behind[:, :], behind[:, :, :], AX.X, ALU.add))
                linked(nc.vector.tensor_scalar(live[:, :], ramp[:, :], tiles_to[:, E - 1:E], None, ALU.is_lt))
                linked(nc.vector.tensor_tensor(tile_row[:, :], ramp[:, :], tiles_behind[:, :], ALU.subtract))
                linked(nc.vector.tensor_scalar(tile_row[:, :], tile_row[:, :], float(P), None, ALU.mult))
                linked(nc.vector.scalar_tensor_tensor(tile_row[:, :], tile_expert[:, :], float(SLOTS), tile_row[:, :],
                                                      ALU.mult, ALU.add))
                linked(nc.vector.scalar_tensor_tensor(load_row[:, :], tile_row[:, :], -float(NULL_ROW), live[:, :],
                                                      ALU.add, ALU.mult))
                nc.vector.tensor_scalar(load_row_int[:, :], load_row[:, :], float(NULL_ROW), None, ALU.add)
                nc.vector.tensor_copy(tile_expert_int[:, :], tile_expert[:, :])
                nc.vector.tensor_copy(next_row_int[:, :], next_row[:, :]).then_inc(table_done, 1)
                dve.wait_ge(xT_in_psum[1], CHUNKS)
                for v in range(2):
                    last = nc.vector.memset(xsT[v][FG:FG + 1, :, :], 1.0)
                last.then_inc(xsT_ones, 1)
                nc.vector.memset(s_w1[FG:FG + E, 1, :], -OFF).then_inc(off_done, 1)

                linked(nc.vector.tensor_tensor(moved[:, :], tiles_to[:, :], n_tiles[:, :], ALU.subtract))
                linked(nc.vector.scalar_tensor_tensor(moved[:, :], moved[:, :], float(P), region[:, :], ALU.mult, ALU.subtract))
                for k, onehot in enumerate((all_first, all_second)):
                    linked(nc.vector.tensor_tensor(onehot[:, :, :], onehot[:, :, :], repeat(moved[:, :], NT), ALU.mult))
                    linked(nc.vector.tensor_reduce(row_move[:, k, :], onehot[:, :, :], AX.X, ALU.add))
                linked(nc.vector.tensor_tensor(y_rows[:, :, :], all_rows[:, :, :], row_move[:, :, :], ALU.add))
                dve.wait_ge(table_done, 1)
                with dve.Fori(0, MOE_TILES // 2) as tt:
                    for v in range(2):
                        dve.wait_ge(hid_in_psum, 2 * (2 * tt + v) + 2)
                        dve.wait_ge(hidT_in_psum, HIDT0 + 2 * tt + v - 1)
                        nc.vector.tensor_scalar(hid[v][:, HID // 2:HID], ps[:, 2 * v + 1, 0:HID // 2], 0.0, None,
                                                ALU.max).then_inc(hid_dve_done, 1)
                    for v in range(2):
                        dve.wait_ge(hidT_in_psum, HIDT0 + 2 * tt + v + 1)
                        dve.wait_ge(ys_in_psum, YSP0 + 2 * tt + v - 1)
                        nc.vector.tensor_copy(hidT[v][:, 3:6, :], ps[:, 5 + 2 * v, 0:3 * P].rearrange("p (m t) -> p m t", m=3)
                                              ).then_inc(hidT_dve_done, 1)
                    for v in range(2):
                        e = dve.value_load(tile_expert_int[0:1, bass.ds(2 * tt + v, 1)], min_val=0, max_val=E - 1)
                        dve.wait_ge(ys_stored, 32 * tt + 16)
                        dve.wait_ge(ys_in_psum, YSP0 + 2 * tt + v + 1)
                        nc.vector.tensor_tensor(ys[v][:, :], ps[:, 2 * v + 1, 0:D],
                                                b2[:, bass.ds(e, 1), :].rearrange("p e d -> p (e d)"),
                                                ALU.add).then_inc(ys_done, 1)

                dve.wait_ge(ys_in_psum, YSP0 + MOE_TILES)
                dve.wait_ge(vals_zero, 1)
                for u in range(2):
                    nc.vector.memset(y_first[u][:, :, :], 0.0)
                    last = nc.vector.memset(y_second[u][:, :, :], 0.0)
                last.then_inc(y_init, 1)
                for u in range(2):
                    nc.vector.memset(vals[u][0:HALF, :, :, 0, DH:VW], 1.0)
                    nc.vector.memset(vals[u][HALF:P, :, :, 1, DH:VW], 1.0)
                    nc.vector.memset(xeT[u][0:R1, :], 0.0)
                    nc.vector.memset(xeT[u][R1:R1 + 1, :], 1.0)
                    nc.vector.memset(sc[u][:, :, T:HALF], 0.0)
                    last = nc.vector.memset(s_hidT[u][:, :, :].rearrange("p m (s t) -> p (m s) t", t=HALF)[:, :, T:HALF], 0.0)
                last.then_inc(late_const, 1)

                W = [0, 4]
                with dve.Fori(0, CHUNKS // 2) as cc:
                    for u in range(2):
                        nc.vector.tensor_copy(rows_now[u][:, :, :], y_rows[:, :, bass.ds((2 * cc + u) * TILES, TILES)]).then_inc(rows_now_done, 1)
                    for u in range(2):
                        dve.wait_ge(gathered[u], MOVES * cc + MOVES)
                        nc.vector.tensor_copy(carrier[u][:, 7:8], y_second[u][:, 0, 0:1])
                        for i in range(TILES):
                            last = nc.vector.scalar_tensor_tensor(
                                tile_of(h, cc, u, i), y_first[u][:, i, :], tile_of(all_gates, cc, u, i)[:, 0:1],
                                tile_of(h, cc, u, i), ALU.mult, ALU.add)
                        last.then_inc(first_added, 1)
                        dve.wait_ge(first_added, count(cc, u))
                        for i in range(TILES):
                            last = nc.vector.scalar_tensor_tensor(
                                tile_of(h, cc, u, i), y_second[u][:, i, :], tile_of(all_gates, cc, u, i)[:, 1:2],
                                tile_of(h, cc, u, i), ALU.mult, ALU.add)
                        last.then_inc(moe_added, 1)
                    for u in range(2):
                        dve.wait_ge(moe_added, count(cc, u))
                        nc.vector.tensor_copy(carrier[u][:, 8:9], y_second[u][:, 0, 0:1])
                        norm_stats(2, u, lambda i: tile_of(h, cc, u, i), count(cc, u))
                    for u in range(2):
                        norm_apply(2, u, lambda i: tile_of(h, cc, u, i), count(cc, u))
                    for u in range(2):
                        for j in range(HG):
                            dve.wait_ge(k_in_psum, 3 * (2 * cc + u) + j + 1)
                            nc.vector.tensor_copy(kk[u][:, j, :, 0, :], packed(ps[:, W[u] + (3, 1, 3)[j], 0:CT])).then_inc(k_done, 1)
                        dve.wait_ge(v_in_psum, count(cc, u))
                        for bank in range(2):
                            last = nc.vector.tensor_copy(
                                vals[u][HALF:P, 4 * bank:4 * bank + 4, :, 1, 0:DH],
                                ps[HALF:P, W[u] + bank, 0:4 * FG].rearrange("p (s h d) -> p s h d", s=4, d=DH))
                        last.then_inc(v_high_done, 1)
                    for u in range(2):
                        dve.wait_ge(kk_in_psum, 3 * (2 * cc + u) + 2)
                        nc.vector.tensor_copy(kk[u][:, 1, :, 1, :], packed(ps[:, W[u] + 3, 0:CT])).then_inc(kk_dve_done, 1)
                    for i in range(TILES):
                        for u in range(2):
                            n = 8 * cc + 2 * i + u + 1
                            dst = sc[u][:, HEADS * i:HEADS * i + HEADS, 0:T]
                            dve.wait_ge(squares_done, n)
                            nc.vector.tensor_tensor(dst, squares[u][:, :, 0, :], squares[u][:, :, 1, :],
                                                    ALU.add).then_inc(sc2_done, 1)
                            dve.wait_ge(sc2_done, n)
                            nc.vector.tensor_reduce(sc_max[u][:, HEADS * i:HEADS * i + HEADS], dst, AX.X,
                                                    ALU.max).then_inc(sc2_max_done, 1)
                    for u in range(2):
                        dve.wait_ge(sqrt_done, count(cc, u))
                        dve.wait_ge(sqrt_max_done, count(cc, u))
                        nc.vector.tensor_tensor(sc[u][:, :, 0:T], sc[u][:, :, 0:T], spread(sc_max[u][:, :], T),
                                                ALU.subtract).then_inc(sc_shifted, 1)
                    for i in range(TILES + 1):
                        for u in range(2):
                            if i < TILES:
                                dve.wait_ge(pT_in_psum, 8 * cc + 2 * i + u + 1)
                                if i:
                                    dve.wait_ge(ctx_in_psum, 8 * cc + 2 * i + u - 1)
                                nc.vector.tensor_copy(probsT[u][:, 3:6, :], ps[:, W[u] + 1, 0:3 * P]).then_inc(pT_dve_done, 1)
                            if i >= 1:
                                n = 8 * cc + 2 * (i - 1) + u + 1
                                got = ps[:, W[u] + 2 + i % 2, 0:HEADS * VW].rearrange("p (r j d) -> p r j d", r=4, d=VW)
                                dve.wait_ge(ctx_in_psum, n)
                                nc.vector.reciprocal(inv_sum[u][:, :].rearrange("p (r j) -> p r j", r=4),
                                                     got[:, :, :, DH]).then_inc(inv_sum_done, 1)
                                dve.wait_ge(inv_sum_done, n)
                                nc.vector.tensor_tensor(
                                    ctx_tok[u][:, i - 1, :].rearrange("p (j r d) -> p r j d", j=HG, r=4),
                                    got[:, :, :, 0:DH],
                                    spread(inv_sum[u][:, :].rearrange("p (r j) -> p r j", r=4), DH),
                                    ALU.mult).then_inc(ctx_scaled, 1)
                    for u in range(2):
                        dve.wait_ge(ctx_scaled, 8 * cc + 7 + u)
                        nc.vector.tensor_tensor(chunk_of(h, cc, u), chunk_of(h, cc, u), ctx_tok[u][:, :, :],
                                                ALU.add).then_inc(attended, 1)
                    for u in range(2):
                        dve.wait_ge(attended, count(cc, u))
                        nc.vector.tensor_copy(carrier[u][:, 5:6], ctx_tok[u][:, 0, 0:1])
                        norm_stats(3, u, lambda i: tile_of(h, cc, u, i), count(cc, u))
                    for u in range(2):
                        norm_apply(3, u, lambda i: tile_of(h, cc, u, i), count(cc, u))
                    for u in range(2):
                        n = count(cc, u)
                        got = ps[:, W[u] + 3, 0:TILES * E].rearrange("p (i e) -> p i e", e=E)
                        dve.wait_ge(s_logits_in_psum, n)
                        nc.vector.tensor_reduce(s_max[u][:, :], got, AX.X, ALU.max).then_inc(s_max_done, 1)
                        dve.wait_ge(s_max_done, n)
                        nc.vector.tensor_tensor(s_logits[u][:, :, :], got, spread(s_max[u][:, :], E),
                                                ALU.subtract).then_inc(s_shifted, 1)
                    for u in range(2):
                        n = count(cc, u)
                        dve.wait_ge(s_exp_done, n)
                        nc.vector.scalar_tensor_tensor(s_rank[u][:, :, :], s_exp[u][:, :, :], 1.0, repeat(expert_rank[:, :], TILES),
                                                       ALU.is_equal, ALU.mult).then_inc(s_rank_done, 1)
                        nc.vector.tensor_reduce(s_sum[u][:, :], s_exp[u][:, :, :], AX.X, ALU.add).then_inc(s_sum_done, 1)
                        dve.wait_ge(s_rank_done, n)
                        nc.vector.tensor_reduce(s_best[u][:, :], s_rank[u][:, :, :], AX.X, ALU.max).then_inc(s_best_done, 1)
                        dve.wait_ge(s_best_done, n)
                        nc.vector.tensor_tensor(s_onehot[u][:, :, :], s_rank[u][:, :, :], spread(s_best[u][:, :], E),
                                                ALU.is_equal).then_inc(onehot_done, 1)
                        dve.wait_ge(s_sum_done, n)
                        nc.vector.reciprocal(s_prob[u][:, :], s_sum[u][:, :]).then_inc(s_prob_done, 1)
                    for u in range(2):
                        n = count(cc, u)
                        dve.wait_ge(s_out_in_psum, n)
                        dve.wait_ge(s_prob_done, n)
                        dve.wait_ge(out_done, OUT0 + 64 * cc)
                        for i in range(TILES):
                            last = nc.vector.scalar_tensor_tensor(
                                out_tok[u][:, i, :], tokv(W[u])[:, i // 2, i % 2, :], s_prob[u][:, i:i + 1],
                                tile_of(h, cc, u, i), ALU.mult, ALU.add)
                        last.then_inc(out_ready, 1)


def _layout(x, cls_tok, L0_tok_W, L0_attn_V_w, L0_attn_U_w, L0_attn_E1_w, L0_attn_E1_b, L0_attn_E2_w, L0_attn_E2_b,
            L0_attn_a_base, L0_attn_a_delta, L0_attn_C_w, L0_attn_G_w, L0_attn_G_b, L0_ffn_Wg, L0_ffn_W1, L0_ffn_b1,
            L0_ffn_W2, L0_ffn_b2, L1_attn_Wqr, L1_attn_Wqi, L1_attn_Wkr, L1_attn_Wki, L1_attn_Wv, L1_ffn_enc_w,
            L1_ffn_enc_b, L1_ffn_sw_w, L1_ffn_sw_b, L1_ffn_w1, L1_ffn_b1, L1_ffn_w2, L1_ffn_b2):
    import numpy as np
    np_ = {}

    def groups(w, bias=None):
        a = np.reshape(np.asarray(w), (2, FG, -1)).transpose(1, 0, 2)
        if bias is None:
            return np.ascontiguousarray(a)
        row = np.zeros((1, 2, a.shape[2]), a.dtype)
        row[0, 1] = np.asarray(bias)
        return np.concatenate([a, row], 0)

    p = np.asarray(x).reshape(B, 3, 7, 16, 7, 16).transpose(3, 5, 1, 0, 2, 4).reshape(HID, B, T - 1)
    full = np.zeros((HID, B, HALF), p.dtype)
    full[:, :, 1:T] = p
    np_["patches"] = np.ascontiguousarray(
        full.reshape(KC, P, CHUNKS, CW).transpose(2, 1, 0, 3))
    np_["w_tok"] = np.ascontiguousarray(np.asarray(L0_tok_W).T.reshape(KC, P, D).transpose(1, 0, 2))
    np_["cls"] = np.asarray(cls_tok).reshape(1, D)
    np_["V"] = groups(np.asarray(L0_attn_V_w).T)
    np_["U"] = np.ascontiguousarray(np.asarray(L0_attn_U_w).T)
    np_["E1"] = groups(np.asarray(L0_attn_E1_w).T, L0_attn_E1_b)
    np_["E2"] = np.ascontiguousarray(np.repeat(np.asarray(L0_attn_E2_w), D // 3, axis=0).T)
    np_["E2b"] = np.ascontiguousarray(np.repeat(np.asarray(L0_attn_E2_b), D // 3).reshape(2, FG).T)
    np_["a_base"] = np.ascontiguousarray(np.asarray(L0_attn_a_base).reshape(2, FG).T)
    np_["a_delta"] = np.ascontiguousarray(np.asarray(L0_attn_a_delta).reshape(2, FG).T)
    np_["C"] = groups(np.asarray(L0_attn_C_w).T)
    np_["G"] = groups(np.asarray(L0_attn_G_w).T, L0_attn_G_b)
    np_["Wg"] = groups(L0_ffn_Wg)
    np_["W1"] = np.stack([groups(w, b) for w, b in zip(np.asarray(L0_ffn_W1), np.asarray(L0_ffn_b1))])
    np_["W2"] = np.asarray(L0_ffn_W2).reshape(E, HC, P, D).transpose(0, 2, 1, 3).reshape(E, P, HC * D)
    np_["b2"] = np.asarray(L0_ffn_b2).reshape(E, 1, D)

    def complex_heads(re, im):
        both = np.stack([np.asarray(re).reshape(HEADS, DH, D), np.asarray(im).reshape(HEADS, DH, D)], 1)
        return groups(both.reshape(HEADS * 2 * DH, D).T)

    np_["Wq"] = complex_heads(L1_attn_Wqr, L1_attn_Wqi)
    np_["Wk"] = complex_heads(L1_attn_Wkr, L1_attn_Wki)
    order = [(n % HG) * 4 + n // HG for n in range(HEADS)]
    wv = np.asarray(L1_attn_Wv).reshape(HEADS, DH, D)[order[0::2] + order[1::2]]
    np_["Wv"] = groups(wv.reshape(D, D).T)
    np_["enc_w"] = groups(L1_ffn_enc_w)
    np_["enc_b"] = np.asarray(L1_ffn_enc_b).reshape(R1, 1)
    np_["sw"] = np.concatenate([np.asarray(L1_ffn_sw_w), np.asarray(L1_ffn_sw_b)[None]], 0)
    np_["s_w1"] = groups(np.asarray(L1_ffn_w1).transpose(1, 0, 2).reshape(D, E * R1))
    np_["s_b1"] = np.asarray(L1_ffn_b1)
    np_["s_w2"] = np.asarray(L1_ffn_w2).reshape(4, P, D).transpose(1, 0, 2)
    np_["s_b2"] = np.asarray(L1_ffn_b2)
    return np_


def kernel(**inputs):
    import numpy as _np
    import concourse.bacc as _bacc
    from concourse import mybir as _mybir
    from concourse.bass_utils import run_bass_kernel_spmd as _run

    nc = _bacc.Bacc("TRN2", target_bir_lowering=False, num_devices=1)
    laid = _layout(**inputs)
    arrays, A = {}, {}
    for name, a in laid.items():
        arrays[f"in_{name}"] = _np.ascontiguousarray(a)
        A[name] = nc.dram_tensor(f"in_{name}", a.shape, _mybir.dt.from_np(a.dtype), kind="ExternalInput").ap()
    out = nc.dram_tensor("out_0", (B * T, D), _mybir.dt.from_np(_np.dtype("float32")), kind="ExternalOutput").ap()
    build(nc, A, out)
    r = _run(nc, [arrays], core_ids=[0])
    return r.results[0]["out_0"].reshape(B, T, D)
```

```python
from contextlib import ExitStack

import concourse.bass as bass
from concourse import mybir

ALU = mybir.AluOpType
ACT = mybir.ActivationFunctionType
AX = mybir.AxisListType
F32 = mybir.dt.float32
I32 = mybir.dt.int32

P = 128
B, T, D = 32, 50, 192
FG = 96
HALF = 64
CB = 8
CT = CB * T
CW = CB * HALF
TILES = CB // 2
CHUNKS = B // CB
NT = B // 2
KC = 6
E = 8
HID = 768
HC = HID // P
RE = 64
R1 = 64
HEADS, DH = 12, 16
HG = 3
EPS = 1e-5
HW = 2 * T
VW = DH + 1
SCALE2 = 1.0 / DH
SLOTS = 14 * P
MOE_TILES = 2 * B * T // P + E - 1
TABLE = MOE_TILES + 4
MOST_TILES = SLOTS // P - 1
NULL_ROW = E * SLOTS
ROWS = NULL_ROW + P
SKIP = float(1 << 20)
SBUF_START = 16512
TIE = -2.0 ** -25
OFF = 1e18


def build(nc, A, out):
    with ExitStack() as ctx:
        here = [SBUF_START]

        def sb(name, shape, dt=F32):
            size = 4
            for n in shape[1:]:
                size *= n
            t = nc.alloc_sbuf_tensor_at(name, shape, dt, offset=here[0])
            here[0] += -(-size // 32) * 32
            return t

        def sem(name):
            return ctx.enter_context(nc.semaphore(name))

        def seqs(ap):
            return ap.rearrange("p (s t) -> p s t", t=HALF)[:, :, 0:T]

        def packed(ap):
            return ap.rearrange("p (s t) -> p s t", t=T)

        ps = ctx.enter_context(nc.psum_tensor("ps", [P, 8, 512], F32))

        w_tok = sb("w_tok", [P, KC, D])
        cls = sb("cls", [P, D])
        u_w = sb("u_w", [RE + 16, D])
        ev_w = sb("ev_w", [FG + 1, 2, RE + 16])
        e2_w = sb("e2_w", [64, D])
        e2_b = sb("e2_b", [FG, 2])
        a_base = sb("a_base", [FG, 2])
        a_delta = sb("a_delta", [FG, 2])
        tanh_delta = sb("tanh_delta", [FG, 2])
        half_e2_b = sb("half_e2_b", [FG, 2])
        lam_scale = sb("lam_scale", [FG, 2])
        lam_bias = sb("lam_bias", [FG, 2])
        lam_mid = sb("lam_mid", [FG, 2])
        c_w = sb("c_w", [FG, 2, D])
        g_w = sb("g_w", [FG + 1, 2, D])
        gate_w = sb("gate_w", [FG, 2, E])
        ident = sb("ident", [P, P])
        neg_half = sb("neg_half", [P, TILES])
        eps = sb("eps", [P, TILES])

        to_kk = sb("to_kk", [P, P])

        def two(name, shape, dt=F32):
            return [sb(f"{name}{u}", shape, dt) for u in range(2)]

        stats = two("stats", [P, TILES, 6])
        meanvar = two("meanvar", [P, TILES, 2])
        rstd = two("rstd", [P, TILES])
        x_tok = two("x_tok", [P, TILES, D])
        xT = two("xT", [FG + E, 2, CW])
        h = sb("h", [P, NT, D])
        ramp = sb("ramp", [P, TABLE])
        ramp_int = sb("ramp_int", [P, TABLE], I32)
        expert_rank = sb("expert_rank", [P, E])
        later = sb("later", [P, P])
        every = sb("every", [P, P])
        row_index_int = sb("row_index_int", [P, 1], I32)
        row_index = sb("row_index", [P, 1])
        in_first = sb("in_first", [P, 1])
        in_second = sb("in_second", [P, 1])
        valid = sb("valid", [P, 1])
        skip = sb("skip", [P, 1])
        region = sb("region", [P, E])
        next_row = sb("next_row", [P, E])
        r_max = two("r_max", [P, TILES])
        r_shift = two("r_shift", [P, TILES, E])
        r_exp = two("r_exp", [P, TILES, E])
        r_sum = two("r_sum", [P, TILES])
        best = two("best", [P, TILES])
        second_exp = two("second_exp", [P, TILES])
        rank = two("rank", [P, TILES, E])
        others = two("others", [P, TILES, E])
        chosen = two("chosen", [P, TILES + 1, E])
        row_of = two("row_of", [P, TILES, E])
        row_sum = two("row_sum", [P, 2, TILES])
        rows = two("rows", [P, 2, TILES], I32)
        all_first = sb("all_first", [P, NT, E])
        all_second = sb("all_second", [P, NT, E])
        all_rows = sb("all_rows", [P, 2, NT])
        row_move = sb("row_move", [P, 2, NT])
        moved = sb("moved", [P, E])
        y_sum = sb("y_sum", [P, 2, NT])
        y_rows = sb("y_rows", [P, 2, NT], I32)
        all_gates = sb("all_gates", [P, NT, 2])
        counts = sb("counts", [P, E])
        steps128 = sb("steps128", [P, MOST_TILES])
        n_tiles = sb("n_tiles", [P, E])
        ones_e = sb("ones_e", [P, E])
        tiles_to = sb("tiles_to", [P, E])
        tile_expert = sb("tile_expert", [P, TABLE])
        tiles_behind = sb("tiles_behind", [P, TABLE])
        live = sb("live", [P, TABLE])
        tile_row = sb("tile_row", [P, TABLE])
        load_row = sb("load_row", [P, TABLE])
        tile_expert_int = sb("tile_expert_int", [P, TABLE], I32)
        load_row_int = sb("load_row_int", [P, TABLE], I32)
        next_row_int = sb("next_row_int", [P, E], I32)
        zeros = sb("zeros", [P, D])
        shared = here[0]

        patches = two("patches", [P, KC, CW])
        h_plus_x = two("h_plus_x", [P, TILES, D])
        zT = two("zT", [RE + 16, CW])
        gelu_e = two("gelu_e", [64, CT])
        lam = two("lam", [FG, 2, CW])
        sT = two("sT", [FG, 2, CW])
        gelu_at = here[0]
        gelu_y = two("gelu_y", [P, TILES, D])
        tanh_g = two("tanh_g", [P, TILES, D])
        x2_tok = two("x2_tok", [P, TILES, D])
        experts_at = here[0]

        w1 = sb("w1", [FG + 1, E, 2, HID])
        w2 = sb("w2", [P, E, HC * D])
        b2 = sb("b2", [P, E, D])

        here[0] = gelu_at
        over = sb("over", [P, E, MOST_TILES])
        behind = sb("behind", [P, TABLE, E - 1])
        here[0] = shared
        wq = sb("wq", [FG, 2, HG * P])
        wk = sb("wk", [FG, 2, HG * P])
        wv = sb("wv", [FG, 2, D])
        enc_w = sb("enc_w", [FG, 2, R1])
        enc_b = sb("enc_b", [R1, 1])
        sw_w = sb("sw_w", [R1 + 1, E])
        s_w1 = sb("s_w1", [FG + E, 2, E * R1])
        s_w2 = sb("s_w2", [P, 4, D])
        s_b2 = sb("s_b2", [FG + E, D])
        assert here[0] <= shared + 2 * 4 * KC * CW
        tiles_at = here[0]
        xs = two("xs", [P, D])
        xsT = two("xsT", [FG + 1, 2, P])
        w1_now = two("w1_now", [FG + 1, 2, HID])
        hidT = two("hidT", [P, HC, P])
        ys = two("ys", [P, D])
        tiles_end = here[0]
        q = two("q", [P, HG, CW])
        vals = two("vals", [P, CB, HEADS // 2, 2, VW])
        xeT = two("xeT", [R1 + 1, CW])
        assert here[0] <= experts_at

        sc = two("sc", [P, TILES * HEADS, HALF])
        kk = two("kk", [P, HG, CB, 2, T])
        y_first = two("y_first", [P, TILES, D])
        y_second = two("y_second", [P, TILES, D])
        squares = two("squares", [P, HEADS, 2, T])
        sc_max = two("sc_max", [P, TILES * HEADS])
        probsT = two("probsT", [P, HEADS // 2, P])
        inv_sum = two("inv_sum", [P, HEADS])
        ctx_tok = two("ctx_tok", [P, TILES, D])
        s_logits = two("s_logits", [P, TILES, E])
        s_max = two("s_max", [P, TILES])
        s_exp = two("s_exp", [P, TILES, E])
        s_sum = two("s_sum", [P, TILES])
        s_prob = two("s_prob", [P, TILES])
        s_rank = two("s_rank", [P, TILES, E])
        s_best = two("s_best", [P, TILES])
        s_onehot = two("s_onehot", [P, TILES, E])
        here[0] = tiles_at
        s_hidT = two("s_hidT", [P, 4, CW])
        out_tok = two("out_tok", [P, TILES, D])
        assert here[0] <= tiles_end

        xs_dram = nc.dram_tensor("xs_dram", (ROWS, D), F32, kind="Internal").ap()
        ys_dram = nc.dram_tensor("ys_dram", (MOE_TILES * P, D), F32, kind="Internal").ap()

        first_load = sem("first_load")
        load = sem("load")
        cls_in = sem("cls_in")
        embedded = sem("embedded")
        ident_zero = sem("ident_zero")
        ident_done = sem("ident_done")
        cls_zero = sem("cls_zero")
        const_done = sem("const_done")
        pads_done = sem("pads_done")
        patches_in = [sem("patches_in0"), sem("patches_in1")]
        first_patches_in = sem("first_patches_in")
        patch_done = sem("patch_done")
        stats_done, var_done, eps_added, rstd_done, x_done, xT_in_psum, xT_done = (
            [sem(f"{name}{n}") for n in range(4)]
            for name in ("stats_done", "var_done", "eps_added", "rstd_done", "x_done", "xT_in_psum", "xT_done"))
        r_shifted = sem("r_shifted")
        r_exp_done = sem("r_exp_done")
        route_step = sem("route_step")
        second_done = sem("second_done")
        chosen_done = sem("chosen_done")
        ranks_in_psum = sem("ranks_in_psum")
        rows_done = sem("rows_done")
        off_done = sem("off_done")
        y_rows_done = sem("y_rows_done")
        ramp_copied = sem("ramp_copied")
        row_step = sem("row_step")
        xsT_ones = sem("xsT_ones")
        scattered = [sem("scattered0"), sem("scattered1")]
        null_zero = sem("null_zero")
        tails_zero = sem("tails_zero")
        act_tails_zero = sem("act_tails_zero")
        table_step = sem("table_step")
        table_done = sem("table_done")
        next_rows_done = sem("next_rows_done")
        ramp_done = sem("ramp_done")
        later_done = sem("later_done")
        rank_maps_done = sem("rank_maps_done")
        ones_done = sem("ones_done")
        w_in = sem("w_in")
        late_in = sem("late_in")
        xs_in = sem("xs_in")
        xsT_in_psum = sem("xsT_in_psum")
        xsT_done = sem("xsT_done")
        hid_in_psum = sem("hid_in_psum")
        w1_act_done = sem("w1_act_done")
        w1_dve_done = sem("w1_dve_done")
        hidT_act_done = sem("hidT_act_done")
        hidT_dve_done = sem("hidT_dve_done")
        ys_in_psum = sem("ys_in_psum")
        ys_done = sem("ys_done")
        ys_stored = sem("ys_stored")
        vals_zero = sem("vals_zero")
        gathered = [[sem(f"gathered_{name}{u}") for u in range(2)] for name in ("first", "second")]
        first_added = sem("first_added")
        moe_added = sem("moe_added")
        logits_in_psum = sem("logits_in_psum")
        late_const = sem("late_const")
        kk_map_zero = sem("kk_map_zero")
        kk_map_half = sem("kk_map_half")
        kk_map_done = sem("kk_map_done")
        q_in_psum = sem("q_in_psum")
        q_done = sem("q_done")
        k_in_psum = sem("k_in_psum")
        k_done = sem("k_done")
        v_in_psum = sem("v_in_psum")
        v_low_done = sem("v_low_done")
        v_high_done = sem("v_high_done")
        kk_in_psum = sem("kk_in_psum")
        kk_act_done = sem("kk_act_done")
        kk_dve_done = sem("kk_dve_done")
        scores_in_psum = sem("scores_in_psum")
        squares_done = sem("squares_done")
        sc2_done = sem("sc2_done")
        sc2_max_done = sem("sc2_max_done")
        sqrt_done = sem("sqrt_done")
        sqrt_max_done = sem("sqrt_max_done")
        sc_shifted = sem("sc_shifted")
        exp_done = sem("exp_done")
        pT_in_psum = sem("pT_in_psum")
        pT_act_done = sem("pT_act_done")
        pT_dve_done = sem("pT_dve_done")
        ctx_in_psum = sem("ctx_in_psum")
        inv_sum_done = sem("inv_sum_done")
        ctx_scaled = sem("ctx_scaled")
        attended = sem("attended")
        enc_in_psum = sem("enc_in_psum")
        enc_done = sem("enc_done")
        s_logits_in_psum = sem("s_logits_in_psum")
        s_max_done = sem("s_max_done")
        s_shifted = sem("s_shifted")
        s_exp_done = sem("s_exp_done")
        s_sum_done = sem("s_sum_done")
        s_prob_done = sem("s_prob_done")
        s_rank_done = sem("s_rank_done")
        s_best_done = sem("s_best_done")
        onehot_done = sem("onehot_done")
        onehotT_in_psum = sem("onehotT_in_psum")
        onehotT_done = sem("onehotT_done")
        s_hid_in_psum = sem("s_hid_in_psum")
        s_hid_done = sem("s_hid_done")
        s_out_in_psum = sem("s_out_in_psum")
        out_ready = sem("out_ready")
        hx_done = sem("hx_done")
        ze_done = sem("ze_done")
        zT_done = sem("zT_done")
        gelu_e_done = sem("gelu_e_done")
        bu_done = sem("bu_done")
        tanh_alpha_done = sem("tanh_alpha_done")
        tanh_lam_done = sem("tanh_lam_done")
        lam_done = sem("lam_done")
        lam_mid_done = sem("lam_mid_done")
        lam_coef_done = sem("lam_coef_done")
        scan_done = sem("scan_done")
        gate_in_psum = sem("gate_in_psum")
        y_in_psum = sem("y_in_psum")
        gelu_y_done = sem("gelu_y_done")
        tanh_g_done = sem("tanh_g_done")
        gated_done = sem("gated_done")
        h_done = sem("h_done")
        tanh_done = sem("tanh_done")
        out_done = sem("out_done")

        PAIRS = CHUNKS // 2
        STORED0, YS0, YSP0 = 16, 2, 2

        MOVES = 2 * TILES * 16
        ROUTE_STEPS, ROW_STEPS = 11, 5

        def repeat(ap, n):
            return bass.AP(ap.tensor, ap.offset, [list(ap.ap[0]), [0, n], *map(list, ap.ap[1:])])

        def count(cc, u):
            return 2 * cc + u + 1

        def chunk_of(buf, cc, u):
            return buf[:, bass.ds((2 * cc + u) * TILES, TILES), :]

        def tile_of(buf, cc, u, i):
            return buf[:, bass.ds((2 * cc + u) * TILES + i, 1), :].rearrange("p i d -> p (i d)")

        def spread(ap, n):
            return bass.AP(ap.tensor, ap.offset, [*map(list, ap.ap), [0, n]])

        loads = [
            (ev_w[:, :, :], A["EV"]), (u_w[RE:RE + 16, :], A["U"]),
            (e2_w[:, :], A["E2"]), (e2_b[:, :], A["E2b"]),
            (a_base[:, :], A["a_base"]), (a_delta[:, :], A["a_delta"]),
            (c_w[:, :, :], A["C"]), (g_w[:, :, :], A["G"]), (gate_w[:, :, :], A["Wg"]),
        ]
        late_loads = [
            (wq[:, :, :], A["Wq"]), (wk[:, :, :], A["Wk"]), (wv[:, :, :], A["Wv"]),
            (enc_w[:, :, :], A["enc_w"]), (enc_b[:, :], A["enc_b"]), (sw_w[:, :], A["sw"]),
            (s_w1[0:FG, :, :], A["s_w1"]), (s_w2[:, :, :], A["s_w2"]), (s_b2[FG:FG + E, :], A["s_b2"]),
        ]
        LOADED = 16 * len(loads)
        WEIGHTS = 3 * 16 * E
        LATE = 16 * (len(late_loads) + E)

        def tokv(slot, width=D):
            return ps[:, slot:slot + 2, 0:2 * width].rearrange("p b (i d) -> p b i d", i=2)

        def spread_tiles(ap):
            return bass.AP(ap.tensor, ap.offset, [list(ap.ap[0]), [0, 2], [0, 2], *map(list, ap.ap[1:])])

        def tok(buf):
            return buf[:, :, :].rearrange("p (b i) d -> p b i d", b=2)

        def zero_tails(engine, experts):
            engine.wait_ge(next_rows_done, 1)
            for e in experts:
                row = engine.value_load(next_row_int[0:1, e:e + 1], min_val=0, max_val=NULL_ROW - P)
                engine.dma_start(xs_dram[bass.ds(row, P), :], zeros[:, :]).then_inc(
                    tails_zero if experts[0] == 0 else act_tails_zero, 16)

        with nc.Block() as block:

            @block.sync
            def _(sp):
                def load_patches(c):
                    sp.dma_start(patches[c % 2][:, :, :], A["patches"][c]).then_inc(patches_in[c % 2], 16)

                def load_expert(e):
                    sp.dma_start(w1[:, e, :, :], A["W1"][e]).then_inc(w_in, 16)
                    sp.dma_start(w2[:, e, :], A["W2"][e]).then_inc(w_in, 16)
                    sp.dma_start(b2[:, e, :], A["b2"][e].to_broadcast([P, D])).then_inc(w_in, 16)

                sp.dma_start(w_tok[:, :, :], A["w_tok"]).then_inc(first_load, 16)
                for half in range(2):
                    sp.dma_start(patches[0][:, :, 2 * P * half:2 * P * half + 2 * P],
                                 A["patches"][0][:, :, 2 * P * half:2 * P * half + 2 * P]
                                 ).then_inc(patches_in[0] if half else first_patches_in, 16)
                sp.wait_ge(cls_zero, 1)
                for row in (0, HALF):
                    sp.dma_start(cls[row:row + 1, :], A["cls"]).then_inc(cls_in, 16)
                load_patches(1)
                for dst, src in loads:
                    sp.dma_start(dst, src).then_inc(load, 16)
                for e in range(E // 2):
                    load_expert(e)
                for c in range(2, CHUNKS):
                    sp.wait_ge(patch_done, c - 1)
                    load_patches(c)
                for e in range(E // 2, E):
                    load_expert(e)
                sp.wait_ge(const_done, 1)
                sp.dma_start(xs_dram[NULL_ROW:NULL_ROW + P, :], zeros[:, :]).then_inc(null_zero, 16)

                sp.wait_ge(patch_done, CHUNKS)
                for dst, src in late_loads:
                    sp.dma_start(dst, src).then_inc(late_in, 16)
                sp.wait_ge(off_done, 1)
                for e in range(E):
                    sp.dma_start(s_w1[FG + e:FG + e + 1, 1, R1 * e:R1 * e + R1], A["s_b1"][e:e + 1, :]).then_inc(late_in, 16)
                zero_tails(sp, range(E // 2))

                sp.wait_ge(table_done, 1)
                loads_of = [sp.value_load(load_row_int[0:1, v:v + 1], min_val=0, max_val=ROWS - P) for v in range(2)]
                sp.wait_ge(null_zero, 16)
                sp.wait_ge(tails_zero, 16 * (E // 2))
                sp.wait_ge(act_tails_zero, 16 * (E // 2))
                for u in range(2):
                    sp.wait_ge(scattered[u], MOVES * PAIRS)
                for v in range(2):
                    sp.dma_start(xs[v][:, :], xs_dram[bass.ds(loads_of[v], P), :]).then_inc(xs_in, 16)
                for v in range(2):
                    sp.wait_ge(xsT_in_psum, v + 1)
                    row = sp.value_load(load_row_int[0:1, v + 2:v + 3], min_val=0, max_val=ROWS - P)
                    sp.dma_start(xs[v][:, :], xs_dram[bass.ds(row, P), :]).then_inc(xs_in, 16)
                with sp.Fori(0, MOE_TILES // 2) as tt:
                    for v in range(2):
                        sp.wait_ge(xsT_in_psum, 2 * tt + v + 3)
                        row = sp.value_load(load_row_int[0:1, bass.ds(2 * tt + 4 + v, 1)], min_val=0, max_val=ROWS - P)
                        sp.dma_start(xs[v][:, :], xs_dram[bass.ds(row, P), :]).then_inc(xs_in, 16)
                    for v in range(2):
                        sp.wait_ge(ys_done, YS0 + 2 * tt + v + 1)
                        sp.dma_start(ys_dram[bass.ds((2 * tt + v) * P, P), :], ys[v][:, :]).then_inc(ys_stored, 16)
                sp.wait_ge(ys_stored, STORED0 + 16 * MOE_TILES)
                sp.wait_ge(w1_act_done, MOE_TILES + 2)
                sp.wait_ge(w1_dve_done, MOE_TILES + 2)
                sp.wait_ge(xs_in, 16 * TABLE)
                for c in range(CHUNKS):
                    sp.wait_ge(out_ready, c + 1)
                    for half in range(2):
                        sp.dma_start(
                            out[CT * c:CT * c + CT, :].rearrange("(i two t) d -> two t i d", two=2, t=T)[half],
                            out_tok[c % 2][HALF * half:HALF * half + T, :, :]).then_inc(out_done, 16)
                sp.wait_ge(out_done, 32 * CHUNKS)

            @block.gpsimd
            def _(pool):
                nc.gpsimd.memset(neg_half[:, :], -0.5)
                nc.gpsimd.memset(eps[:, :], EPS)
                nc.gpsimd.memset(ident[:, :], 0.0).then_inc(ident_zero, 1)
                pool.wait_ge(ident_zero, 1)
                nc.gpsimd.affine_select(out=ident[:, :], in_=ident[:, :], compare_op=ALU.not_equal, fill=1.0,
                                        base=0, pattern=[[-1, P]], channel_multiplier=1).then_inc(ident_done, 1)

                nc.gpsimd.iota(ramp_int[:, :], [[1, TABLE]], base=0, channel_multiplier=0).then_inc(ramp_done, 1)
                nc.gpsimd.iota(row_index_int[:, :], [[1, 1]], base=0, channel_multiplier=1).then_inc(ramp_done, 1)
                nc.gpsimd.memset(every[:, :], 1.0).then_inc(ones_done, 1)
                pool.wait_ge(ones_done, 1)
                nc.gpsimd.affine_select(out=later[:, :], in_=every[:, :], compare_op=ALU.is_gt, fill=0.0,
                                        base=0, pattern=[[1, P]], channel_multiplier=-1).then_inc(later_done, 1)
                halves = to_kk[:, :].rearrange("p (h two d) -> p h two d", h=4, two=2)
                nc.gpsimd.memset(to_kk[:, :], 0.0).then_inc(kk_map_zero, 1)
                pool.wait_ge(kk_map_zero, 1)
                nc.gpsimd.affine_select(out=halves[:, :, 0, :], in_=halves[:, :, 0, :], compare_op=ALU.not_equal,
                                        fill=-1.0, base=-DH, pattern=[[-2 * DH, 4], [-1, DH]],
                                        channel_multiplier=1).then_inc(kk_map_half, 1)
                pool.wait_ge(kk_map_half, 1)
                nc.gpsimd.affine_select(out=halves[:, :, 1, :], in_=halves[:, :, 1, :], compare_op=ALU.not_equal,
                                        fill=1.0, base=0, pattern=[[-2 * DH, 4], [-1, DH]],
                                        channel_multiplier=1).then_inc(kk_map_done, 1)

                def inverse_deviation(norm, u, n):
                    pool.wait_ge(var_done[norm], n)
                    nc.gpsimd.tensor_tensor(rstd[u][:, :], meanvar[u][:, :, 1], eps[:, :],
                                            ALU.add).then_inc(eps_added[norm], 1)
                    pool.wait_ge(eps_added[norm], n)
                    nc.gpsimd.tensor_tensor(rstd[u][:, :], rstd[u][:, :], neg_half[:, :],
                                            ALU.pow).then_inc(rstd_done[norm], 1)

                def scatter(u, tiles):
                    for i in tiles:
                        for k in range(2):
                            nc.gpsimd.indirect_dma_start(
                                out=xs_dram[:, :], out_offset=bass.IndirectOffsetOnAxis(ap=rows[u][:, k, i:i + 1], axis=0),
                                in_=x2_tok[u][:, i, :], in_offset=None, bounds_check=ROWS - 1,
                                oob_is_err=False).then_inc(scattered[u], 16)

                for u in range(2):
                    inverse_deviation(0, u, count(0, u))
                for pair in range(PAIRS):
                    for u in range(2):
                        inverse_deviation(1, u, count(pair, u))
                    if pair < PAIRS - 1:
                        inverse_deviation(0, 0, count(pair + 1, 0))
                    pool.wait_ge(rows_done, count(pair, 0))
                    scatter(0, range(TILES - 1))
                    if pair < PAIRS - 1:
                        inverse_deviation(0, 1, count(pair + 1, 1))
                    scatter(0, range(TILES - 1, TILES))
                    pool.wait_ge(rows_done, count(pair, 1))
                    scatter(1, range(TILES))
                for u in range(2):
                    pool.wait_ge(scattered[u], MOVES * PAIRS)
                pool.wait_ge(table_done, 1)
                for u in range(2):
                    nc.gpsimd.memset(q[u][:, :, :], 0.0)
                    last = nc.gpsimd.memset(vals[u][:, :, :, :, :], 0.0)
                last.then_inc(vals_zero, 1)

                def fetch(pair, u, k):
                    for i in range(TILES):
                        t = (2 * pair + u) * TILES + i
                        nc.gpsimd.indirect_dma_start(
                            out=(y_first, y_second)[k][u][:, i, :], out_offset=None, in_=ys_dram[:, :],
                            in_offset=bass.IndirectOffsetOnAxis(ap=y_rows[:, k, t:t + 1], axis=0),
                            bounds_check=MOE_TILES * P - 1, oob_is_err=False).then_inc(gathered[k][u], 16)

                pool.wait_ge(y_rows_done, 1)
                pool.wait_ge(ys_stored, STORED0 + 16 * MOE_TILES)
                pool.wait_ge(w1_act_done, MOE_TILES + 2)
                pool.wait_ge(w1_dve_done, MOE_TILES + 2)
                fetch(0, 0, 0)
                fetch(0, 0, 1)
                fetch(0, 1, 0)
                for pair in range(PAIRS):
                    inverse_deviation(2, 0, count(pair, 0))
                    if pair == 0:
                        fetch(0, 1, 1)
                    inverse_deviation(2, 1, count(pair, 1))
                    if pair < PAIRS - 1:
                        for u in range(2):
                            pool.wait_ge(moe_added, count(pair, u))
                            fetch(pair + 1, u, 0)
                            fetch(pair + 1, u, 1)
                    for u in range(2):
                        inverse_deviation(3, u, count(pair, u))

            @block.tensor
            def _(pe):
                def turn(norm, u, banks, n):
                    pe.wait_ge(x_done[norm], n)
                    for g in range(2):
                        for i in range(TILES):
                            mm = pe.transpose(ps[0:FG, banks + g, P * i:P * i + P],
                                              (x2_tok if norm == 1 else x_tok)[u][:, i, FG * g:FG * g + FG],
                                              ident[:, :])
                        mm.then_inc(xT_in_psum[norm], 1)

                def group_there(norm, n, g):
                    pe.wait_ge(xT_done[norm], 2 * n - 1 + g)

                pe.wait_ge(first_load, 16)
                X = [0, 4]
                Y = [2, 6]

                def embed(pair, u, tiles=range(TILES)):
                    if pair or u:
                        pe.wait_ge(patches_in[u], 16 * pair + 16)
                    else:
                        pe.wait_ge(first_patches_in, 16)
                    if pair:
                        pe.wait_ge(tanh_g_done, count(pair - 1, u))
                    for i in tiles:
                        dst = tokv(X[u])[:, i // 2, i % 2, :]
                        if pair == u == 0 and i == 2:
                            pe.wait_ge(patches_in[0], 16)
                        for k in range(KC):
                            mm = pe.matmul(dst, patches[u][:, k, P * i:P * i + P], w_tok[:, k, :], start=(k == 0),
                                           stop=(k == KC - 1))
                    if TILES - 1 in tiles:
                        mm.then_inc(patch_done, 1)

                def rank_choices(pair, u):
                    dst = ps[:, Y[u], 64:64 + (TILES + 1) * E]
                    pe.wait_ge(chosen_done, count(pair, u))
                    pe.matmul(dst, later[:, :], chosen[u][:, :, :].rearrange("p i e -> p (i e)"), start=True, stop=False)
                    for n in range(1, TILES + 1):
                        mm = pe.matmul(dst[:, E * n:], every[:, :],
                                       chosen[u][:, 0:TILES + 1 - n, :].rearrange("p i e -> p (i e)"),
                                       start=False, stop=(n == TILES))
                    mm.then_inc(ranks_in_psum, 1)

                for u in range(2):
                    embed(0, u)
                pe.wait_ge(ident_done, 1)
                pe.wait_ge(pads_done, 1)
                pe.wait_ge(load, LOADED)
                pe.wait_ge(rank_maps_done, 1)
                for cc in range(PAIRS):
                    for u in range(2):
                        if cc:
                            pe.wait_ge(rows_done, count(cc - 1, u))
                        turn(0, u, Y[u], count(cc, u))
                        pe.wait_ge(embedded, count(cc, u))
                        for g in range(2):
                            group_there(0, count(cc, u), g)
                            k = FG + g
                            mm = pe.matmul(ps[0:RE + 16, X[u], 0:CT], ev_w[0:k, g, :], seqs(xT[u][0:k, g, :]),
                                           start=(g == 0), stop=(g == 1))
                        mm.then_inc(ze_done, 1)
                        pe.wait_ge(zT_done, 2 * cc + u + 1)
                        for g in range(2):
                            pe.matmul(ps[0:FG, Y[u] + g, :], u_w[RE:RE + 16, FG * g:FG * g + FG], zT[u][RE:RE + 16, :],
                                      start=True, stop=True)
                        pe.wait_ge(gelu_e_done, 2 * cc + u + 1)
                        for g in range(2):
                            mm = pe.matmul(ps[0:FG, X[u] + g, 0:CT], e2_w[:, FG * g:FG * g + FG], gelu_e[u][:, :],
                                           start=True, stop=True)
                        mm.then_inc(bu_done, 1)
                    for u in range(2):
                        pe.wait_ge(tanh_alpha_done, 2 * cc + u + 1)
                        for i in range(TILES):
                            for g in range(2):
                                mm = pe.matmul(tokv(X[u])[:, i // 2, i % 2, :],
                                               xT[u][0:FG + g, g, P * i:P * i + P], g_w[0:FG + g, g, :],
                                               start=(g == 0), stop=(g == 1))
                        mm.then_inc(gate_in_psum, 1)
                        pe.wait_ge(scan_done, 2 * cc + u + 1)
                        for i in range(TILES):
                            for g in range(2):
                                mm = pe.matmul(tokv(Y[u])[:, i // 2, i % 2, :],
                                               sT[u][:, g, P * i:P * i + P], c_w[:, g, :],
                                               start=(g == 0), stop=(g == 1))
                        mm.then_inc(y_in_psum, 1)

                    if cc < PAIRS - 1:
                        embed(cc + 1, 0)
                    for u in range(2):
                        pe.wait_ge(gelu_y_done, count(cc, u))
                        turn(1, u, Y[u], count(cc, u))
                        if u == 1 and cc == PAIRS - 1:
                            rank_choices(cc, 0)
                        for i in range(TILES):
                            for g in range(2):
                                if i == 0:
                                    group_there(1, count(cc, u), g)
                                mm = pe.matmul(ps[:, Y[u], E * i:E * i + E], xT[u][0:FG, g, P * i:P * i + P],
                                               gate_w[:, g, :], start=(g == 0), stop=(g == 1))
                        mm.then_inc(logits_in_psum, 1)
                    if cc < PAIRS - 1:
                        rank_choices(cc, 0)
                        embed(cc + 1, 1, range(TILES // 2))
                        rank_choices(cc, 1)
                        embed(cc + 1, 1, range(TILES // 2, TILES))
                    else:
                        rank_choices(cc, 1)

                def turn_rows(v, n):
                    pe.wait_ge(xs_in, 16 * n)
                    for g in range(2):
                        mm = pe.transpose(ps[0:FG, 2 * v, P * g:P * g + P], xs[v][:, FG * g:FG * g + FG], ident[:, :])
                    mm.then_inc(xsT_in_psum, 1)

                pe.wait_ge(w_in, WEIGHTS)
                pe.wait_ge(xsT_ones, 1)
                pe.wait_ge(table_done, 1)
                for v in range(2):
                    turn_rows(v, 2)
                with pe.Fori(0, MOE_TILES // 2) as tt:
                    experts = [pe.value_load(tile_expert_int[0:1, bass.ds(2 * tt + v, 1)], min_val=0, max_val=E - 1)
                               for v in range(2)]
                    for v in range(2):
                        pe.wait_ge(xsT_done, 2 * tt + v + 1)
                        pe.wait_ge(w1_act_done, 2 * tt + v + 1)
                        pe.wait_ge(w1_dve_done, 2 * tt + v + 1)
                        for m in range(HC):
                            for g in range(2):
                                k = FG + g
                                mm = pe.matmul(ps[:, 4 + 2 * v + m // 3, P * (m % 3):P * (m % 3) + P],
                                               w1_now[v][0:k, g, P * m:P * m + P], xsT[v][0:k, g, :],
                                               start=(g == 0), stop=(g == 1))
                        mm.then_inc(hid_in_psum, 1)
                    for v in range(2):
                        turn_rows(v, 2 * tt + 4)
                    for v in range(2):
                        pe.wait_ge(hidT_act_done, 2 * tt + v + 1)
                        pe.wait_ge(ys_done, 2 * tt + v + 1)
                        for m in range(HC):
                            if m == HC // 2:
                                pe.wait_ge(hidT_dve_done, 2 * tt + v + 1)
                            mm = pe.matmul(ps[:, 2 * v + 1, 0:D], hidT[v][:, m, :],
                                           w2[:, bass.ds(experts[v], 1), D * m:D * m + D].rearrange("p e n -> p (e n)"),
                                           start=(m == 0), stop=(m == HC - 1))
                        mm.then_inc(ys_in_psum, 1)

                pe.wait_ge(kk_map_done, 1)
                pe.wait_ge(late_const, 1)
                pe.wait_ge(late_in, LATE)
                pe.wait_ge(xsT_done, MOE_TILES + 2)
                pe.wait_ge(ys_done, YS0 + MOE_TILES)
                W = [0, 4]
                for cc in range(PAIRS):
                    def normed(u):
                        if cc:
                            pe.wait_ge(out_ready, count(cc - 1, u))
                        turn(2, u, W[u], count(cc, u))

                    def queries_keys(u):
                        for j in range(HG):
                            for bank, w, read, done, there in ((2, wq, 0, q_done, q_in_psum),
                                                               (3, wk, 1, k_done, k_in_psum)):
                                if j == 2:
                                    pe.wait_ge(done, 3 * (2 * cc + u) + 1)
                                for g in range(2):
                                    if j == 0 and w is wq:
                                        group_there(2, count(cc, u), g)
                                    mm = pe.matmul(ps[:, W[u] + (bank if j != 1 else read), 0:CT],
                                                   w[:, g, P * j:P * j + P], seqs(xT[u][0:FG, g, :]),
                                                   start=(g == 0), stop=(g == 1))
                                mm.then_inc(there, 1)

                    def values(u):
                        pe.wait_ge(q_done, 3 * (2 * cc + u) + 2)
                        pe.wait_ge(k_done, 3 * (2 * cc + u) + 2)
                        for s_ in range(CB):
                            for odd in range(2):
                                for g in range(2):
                                    mm = pe.matmul(ps[HALF * odd:HALF * odd + HALF, W[u] + s_ // 4,
                                                      FG * (s_ % 4):FG * (s_ % 4) + FG],
                                                   xT[u][0:FG, g, HALF * s_:HALF * s_ + HALF],
                                                   wv[:, g, FG * odd:FG * odd + FG], start=(g == 0), stop=(g == 1))
                        mm.then_inc(v_in_psum, 1)

                    def mapped_keys(u):
                        pe.wait_ge(q_done, 3 * (2 * cc + u) + 3)
                        pe.wait_ge(k_done, 3 * (2 * cc + u) + 3)
                        for j in range(HG):
                            if j == 2:
                                pe.wait_ge(v_low_done, count(cc, u))
                                pe.wait_ge(v_high_done, count(cc, u))
                            mm = pe.matmul(ps[:, W[u] + (2, 3, 0)[j], 0:CT], to_kk[:, :], kk[u][:, j, :, 0, :],
                                           start=True, stop=True).then_inc(kk_in_psum, 1)

                    def scores(t):
                        u, i = divmod(t, TILES)
                        if t < 2:
                            pe.wait_ge(kk_act_done, 2 * count(cc, t))
                            pe.wait_ge(kk_dve_done, count(cc, t))
                        else:
                            pe.wait_ge(squares_done, 8 * cc + t - 1)
                        for b in range(2):
                            for j in range(HG):
                                for r in range(4):
                                    mm = pe.matmul(ps[HALF * b:HALF * b + HALF, W[t % 2] + r, HW * j:HW * j + HW],
                                                   q[u][32 * r:32 * r + 32, j, P * i + HALF * b:P * i + HALF * b + HALF],
                                                   kk[u][32 * r:32 * r + 32, j, 2 * i + b, :, :],
                                                   start=True, stop=True)
                        mm.then_inc(scores_in_psum, 1)

                    normed(0)
                    queries_keys(0)
                    values(0)
                    normed(1)
                    mapped_keys(0)
                    queries_keys(1)
                    values(1)
                    mapped_keys(1)
                    for t in range(2 * TILES):
                        scores(t)
                    for t in range(2 * TILES + 1):
                        if t < 2 * TILES:
                            u, i = divmod(t, TILES)
                            if i == 0:
                                pe.wait_ge(exp_done, count(cc, u))
                            if t < 2:
                                pe.wait_ge(squares_done, 8 * cc + 7 + t)
                            else:
                                pe.wait_ge(pT_act_done, 8 * cc + t - 1)
                                pe.wait_ge(pT_dve_done, 8 * cc + t - 1)
                            for pr in range(HEADS // 2):
                                h0 = HEADS * i + 2 * pr
                                mm = pe.transpose(ps[:, W[t % 2] + pr // 3, P * (pr % 3):P * (pr % 3) + P],
                                                  sc[u][:, h0:h0 + 2, :].rearrange("p h k -> p (h k)"), ident[:, :])
                            mm.then_inc(pT_in_psum, 1)
                        if t >= 1:
                            u, i = divmod(t - 1, TILES)
                            slot = (t - 1) % 2
                            pe.wait_ge(pT_act_done, 8 * cc + t)
                            pe.wait_ge(pT_dve_done, 8 * cc + t)
                            if t >= 3:
                                pe.wait_ge(ctx_scaled, 8 * cc + t - 2)
                            for b in range(2):
                                for pr in range(HEADS // 2):
                                    mm = pe.matmul(ps[HALF * b:HALF * b + HALF, W[slot] + 2, 2 * VW * pr:2 * VW * pr + 2 * VW],
                                                   probsT[slot][:, pr, HALF * b:HALF * b + HALF],
                                                   vals[u][:, 2 * i + b, pr, :, :], start=True, stop=True)
                            mm.then_inc(ctx_in_psum, 1)
                    def hidden(u, g, parts):
                        k = FG + E * g
                        for m in parts:
                            mm = pe.matmul(ps[:, W[u] + m, 0:CT], s_w1[0:k, g, P * m:P * m + P],
                                           seqs(xT[u][0:k, g, :]), start=(g == 0), stop=(g == 1))
                        return mm

                    for u in range(2):
                        turn(3, u, W[u], count(cc, u))
                        pe.wait_ge(ctx_scaled, 8 * cc + 7 + u)
                        for g in range(2):
                            group_there(3, count(cc, u), g)
                            mm = pe.matmul(ps[0:R1, W[u] + 2, 0:CT], enc_w[:, g, :], seqs(xT[u][0:FG, g, :]),
                                           start=(g == 0), stop=(g == 1))
                        mm.then_inc(enc_in_psum, 1)
                        if u == 0:
                            hidden(0, 0, range(2))

                    for u in range(2):
                        pe.wait_ge(enc_done, count(cc, u))
                        for i in range(TILES):
                            mm = pe.matmul(ps[:, W[u] + 3, E * i:E * i + E], xeT[u][:, P * i:P * i + P], sw_w[:, :],
                                           start=True, stop=True)
                        mm.then_inc(s_logits_in_psum, 1)
                        hidden(1, 0, [u])
                    for u in range(2):
                        pe.wait_ge(onehot_done, count(cc, u))
                        for i in range(TILES):
                            mm = pe.matmul(ps[FG:FG + E, W[u] + 2, P * i:P * i + P], s_onehot[u][:, i, :], ident[:, :],
                                           start=True, stop=True)
                        mm.then_inc(onehotT_in_psum, 1)
                    for u in range(2):
                        pe.wait_ge(onehotT_done, count(cc, u))
                        for m in range(4):
                            if m >= 2:
                                hidden(u, 0, [m])
                            hidden(u, 1, [m]).then_inc(s_hid_in_psum, 1)
                    for u in range(2):
                        pe.wait_ge(s_hid_done, 4 * (2 * cc + u) + 4)
                        for i in range(TILES):
                            dst = tokv(W[u])[:, i // 2, i % 2, :]
                            for m in range(4):
                                pe.matmul(dst, s_hidT[u][:, m, P * i:P * i + P], s_w2[:, m, :], start=(m == 0), stop=False)
                            mm = pe.matmul(dst, xT[u][FG:FG + E, 1, P * i:P * i + P], s_b2[FG:FG + E, :],
                                           start=False, stop=True)
                        mm.then_inc(s_out_in_psum, 1)

            @block.scalar
            def _(act):
                act.wait_ge(load, LOADED)
                act.wait_ge(pads_done, 1)
                nc.scalar.activation(tanh_delta[:, :], a_delta[:, :], ACT.Tanh).then_inc(tanh_done, 1)
                act.wait_ge(lam_coef_done, 3)

                def turned(norm, u, banks, n):
                    for g in range(2):
                        act.wait_ge(xT_in_psum[norm], 2 * n - 1 + g)
                        nc.scalar.copy(seqs(xT[u][0:FG, g, :]), seqs(ps[0:FG, banks + g, :])).then_inc(xT_done[norm], 1)

                X = [0, 4]
                Y = [2, 6]
                for cc in range(PAIRS):
                    for u in range(2):
                        turned(0, u, Y[u], count(cc, u))
                        act.wait_ge(ze_done, 2 * cc + u + 1)
                        nc.scalar.copy(seqs(zT[u][RE:RE + 16, :]), packed(ps[RE:RE + 16, X[u], 0:CT])).then_inc(zT_done, 1)
                        nc.scalar.activation(gelu_e[u][:, :], ps[0:RE, X[u], 0:CT],
                                             ACT.Gelu).then_inc(gelu_e_done, 1)
                    for u in range(2):
                        act.wait_ge(bu_done, 2 * cc + u + 1)
                        for g in range(2):
                            last = nc.scalar.activation(seqs(lam[u][:, g, :]), packed(ps[0:FG, X[u] + g, 0:CT]),
                                                        ACT.Tanh, bias=half_e2_b[:, g:g + 1], scale=0.5)
                        last.then_inc(tanh_alpha_done, 1)
                        act.wait_ge(tanh_alpha_done, 2 * cc + u + 1)
                        for g in range(2):
                            last = nc.scalar.activation(seqs(lam[u][:, g, :]), seqs(lam[u][:, g, :]),
                                                        ACT.Tanh, bias=lam_bias[:, g:g + 1],
                                                        scale=lam_scale[:, g:g + 1])
                        last.then_inc(tanh_lam_done, 1)
                    for u in range(2):
                        act.wait_ge(gate_in_psum, 2 * cc + u + 1)
                        nc.scalar.activation(tok(tanh_g[u]), tokv(X[u]), ACT.Tanh,
                                             scale=0.5).then_inc(tanh_g_done, 1)
                        act.wait_ge(y_in_psum, 2 * cc + u + 1)
                        nc.scalar.activation(tok(gelu_y[u]), tokv(Y[u]), ACT.Gelu).then_inc(gelu_y_done, 1)

                    for u in range(2):
                        turned(1, u, Y[u], count(cc, u))
                        act.wait_ge(r_shifted, count(cc, u))
                        nc.scalar.activation(r_exp[u][:, :, :], r_shift[u][:, :, :], ACT.Exp).then_inc(r_exp_done, 1)

                def rows_turned(v, n):
                    act.wait_ge(xsT_in_psum, n)
                    nc.scalar.copy(xsT[v][0:FG, :, :], ps[0:FG, 2 * v, 0:2 * P].rearrange("p (g t) -> p g t", g=2)
                                   ).then_inc(xsT_done, 1)

                def next_w1(v, tile):
                    e = act.value_load(tile_expert_int[0:1, tile], min_val=0, max_val=E - 1)
                    nc.scalar.copy(w1_now[v][0:FG, 0, :], w1[0:FG, bass.ds(e, 1), 0, :].rearrange("p e n -> p (e n)")
                                   ).then_inc(w1_act_done, 1)

                zero_tails(act, range(E // 2, E))
                act.wait_ge(w_in, WEIGHTS)
                act.wait_ge(table_done, 1)
                act.wait_ge(xsT_ones, 1)
                for v in range(2):
                    next_w1(v, slice(v, v + 1))
                for v in range(2):
                    rows_turned(v, v + 1)
                with act.Fori(0, MOE_TILES // 2) as tt:
                    for v in range(2):
                        act.wait_ge(ys_in_psum, YSP0 + 2 * tt + v - 1)
                        act.wait_ge(hid_in_psum, 2 * tt + v + 1)
                        nc.scalar.activation(hidT[v][:, 0:3, :],
                                             ps[:, 4 + 2 * v, 0:3 * P].rearrange("p (m t) -> p m t", m=3),
                                             ACT.Relu).then_inc(hidT_act_done, 1)
                        next_w1(v, bass.ds(2 * tt + 2 + v, 1))
                    for v in range(2):
                        rows_turned(v, 2 * tt + v + 3)
                act.wait_ge(late_const, 1)
                W = [0, 4]
                for cc in range(PAIRS):
                    def queries(u):
                        for j in range(HG):
                            act.wait_ge(q_in_psum, 3 * (2 * cc + u) + j + 1)
                            nc.scalar.copy(seqs(q[u][:, j, :]), packed(ps[:, W[u] + (2, 0, 2)[j], 0:CT])
                                           ).then_inc(q_done, 1)

                    def low_values(u):
                        act.wait_ge(v_in_psum, count(cc, u))
                        for bank in range(2):
                            last = nc.scalar.copy(
                                vals[u][0:HALF, 4 * bank:4 * bank + 4, :, 0, 0:DH],
                                ps[0:HALF, W[u] + bank, 0:4 * FG].rearrange("p (s h d) -> p s h d", s=4, d=DH))
                        last.then_inc(v_low_done, 1)

                    def mapped_keys(u):
                        for j in (0, 2):
                            act.wait_ge(kk_in_psum, 3 * (2 * cc + u) + j + 1)
                            nc.scalar.copy(kk[u][:, j, :, 1, :], packed(ps[:, W[u] + (2, 3, 0)[j], 0:CT])
                                           ).then_inc(kk_act_done, 1)

                    def square(t):
                        act.wait_ge(scores_in_psum, 8 * cc + t + 1)
                        if t >= 2:
                            act.wait_ge(sc2_done, 8 * cc + t - 1)
                        nc.scalar.activation(squares[t % 2][:, :, :, :].rearrange("p (r j) c k -> p r (j c k)", r=4),
                                             ps[:, W[t % 2]:W[t % 2] + 4, 0:HG * HW], ACT.Square).then_inc(squares_done, 1)

                    def root(u):
                        act.wait_ge(sc2_max_done, 8 * cc + 4 * u + 4)
                        nc.scalar.activation(sc[u][:, :, 0:T], sc[u][:, :, 0:T], ACT.Sqrt,
                                             scale=SCALE2).then_inc(sqrt_done, 1)
                        nc.scalar.activation(sc_max[u][:, :], sc_max[u][:, :], ACT.Sqrt,
                                             scale=SCALE2).then_inc(sqrt_max_done, 1)

                    def weights(u):
                        act.wait_ge(sc_shifted, count(cc, u))
                        nc.scalar.activation(sc[u][:, :, 0:T], sc[u][:, :, 0:T], ACT.Exp).then_inc(exp_done, 1)

                    def turned_weights(t):
                        act.wait_ge(pT_in_psum, 8 * cc + t + 1)
                        if t >= 2:
                            act.wait_ge(ctx_in_psum, 8 * cc + t - 1)
                        nc.scalar.copy(probsT[t % 2][:, 0:3, :], ps[:, W[t % 2], 0:3 * P]).then_inc(pT_act_done, 1)

                    turned(2, 0, W[0], count(cc, 0))
                    queries(0)
                    low_values(0)
                    turned(2, 1, W[1], count(cc, 1))
                    mapped_keys(0)
                    queries(1)
                    low_values(1)
                    mapped_keys(1)
                    for t in range(6):
                        square(t)
                    root(0)
                    square(6)
                    weights(0)
                    square(7)
                    turned_weights(0)
                    root(1)
                    turned_weights(1)
                    turned_weights(2)
                    weights(1)
                    for t in range(3, 2 * TILES):
                        turned_weights(t)
                    for u in range(2):
                        turned(3, u, W[u], count(cc, u))
                        act.wait_ge(enc_in_psum, count(cc, u))
                        nc.scalar.activation(seqs(xeT[u][0:R1, :]), packed(ps[0:R1, W[u] + 2, 0:CT]), ACT.Identity,
                                             bias=enc_b[:, 0:1]).then_inc(enc_done, 1)
                    for u in range(2):
                        act.wait_ge(s_shifted, count(cc, u))
                        nc.scalar.activation(s_exp[u][:, :, :], s_logits[u][:, :, :], ACT.Exp).then_inc(s_exp_done, 1)
                    for u in range(2):
                        act.wait_ge(onehotT_in_psum, count(cc, u))
                        nc.scalar.copy(xT[u][FG:FG + E, 1, :], ps[FG:FG + E, W[u] + 2, :]).then_inc(onehotT_done, 1)
                    for u in range(2):
                        for m in range(4):
                            act.wait_ge(s_hid_in_psum, 4 * (2 * cc + u) + m + 1)
                            nc.scalar.activation(seqs(s_hidT[u][:, m, :]), packed(ps[:, W[u] + m, 0:CT]),
                                                 ACT.Gelu).then_inc(s_hid_done, 1)

            @block.vector
            def _(dve):
                X = [0, 4]
                Y = [2, 6]
                nc.vector.memset(cls[:, :], 0.0).then_inc(cls_zero, 1)
                for u in range(2):
                    nc.vector.memset(lam[u][:, :, :], 0.0)
                    nc.vector.memset(zT[u][RE:RE + 16, :], 0.0)
                    nc.vector.memset(xT[u][0:FG, :, :], 0.0)
                    last = nc.vector.memset(xT[u][FG:FG + 1, :, :], 1.0)
                last.then_inc(pads_done, 1)
                nc.vector.memset(zeros[:, :], 0.0)
                nc.vector.memset(ones_e[:, :], 1.0)
                dve.wait_ge(ramp_done, 2)
                nc.vector.tensor_copy(row_index[:, :], row_index_int[:, :])
                nc.vector.tensor_copy(ramp[:, :], ramp_int[:, :]).then_inc(ramp_copied, 1)
                dve.wait_ge(ramp_copied, 1)
                nc.vector.tensor_scalar(in_first[:, :], row_index[:, :], float(T), None, ALU.is_lt)
                nc.vector.tensor_scalar(in_second[:, :], row_index[:, :], float(HALF), None, ALU.is_ge).then_inc(ramp_copied, 1)
                dve.wait_ge(ramp_copied, 2)
                nc.vector.scalar_tensor_tensor(in_second[:, :], row_index[:, :], float(HALF + T), in_second[:, :],
                                               ALU.is_lt, ALU.mult).then_inc(ramp_copied, 1)
                dve.wait_ge(ramp_copied, 3)
                nc.vector.tensor_tensor(valid[:, :], in_first[:, :], in_second[:, :], ALU.add).then_inc(ramp_copied, 1)
                dve.wait_ge(ramp_copied, 4)
                nc.vector.tensor_scalar(skip[:, :], valid[:, :], -SKIP, SKIP, ALU.mult, ALU.add)
                nc.vector.tensor_scalar(expert_rank[:, :], ramp[:, 0:E], -1.0, float(E), ALU.mult, ALU.add)
                nc.vector.tensor_scalar(steps128[:, :], ramp[:, 0:MOST_TILES], float(P), None, ALU.mult)
                nc.vector.tensor_scalar(region[:, :], ramp[:, 0:E], float(SLOTS), None, ALU.mult)
                nc.vector.tensor_scalar(next_row[:, :], ramp[:, 0:E], float(SLOTS), None, ALU.mult)
                for u in range(2):
                    last = nc.vector.memset(chosen[u][:, TILES, :], 0.0)
                last.then_inc(const_done, 1)
                dve.wait_ge(later_done, 1)
                nc.vector.tensor_scalar(every[:, :], every[:, :], valid[:, 0:1], None, ALU.mult)
                nc.vector.tensor_scalar(later[:, :], later[:, :], valid[:, 0:1], None, ALU.mult).then_inc(rank_maps_done, 1)
                for started, at in ((ys_stored, STORED0), (ys_done, YS0),
                                    (ys_in_psum, YSP0)):
                    dve.sem_inc(started, at)
                dve.wait_ge(load, LOADED)
                nc.vector.tensor_scalar(half_e2_b[:, :], e2_b[:, :], 0.5, None, ALU.mult).then_inc(lam_coef_done, 1)
                dve.wait_ge(tanh_done, 1)
                nc.vector.tensor_scalar(lam_scale[:, :], tanh_delta[:, :], 0.25, None, ALU.mult).then_inc(lam_coef_done, 1)
                nc.vector.scalar_tensor_tensor(lam_mid[:, :], tanh_delta[:, :], 0.5, a_base[:, :], ALU.mult,
                                               ALU.add).then_inc(lam_mid_done, 1)
                dve.wait_ge(lam_mid_done, 1)
                nc.vector.tensor_scalar(lam_bias[:, :], lam_mid[:, :], 0.5, None, ALU.mult).then_inc(lam_coef_done, 1)

                def norm_stats(norm, u, src, n):
                    for i in range(TILES):
                        last = nc.vector.bn_stats(stats[u][:, i, :], src(i))
                    last.then_inc(stats_done[norm], 1)
                    dve.wait_ge(stats_done[norm], n)
                    for i in range(TILES):
                        last = nc.vector.bn_aggr(meanvar[u][:, i, :], stats[u][:, i, :])
                    last.then_inc(var_done[norm], 1)

                def norm_apply(norm, u, src, n):
                    dve.wait_ge(rstd_done[norm], n)
                    for i in range(TILES):
                        last = nc.vector.tensor_scalar((x2_tok if norm == 1 else x_tok)[u][:, i, :], src(i),
                                                       meanvar[u][:, i, 0:1], rstd[u][:, i:i + 1],
                                                       ALU.subtract, ALU.mult)
                    last.then_inc(x_done[norm], 1)

                def embedded_norm(pair, u):
                    n = count(pair, u)

                    def src(i):
                        return h_plus_x[u][:, i, :]

                    dve.wait_ge(patch_done, n)
                    nc.vector.tensor_tensor(tok(h_plus_x[u]), tokv(X[u]), spread_tiles(cls[:, :]),
                                            ALU.add).then_inc(embedded, 1)
                    dve.wait_ge(embedded, n)
                    norm_stats(0, u, src, n)
                    norm_apply(0, u, src, n)
                    dve.wait_ge(x_done[0], n)
                    nc.vector.tensor_tensor(h_plus_x[u][:, :, :], h_plus_x[u][:, :, :], x_tok[u][:, :, :],
                                            ALU.add).then_inc(hx_done, 1)

                dve.wait_ge(cls_in, 32)
                for u in range(2):
                    embedded_norm(0, u)
                for cc in range(PAIRS):
                    if cc == PAIRS - 1:
                        nc.vector.memset(s_w1[FG:FG + E, 1, :], -OFF).then_inc(off_done, 1)
                    for u in range(2):
                        n = 2 * cc + u + 1
                        dve.wait_ge(tanh_lam_done, n)
                        for g in range(2):
                            last = nc.vector.tensor_scalar(seqs(lam[u][:, g, :]), seqs(lam[u][:, g, :]), 0.5, 0.5,
                                                           ALU.mult, ALU.add)
                        last.then_inc(lam_done, 1)
                        dve.wait_ge(lam_done, n)
                        dve.wait_ge(bu_done, n)
                        for g in range(2):
                            last = nc.vector.tensor_tensor_scan(sT[u][:, g, :], lam[u][:, g, :], ps[0:FG, Y[u] + g, :],
                                                                0.0, ALU.mult, ALU.add)
                        last.then_inc(scan_done, 1)
                    for u in range(2):
                        n = 2 * cc + u + 1
                        dve.wait_ge(gelu_y_done, n)
                        dve.wait_ge(tanh_g_done, n)
                        nc.vector.scalar_tensor_tensor(gelu_y[u][:, :, :], tanh_g[u][:, :, :], 1.0, gelu_y[u][:, :, :],
                                                       ALU.add, ALU.mult).then_inc(gated_done, 1)
                        dve.wait_ge(gated_done, n)
                        dve.wait_ge(hx_done, n)
                        nc.vector.scalar_tensor_tensor(h[:, bass.ds((2 * cc + u) * TILES, TILES), :],
                                                       gelu_y[u][:, :, :], 0.5, h_plus_x[u][:, :, :],
                                                       ALU.mult, ALU.add).then_inc(h_done, 1)
                        dve.wait_ge(h_done, n)
                        norm_stats(1, u, lambda i: tile_of(h, cc, u, i), n)
                        if cc:
                            dve.wait_ge(scattered[u], MOVES * cc)
                        norm_apply(1, u, lambda i: tile_of(h, cc, u, i), n)

                    def rows_of(u):
                        n = count(cc, u)
                        k = ROW_STEPS * (2 * cc + u)
                        got = ps[:, Y[u], 64:64 + TILES * E].rearrange("p (i e) -> p i e", e=E)
                        dve.wait_ge(ranks_in_psum, n)
                        nc.vector.tensor_tensor(row_of[u][:, :, :], got, repeat(next_row[:, :], TILES),
                                                ALU.add).then_inc(row_step, 1)
                        dve.wait_ge(row_step, k + 1)
                        nc.vector.tensor_tensor(next_row[:, :], ps[:, Y[u], 64 + TILES * E:64 + (TILES + 1) * E],
                                                next_row[:, :], ALU.add).then_inc(row_step, 1)
                        nc.vector.tensor_tensor(rank[u][:, :, :], chunk_of(all_first, cc, u), row_of[u][:, :, :],
                                                ALU.mult).then_inc(row_step, 1)
                        nc.vector.tensor_tensor(others[u][:, :, :], chunk_of(all_second, cc, u), row_of[u][:, :, :],
                                                ALU.mult).then_inc(row_step, 1)
                        dve.wait_ge(row_step, k + 4)
                        nc.vector.tensor_reduce(row_sum[u][:, 0, :], rank[u][:, :, :], AX.X, ALU.add)
                        nc.vector.tensor_reduce(row_sum[u][:, 1, :], others[u][:, :, :], AX.X, ALU.add).then_inc(row_step, 1)
                        dve.wait_ge(row_step, k + 5)
                        nc.vector.tensor_scalar(rows[u][:, :, :], row_sum[u][:, :, :], valid[:, 0:1], skip[:, 0:1],
                                                ALU.mult, ALU.add)
                        nc.vector.tensor_scalar(all_rows[:, :, bass.ds((2 * cc + u) * TILES, TILES)], row_sum[u][:, :, :],
                                                valid[:, 0:1], skip[:, 0:1], ALU.mult, ALU.add).then_inc(rows_done, 1)

                    for u in range(2):
                        n = count(cc, u)
                        got = ps[:, Y[u], 0:TILES * E].rearrange("p (i e) -> p i e", e=E)
                        k = ROUTE_STEPS * (2 * cc + u)
                        if u == 1 and cc == PAIRS - 1:
                            rows_of(0)
                        dve.wait_ge(logits_in_psum, n)
                        nc.vector.tensor_reduce(r_max[u][:, :], got, AX.X, ALU.max).then_inc(route_step, 1)
                        dve.wait_ge(route_step, k + 1)
                        nc.vector.tensor_tensor(r_shift[u][:, :, :], got, spread(r_max[u][:, :], E),
                                                ALU.subtract).then_inc(r_shifted, 1)
                        first, second = chunk_of(all_first, cc, u), chunk_of(all_second, cc, u)
                        gates = chunk_of(all_gates, cc, u)
                        dve.wait_ge(r_shifted, n)
                        nc.vector.scalar_tensor_tensor(rank[u][:, :, :], r_shift[u][:, :, :], TIE,
                                                       repeat(expert_rank[:, :], TILES),
                                                       ALU.is_ge, ALU.mult).then_inc(route_step, 1)
                        dve.wait_ge(route_step, k + 2)
                        nc.vector.tensor_reduce(best[u][:, :], rank[u][:, :, :], AX.X, ALU.max).then_inc(route_step, 1)
                        dve.wait_ge(route_step, k + 3)
                        nc.vector.tensor_tensor(first, rank[u][:, :, :], spread(best[u][:, :], E),
                                                ALU.is_equal).then_inc(route_step, 1)
                        dve.wait_ge(route_step, k + 4)
                        dve.wait_ge(r_exp_done, n)
                        nc.vector.scalar_tensor_tensor(others[u][:, :, :], first, -2.0, r_exp[u][:, :, :],
                                                       ALU.mult, ALU.add).then_inc(route_step, 1)
                        nc.vector.tensor_reduce(r_sum[u][:, :], r_exp[u][:, :, :], AX.X, ALU.add).then_inc(route_step, 1)
                        dve.wait_ge(route_step, k + 5)
                        nc.vector.tensor_reduce(second_exp[u][:, :], others[u][:, :, :], AX.X, ALU.max).then_inc(route_step, 1)
                        dve.wait_ge(route_step, k + 6)
                        nc.vector.reciprocal(gates[:, :, 0], r_sum[u][:, :]).then_inc(route_step, 1)
                        dve.wait_ge(route_step, k + 7)
                        nc.vector.tensor_tensor(rank[u][:, :, :], others[u][:, :, :], spread(second_exp[u][:, :], E),
                                                ALU.is_equal).then_inc(route_step, 1)
                        dve.wait_ge(route_step, k + 8)
                        nc.vector.tensor_tensor(gates[:, :, 1], second_exp[u][:, :], gates[:, :, 0], ALU.mult)
                        dve.wait_ge(route_step, k + 9)
                        nc.vector.tensor_tensor(rank[u][:, :, :], rank[u][:, :, :], repeat(expert_rank[:, :], TILES),
                                                ALU.mult).then_inc(route_step, 1)
                        dve.wait_ge(route_step, k + 10)
                        nc.vector.tensor_reduce(best[u][:, :], rank[u][:, :, :], AX.X, ALU.max).then_inc(route_step, 1)
                        dve.wait_ge(route_step, k + 11)
                        nc.vector.tensor_tensor(second, rank[u][:, :, :], spread(best[u][:, :], E),
                                                ALU.is_equal).then_inc(second_done, 1)
                        dve.wait_ge(second_done, n)
                        nc.vector.tensor_tensor(chosen[u][:, 0:TILES, :], first, second, ALU.add).then_inc(chosen_done, 1)
                    if cc < PAIRS - 1:
                        rows_of(0)
                        embedded_norm(cc + 1, 0)
                    rows_of(1)
                    if cc < PAIRS - 1:
                        embedded_norm(cc + 1, 1)

                N = TABLE
                steps = [0]

                def linked(ins):
                    steps[0] += 1
                    ins.then_inc(table_step, 1)
                    dve.wait_ge(table_step, steps[0])

                dve.wait_ge(rows_done, CHUNKS)
                dve.wait_ge(row_step, ROW_STEPS * CHUNKS)
                nc.vector.tensor_copy(next_row_int[:, :], next_row[:, :]).then_inc(next_rows_done, 1)
                linked(nc.vector.tensor_tensor(counts[:, :], next_row[:, :], region[:, :], ALU.subtract))
                linked(nc.vector.tensor_tensor(over[:, :, :], spread(counts[:, :], MOST_TILES), repeat(steps128[:, :], E), ALU.is_gt))
                linked(nc.vector.tensor_reduce(n_tiles[:, :], over[:, :, :], AX.X, ALU.add))
                linked(nc.vector.tensor_tensor_scan(tiles_to[:, :], ones_e[:, :], n_tiles[:, :], 0.0, ALU.mult, ALU.add))
                linked(nc.vector.tensor_tensor(behind[:, :, :], spread(ramp[:, :], E - 1), repeat(tiles_to[:, 0:E - 1], N),
                                               ALU.is_ge))
                linked(nc.vector.tensor_reduce(tile_expert[:, :], behind[:, :, :], AX.X, ALU.add))
                linked(nc.vector.tensor_tensor(behind[:, :, :], behind[:, :, :], repeat(n_tiles[:, 0:E - 1], N), ALU.mult))
                linked(nc.vector.tensor_reduce(tiles_behind[:, :], behind[:, :, :], AX.X, ALU.add))
                linked(nc.vector.tensor_scalar(live[:, :], ramp[:, :], tiles_to[:, E - 1:E], None, ALU.is_lt))
                linked(nc.vector.tensor_tensor(tile_row[:, :], ramp[:, :], tiles_behind[:, :], ALU.subtract))
                linked(nc.vector.tensor_scalar(tile_row[:, :], tile_row[:, :], float(P), None, ALU.mult))
                linked(nc.vector.scalar_tensor_tensor(tile_row[:, :], tile_expert[:, :], float(SLOTS), tile_row[:, :],
                                                      ALU.mult, ALU.add))
                linked(nc.vector.scalar_tensor_tensor(load_row[:, :], tile_row[:, :], -float(NULL_ROW), live[:, :],
                                                      ALU.add, ALU.mult))
                nc.vector.tensor_scalar(load_row_int[:, :], load_row[:, :], float(NULL_ROW), None, ALU.add)
                nc.vector.tensor_copy(tile_expert_int[:, :], tile_expert[:, :]).then_inc(table_done, 1)
                dve.wait_ge(xT_in_psum[1], 2 * CHUNKS)
                for v in range(2):
                    last = nc.vector.memset(xsT[v][FG:FG + 1, :, :], 1.0)
                last.then_inc(xsT_ones, 1)

                dve.wait_ge(table_done, 1)
                dve.wait_ge(w_in, WEIGHTS)
                for v in range(2):
                    e = dve.value_load(tile_expert_int[0:1, v:v + 1], min_val=0, max_val=E - 1)
                    nc.vector.tensor_copy(w1_now[v][:, 1, :], w1[:, bass.ds(e, 1), 1, :].rearrange("p e n -> p (e n)")
                                          ).then_inc(w1_dve_done, 1)

                linked(nc.vector.tensor_tensor(moved[:, :], tiles_to[:, :], n_tiles[:, :], ALU.subtract))
                linked(nc.vector.scalar_tensor_tensor(moved[:, :], moved[:, :], float(P), region[:, :], ALU.mult, ALU.subtract))
                for k, onehot in enumerate((all_first, all_second)):
                    linked(nc.vector.tensor_tensor(onehot[:, :, :], onehot[:, :, :], repeat(moved[:, :], NT), ALU.mult))
                    linked(nc.vector.tensor_reduce(row_move[:, k, :], onehot[:, :, :], AX.X, ALU.add))
                linked(nc.vector.tensor_tensor(y_sum[:, :, :], all_rows[:, :, :], row_move[:, :, :], ALU.add))
                nc.vector.tensor_scalar(y_rows[:, :, :], y_sum[:, :, :], valid[:, 0:1], None, ALU.mult).then_inc(y_rows_done, 1)
                def next_w1(v, tile):
                    e = dve.value_load(tile_expert_int[0:1, tile], min_val=0, max_val=E - 1)
                    nc.vector.tensor_copy(w1_now[v][:, 1, :], w1[:, bass.ds(e, 1), 1, :].rearrange("p e n -> p (e n)")
                                          ).then_inc(w1_dve_done, 1)

                with dve.Fori(0, MOE_TILES // 2) as tt:
                    for v in range(2):
                        dve.wait_ge(ys_in_psum, YSP0 + 2 * tt + v - 1)
                        dve.wait_ge(hid_in_psum, 2 * tt + v + 1)
                        nc.vector.tensor_scalar(hidT[v][:, 3:6, :],
                                                ps[:, 5 + 2 * v, 0:3 * P].rearrange("p (m t) -> p m t", m=3), 0.0, None,
                                                ALU.max).then_inc(hidT_dve_done, 1)
                        next_w1(v, bass.ds(2 * tt + 2 + v, 1))
                    for v in range(2):
                        e = dve.value_load(tile_expert_int[0:1, bass.ds(2 * tt + v, 1)], min_val=0, max_val=E - 1)
                        dve.wait_ge(ys_stored, 32 * tt + 16)
                        dve.wait_ge(ys_in_psum, YSP0 + 2 * tt + v + 1)
                        nc.vector.tensor_tensor(ys[v][:, :], ps[:, 2 * v + 1, 0:D],
                                                b2[:, bass.ds(e, 1), :].rearrange("p e d -> p (e d)"),
                                                ALU.add).then_inc(ys_done, 1)

                dve.wait_ge(ys_in_psum, YSP0 + MOE_TILES)
                dve.wait_ge(vals_zero, 1)
                for u in range(2):
                    nc.vector.memset(vals[u][0:HALF, :, :, 0, DH:VW], 1.0)
                    nc.vector.memset(vals[u][HALF:P, :, :, 1, DH:VW], 1.0)
                    nc.vector.memset(xeT[u][0:R1, :], 0.0)
                    nc.vector.memset(xeT[u][R1:R1 + 1, :], 1.0)
                    nc.vector.memset(sc[u][:, :, T:HALF], 0.0)
                dve.wait_ge(xsT_done, MOE_TILES + 2)
                dve.wait_ge(w1_act_done, MOE_TILES + 2)
                dve.wait_ge(w1_dve_done, MOE_TILES + 2)
                dve.wait_ge(ys_stored, STORED0 + 16 * MOE_TILES)
                for u in range(2):
                    last = nc.vector.memset(s_hidT[u][:, :, :].rearrange("p m (s t) -> p (m s) t", t=HALF)[:, :, T:HALF], 0.0)
                last.then_inc(late_const, 1)

                W = [0, 4]

                def add_experts(pair, u):
                    for out_of, gate, added in ((y_first, 0, first_added), (y_second, 1, moe_added)):
                        dve.wait_ge(gathered[gate][u], MOVES // 2 * (pair + 1))
                        for i in range(TILES):
                            last = nc.vector.scalar_tensor_tensor(
                                tile_of(h, pair, u, i), out_of[u][:, i, :], tile_of(all_gates, pair, u, i)[:, gate:gate + 1],
                                tile_of(h, pair, u, i), ALU.mult, ALU.add)
                        last.then_inc(added, 1)
                        dve.wait_ge(added, count(pair, u))
                    norm_stats(2, u, lambda i: tile_of(h, pair, u, i), count(pair, u))

                def start(pair):
                    add_experts(pair, 0)
                    norm_apply(2, 0, lambda i: tile_of(h, pair, 0, i), count(pair, 0))
                    add_experts(pair, 1)
                    norm_apply(2, 1, lambda i: tile_of(h, pair, 1, i), count(pair, 1))

                start(0)
                for cc in range(PAIRS):
                    def keys(u):
                        for j in range(HG):
                            dve.wait_ge(k_in_psum, 3 * (2 * cc + u) + j + 1)
                            nc.vector.tensor_copy(kk[u][:, j, :, 0, :], packed(ps[:, W[u] + (3, 1, 3)[j], 0:CT])
                                                  ).then_inc(k_done, 1)

                    def high_values(u):
                        dve.wait_ge(v_in_psum, count(cc, u))
                        for bank in range(2):
                            last = nc.vector.tensor_copy(
                                vals[u][HALF:P, 4 * bank:4 * bank + 4, :, 1, 0:DH],
                                ps[HALF:P, W[u] + bank, 0:4 * FG].rearrange("p (s h d) -> p s h d", s=4, d=DH))
                        last.then_inc(v_high_done, 1)

                    def mapped_keys(u):
                        dve.wait_ge(kk_in_psum, 3 * (2 * cc + u) + 2)
                        nc.vector.tensor_copy(kk[u][:, 1, :, 1, :], packed(ps[:, W[u] + 3, 0:CT])).then_inc(kk_dve_done, 1)

                    def add_squares(t):
                        u, i = divmod(t, TILES)
                        dst = sc[u][:, HEADS * i:HEADS * i + HEADS, 0:T]
                        dve.wait_ge(squares_done, 8 * cc + t + 1)
                        nc.vector.tensor_tensor(dst, squares[t % 2][:, :, 0, :], squares[t % 2][:, :, 1, :],
                                                ALU.add).then_inc(sc2_done, 1)
                        dve.wait_ge(sc2_done, 8 * cc + t + 1)
                        nc.vector.tensor_reduce(sc_max[u][:, HEADS * i:HEADS * i + HEADS], dst, AX.X,
                                                ALU.max).then_inc(sc2_max_done, 1)

                    def shift(u):
                        dve.wait_ge(sqrt_done, count(cc, u))
                        dve.wait_ge(sqrt_max_done, count(cc, u))
                        nc.vector.tensor_tensor(sc[u][:, :, 0:T], sc[u][:, :, 0:T], spread(sc_max[u][:, :], T),
                                                ALU.subtract).then_inc(sc_shifted, 1)

                    def turned_weights(t):
                        dve.wait_ge(pT_in_psum, 8 * cc + t + 1)
                        if t >= 2:
                            dve.wait_ge(ctx_in_psum, 8 * cc + t - 1)
                        nc.vector.tensor_copy(probsT[t % 2][:, 3:6, :], ps[:, W[t % 2] + 1, 0:3 * P]).then_inc(pT_dve_done, 1)

                    def context(t):
                        u, i = divmod(t, TILES)
                        got = ps[:, W[t % 2] + 2, 0:HEADS * VW].rearrange("p (r j d) -> p r j d", r=4, d=VW)
                        dve.wait_ge(ctx_in_psum, 8 * cc + t + 1)
                        nc.vector.reciprocal(inv_sum[t % 2][:, :].rearrange("p (r j) -> p r j", r=4),
                                             got[:, :, :, DH]).then_inc(inv_sum_done, 1)
                        dve.wait_ge(inv_sum_done, 8 * cc + t + 1)
                        nc.vector.tensor_tensor(
                            ctx_tok[u][:, i, :].rearrange("p (j r d) -> p r j d", j=HG, r=4), got[:, :, :, 0:DH],
                            spread(inv_sum[t % 2][:, :].rearrange("p (r j) -> p r j", r=4), DH),
                            ALU.mult).then_inc(ctx_scaled, 1)

                    def attend(u):
                        dve.wait_ge(ctx_scaled, 8 * cc + 4 * u + 4)
                        nc.vector.tensor_tensor(chunk_of(h, cc, u), chunk_of(h, cc, u), ctx_tok[u][:, :, :],
                                                ALU.add).then_inc(attended, 1)
                        dve.wait_ge(attended, count(cc, u))
                        norm_stats(3, u, lambda i: tile_of(h, cc, u, i), count(cc, u))

                    keys(0)
                    high_values(0)
                    mapped_keys(0)
                    keys(1)
                    high_values(1)
                    mapped_keys(1)
                    for t in range(6):
                        add_squares(t)
                    shift(0)
                    add_squares(6)
                    add_squares(7)
                    turned_weights(0)
                    turned_weights(1)
                    context(0)
                    shift(1)
                    for t in range(2, 2 * TILES + 1):
                        if t < 2 * TILES:
                            turned_weights(t)
                        context(t - 1)
                        if t == TILES + 1:
                            attend(0)
                        elif t == TILES + 3:
                            norm_apply(3, 0, lambda i: tile_of(h, cc, 0, i), count(cc, 0))
                    attend(1)
                    norm_apply(3, 1, lambda i: tile_of(h, cc, 1, i), count(cc, 1))
                    for u in range(2):
                        n = count(cc, u)
                        got = ps[:, W[u] + 3, 0:TILES * E].rearrange("p (i e) -> p i e", e=E)
                        dve.wait_ge(s_logits_in_psum, n)
                        nc.vector.tensor_reduce(s_max[u][:, :], got, AX.X, ALU.max).then_inc(s_max_done, 1)
                        dve.wait_ge(s_max_done, n)
                        nc.vector.tensor_tensor(s_logits[u][:, :, :], got, spread(s_max[u][:, :], E),
                                                ALU.subtract).then_inc(s_shifted, 1)
                        dve.wait_ge(s_shifted, n)
                        nc.vector.scalar_tensor_tensor(s_rank[u][:, :, :], s_logits[u][:, :, :], TIE,
                                                       repeat(expert_rank[:, :], TILES),
                                                       ALU.is_ge, ALU.mult).then_inc(s_rank_done, 1)
                        dve.wait_ge(s_rank_done, n)
                        nc.vector.tensor_reduce(s_best[u][:, :], s_rank[u][:, :, :], AX.X, ALU.max).then_inc(s_best_done, 1)
                        dve.wait_ge(s_best_done, n)
                        nc.vector.tensor_tensor(s_onehot[u][:, :, :], s_rank[u][:, :, :], spread(s_best[u][:, :], E),
                                                ALU.is_equal).then_inc(onehot_done, 1)
                    for u in range(2):
                        n = count(cc, u)
                        dve.wait_ge(s_exp_done, n)
                        nc.vector.tensor_reduce(s_sum[u][:, :], s_exp[u][:, :, :], AX.X, ALU.add).then_inc(s_sum_done, 1)
                        dve.wait_ge(s_sum_done, n)
                        nc.vector.reciprocal(s_prob[u][:, :], s_sum[u][:, :]).then_inc(s_prob_done, 1)
                    if cc < PAIRS - 1:
                        start(cc + 1)
                    for u in range(2):
                        n = count(cc, u)
                        dve.wait_ge(s_out_in_psum, n)
                        dve.wait_ge(s_prob_done, n)
                        if cc:
                            dve.wait_ge(out_done, 32 * count(cc - 1, 1))
                        for i in range(TILES):
                            last = nc.vector.scalar_tensor_tensor(
                                out_tok[u][:, i, :], tokv(W[u])[:, i // 2, i % 2, :], s_prob[u][:, i:i + 1],
                                tile_of(h, cc, u, i), ALU.mult, ALU.add)
                        last.then_inc(out_ready, 1)


def _layout(x, cls_tok, L0_tok_W, L0_attn_V_w, L0_attn_U_w, L0_attn_E1_w, L0_attn_E1_b, L0_attn_E2_w, L0_attn_E2_b,
            L0_attn_a_base, L0_attn_a_delta, L0_attn_C_w, L0_attn_G_w, L0_attn_G_b, L0_ffn_Wg, L0_ffn_W1, L0_ffn_b1,
            L0_ffn_W2, L0_ffn_b2, L1_attn_Wqr, L1_attn_Wqi, L1_attn_Wkr, L1_attn_Wki, L1_attn_Wv, L1_ffn_enc_w,
            L1_ffn_enc_b, L1_ffn_sw_w, L1_ffn_sw_b, L1_ffn_w1, L1_ffn_b1, L1_ffn_w2, L1_ffn_b2):
    import numpy as np
    np_ = {}

    def groups(w, bias=None):
        a = np.reshape(np.asarray(w), (2, FG, -1)).transpose(1, 0, 2)
        if bias is None:
            return np.ascontiguousarray(a)
        row = np.zeros((1, 2, a.shape[2]), a.dtype)
        row[0, 1] = np.asarray(bias)
        return np.concatenate([a, row], 0)

    p = np.asarray(x).reshape(B, 3, 7, 16, 7, 16).transpose(3, 5, 1, 0, 2, 4).reshape(HID, B, T - 1)
    full = np.zeros((HID, B, HALF), p.dtype)
    full[:, :, 1:T] = p
    np_["patches"] = np.ascontiguousarray(
        full.reshape(KC, P, CHUNKS, CW).transpose(2, 1, 0, 3))
    np_["w_tok"] = np.ascontiguousarray(np.asarray(L0_tok_W).T.reshape(KC, P, D).transpose(1, 0, 2))
    np_["cls"] = np.asarray(cls_tok).reshape(1, D)
    v = np.asarray(L0_attn_V_w).T
    np_["EV"] = groups(np.concatenate([np.asarray(L0_attn_E1_w).T, v], 1),
                       np.concatenate([np.asarray(L0_attn_E1_b), np.zeros(16, v.dtype)]))
    np_["U"] = np.ascontiguousarray(np.asarray(L0_attn_U_w).T)
    np_["E2"] = np.ascontiguousarray(np.repeat(np.asarray(L0_attn_E2_w), D // 3, axis=0).T)
    np_["E2b"] = np.ascontiguousarray(np.repeat(np.asarray(L0_attn_E2_b), D // 3).reshape(2, FG).T)
    np_["a_base"] = np.ascontiguousarray(np.asarray(L0_attn_a_base).reshape(2, FG).T)
    np_["a_delta"] = np.ascontiguousarray(np.asarray(L0_attn_a_delta).reshape(2, FG).T)
    np_["C"] = groups(np.asarray(L0_attn_C_w).T)
    np_["G"] = groups(np.asarray(L0_attn_G_w).T, L0_attn_G_b)
    np_["Wg"] = groups(L0_ffn_Wg)
    np_["W1"] = np.stack([groups(w, b) for w, b in zip(np.asarray(L0_ffn_W1), np.asarray(L0_ffn_b1))])
    np_["W2"] = np.asarray(L0_ffn_W2).reshape(E, HC, P, D).transpose(0, 2, 1, 3).reshape(E, P, HC * D)
    np_["b2"] = np.asarray(L0_ffn_b2).reshape(E, 1, D)

    def complex_heads(re, im):
        both = np.stack([np.asarray(re).reshape(HEADS, DH, D), np.asarray(im).reshape(HEADS, DH, D)], 1)
        return groups(both.reshape(HEADS * 2 * DH, D).T)

    np_["Wq"] = complex_heads(L1_attn_Wqr, L1_attn_Wqi)
    np_["Wk"] = complex_heads(L1_attn_Wkr, L1_attn_Wki)
    order = [(n % HG) * 4 + n // HG for n in range(HEADS)]
    wv = np.asarray(L1_attn_Wv).reshape(HEADS, DH, D)[order[0::2] + order[1::2]]
    np_["Wv"] = groups(wv.reshape(D, D).T)
    np_["enc_w"] = groups(L1_ffn_enc_w)
    np_["enc_b"] = np.asarray(L1_ffn_enc_b).reshape(R1, 1)
    np_["sw"] = np.concatenate([np.asarray(L1_ffn_sw_w), np.asarray(L1_ffn_sw_b)[None]], 0)
    np_["s_w1"] = groups(np.asarray(L1_ffn_w1).transpose(1, 0, 2).reshape(D, E * R1))
    np_["s_b1"] = np.asarray(L1_ffn_b1)
    np_["s_w2"] = np.asarray(L1_ffn_w2).reshape(4, P, D).transpose(1, 0, 2)
    np_["s_b2"] = np.asarray(L1_ffn_b2)
    return np_


def kernel(**inputs):
    import numpy as _np
    import concourse.bacc as _bacc
    from concourse import mybir as _mybir
    from concourse.bass_utils import run_bass_kernel_spmd as _run

    nc = _bacc.Bacc("TRN2", target_bir_lowering=False, num_devices=1)
    laid = _layout(**inputs)
    arrays, A = {}, {}
    for name, a in laid.items():
        arrays[f"in_{name}"] = _np.ascontiguousarray(a)
        A[name] = nc.dram_tensor(f"in_{name}", a.shape, _mybir.dt.from_np(a.dtype), kind="ExternalInput").ap()
    out = nc.dram_tensor("out_0", (B * T, D), _mybir.dt.from_np(_np.dtype("float32")), kind="ExternalOutput").ap()
    build(nc, A, out)
    r = _run(nc, [arrays], core_ids=[0])
    return r.results[0]["out_0"].reshape(B, T, D)
```
